# Optimizing a Trainium2 kernel written in Bass

```python
import numpy as np
import jax
import jax.numpy as jnp

def _softmax(x, axis=-1):
    return jax.nn.softmax(x, axis=axis)

def _gelu(x):
    return jax.nn.gelu(x, approximate=True)

def _silu(x):
    return jax.nn.silu(x)

def _sigmoid(x):
    return jax.nn.sigmoid(x)

def _layernorm(x, axis=-1, eps=1e-05):
    m = jnp.mean(x, axis=axis, keepdims=True)
    v = jnp.var(x, axis=axis, keepdims=True)
    return (x - m) / jnp.sqrt(v + eps)

def _scatter_add(tgt, idx, src, axis=0):
    return tgt.at[idx].add(src)

def _segment_sum(src, seg, n):
    return jax.ops.segment_sum(src, seg, n)
kernel_name = 'mk_seq_postln_d2_jaxref_r8_f6f516'

def setup_inputs(seed: int=0):
    np.random.seed(seed)
    _w = jnp.asarray

    def _L0_attn_setup():
        import jax, jax.numpy as jnp
        import numpy as np
        H, EXP, N, CONV = (128, 2, 16, 4)
        INNER = H * EXP
        DTR = max(H // 16, 1)
        BATCH, SEQ = (2, 128)

        def _forward(x, norm_w, norm_b, in_w, in_b, conv_w, conv_b, bc_w, bc_b, dtr_w, dtr_b, dt_w, dt_b, out_w, out_b):
            B, L, _ = x.shape
            mu = x.mean(-1, keepdims=True)
            var = ((x - mu) ** 2).mean(-1, keepdims=True)
            normed = (x - mu) * jax.lax.rsqrt(var + 1e-05) * norm_w + norm_b
            xz = normed @ in_w + in_b
            xb, z = (xz[..., :INNER], xz[..., INNER:])
            xp = jnp.pad(xb, ((0, 0), (CONV - 1, 0), (0, 0)))
            xc = sum((xp[:, k:k + L, :] * conv_w[:, k] for k in range(CONV))) + conv_b
            xa = jax.nn.silu(xc)
            bc = xa @ bc_w + bc_b
            Bm, Cm = (bc[..., :N], bc[..., N:])
            dt = jax.nn.softplus((xa @ dtr_w + dtr_b) @ dt_w + dt_b)
            dt = jnp.clip(dt, 0.001, 0.1)
            a_diag = -(jnp.arange(N, dtype=jnp.float32) + 1.0)
            a_bar = jnp.exp(dt[..., None] * a_diag)
            dt_mean = dt.mean(axis=2, keepdims=True)[..., None]
            bx = dt_mean * Bm[:, :, None, :] * xa[..., None]

            def step(h, ts):
                a_t, bx_t, c_t = ts
                h = a_t * h + bx_t
                y = jnp.einsum('bdn,bn->bd', h, c_t)
                return (h, y)
            h0 = jnp.zeros((B, INNER, N), x.dtype)
            _, ys = jax.lax.scan(step, h0, (a_bar.transpose(1, 0, 2, 3), bx.transpose(1, 0, 2, 3), Cm.transpose(1, 0, 2)))
            ssm_out = ys.transpose(1, 0, 2)
            gated = ssm_out * jax.nn.silu(z)
            return gated @ out_w + out_b
        key = jax.random.key(seed)
        ks = jax.random.split(key, 16)
        g = lambda k, shape, s=0.02: jax.random.normal(k, shape, dtype=jnp.float32) * s
        return {'x': jax.random.normal(ks[0], (BATCH, SEQ, H), dtype=jnp.float32), 'norm_w': jnp.ones((H,), jnp.float32), 'norm_b': jnp.zeros((H,), jnp.float32), 'in_w': g(ks[1], (H, 2 * INNER)), 'in_b': jnp.zeros((2 * INNER,), jnp.float32), 'conv_w': g(ks[2], (INNER, CONV), 0.1), 'conv_b': jnp.zeros((INNER,), jnp.float32), 'bc_w': g(ks[3], (INNER, 2 * N)), 'bc_b': jnp.zeros((2 * N,), jnp.float32), 'dtr_w': g(ks[4], (INNER, DTR)), 'dtr_b': jnp.zeros((DTR,), jnp.float32), 'dt_w': g(ks[5], (DTR, INNER)), 'dt_b': jnp.zeros((INNER,), jnp.float32), 'out_w': g(ks[6], (INNER, H)), 'out_b': jnp.zeros((H,), jnp.float32)}
    _L0_attn_in = _L0_attn_setup()

    def _L0_ffn_setup():
        import jax, jax.numpy as jnp
        import numpy as np
        import math
        N_EXP = 8
        TOP_K = 2
        CAPACITY_FACTOR = 1.25

        def _capacity(num_tokens):
            cap = math.floor(TOP_K * CAPACITY_FACTOR * num_tokens / N_EXP)
            cap += cap % 2
            return int(cap)
        key = jax.random.key(seed)
        k1, k2, k3, k4 = jax.random.split(key, 4)
        B, C, d = (4, 128, 128)
        x = jax.random.normal(k1, (B, C, d), dtype=jnp.float32)
        w_g = jax.random.normal(k2, (d, N_EXP), dtype=jnp.float32) * 0.02
        c_fc = jax.random.normal(k3, (N_EXP, d, 4 * d), dtype=jnp.float32) * 0.02
        c_proj = jax.random.normal(k4, (N_EXP, 4 * d, d), dtype=jnp.float32) * 0.02
        return {'x': x, 'w_g': w_g, 'c_fc': c_fc, 'c_proj': c_proj}
    _L0_ffn_in = _L0_ffn_setup()

    def _L1_attn_setup():
        import jax, jax.numpy as jnp
        import numpy as np
        NUM_HEADS = 4
        CHUNK = 64
        GATE_NORM = 16.0
        EPS = 1e-05

        def _xavier(key, fan_in, fan_out):
            gain = 2.0 ** (-2.5)
            limit = gain * np.sqrt(6.0 / (fan_in + fan_out))
            return jax.random.uniform(key, (fan_in, fan_out), jnp.float32, -limit, limit)

        def _to_chunks(t, B, H, NC, C):
            d = t.shape[-1]
            return t.reshape(B, H, NC, C, d).transpose(2, 0, 1, 3, 4)

        def _gla_forward(x, Wq, Wk, Wv, Wg, gk_w1, gk_w2, gk_b2, g_norm_w, Wo):
            B, L, D = x.shape
            H = NUM_HEADS
            C = CHUNK
            NC = L // C
            q = x @ Wq
            k = x @ Wk
            v = x @ Wv
            gk = jax.nn.log_sigmoid(x @ gk_w1 @ gk_w2 + gk_b2) / GATE_NORM

            def split_heads(t):
                return t.reshape(B, L, H, -1).transpose(0, 2, 1, 3)
            q, k, v, gk = map(split_heads, (q, k, v, gk))
            dk = q.shape[-1]
            scale = dk ** (-0.5)
            qc = _to_chunks(q, B, H, NC, C)
            kc = _to_chunks(k, B, H, NC, C)
            vc = _to_chunks(v, B, H, NC, C)
            gc = _to_chunks(gk, B, H, NC, C)
            Bcum = jnp.cumsum(gc, axis=3)
            causal = jnp.tril(jnp.ones((C, C), jnp.float32))

            def step(Hst, inp):
                qi, ki, vi, bi = inp
                qg = qi * jnp.exp(bi) * scale
                kg = ki * jnp.exp(-bi)
                o_inter = jnp.einsum('bhcd,bhde->bhce', qg, Hst)
                A = jnp.einsum('bhtd,bhsd->bhts', qg, kg) * causal
                o_intra = jnp.einsum('bhts,bhse->bhte', A, vi)
                b_last = bi[:, :, -1:, :]
                kH = ki * jnp.exp(b_last - bi)
                H_new = jnp.exp(b_last).transpose(0, 1, 3, 2) * Hst + jnp.einsum('bhcd,bhce->bhde', kH, vi)
                return (H_new, o_inter + o_intra)
            dv = v.shape[-1]
            H0 = jnp.zeros((B, H, dk, dv), jnp.float32)
            _, oc = jax.lax.scan(step, H0, (qc, kc, vc, Bcum))
            o = oc.transpose(1, 2, 0, 3, 4).reshape(B, H, L, dv)
            o = o.transpose(0, 2, 1, 3)
            rms = jnp.sqrt(jnp.mean(o * o, axis=-1, keepdims=True) + EPS)
            o_n = o / rms * g_norm_w
            g = (x @ Wg).reshape(B, L, H, dv)
            o = o_n * g * jax.nn.sigmoid(g)
            return o.reshape(B, L, H * dv) @ Wo
        key = jax.random.key(seed)
        ks = jax.random.split(key, 8)
        B, L, D = (4, 256, 128)
        Dk, Dv, R = (128, 256, 16)
        x = jax.random.normal(ks[0], (B, L, D), jnp.float32)
        return {'x': x, 'Wq': _xavier(ks[1], D, Dk), 'Wk': _xavier(ks[2], D, Dk), 'Wv': _xavier(ks[3], D, Dv), 'Wg': _xavier(ks[4], D, Dv), 'gk_w1': _xavier(ks[5], D, R), 'gk_w2': _xavier(ks[6], R, Dk), 'gk_b2': jnp.zeros((Dk,), jnp.float32), 'g_norm_w': jnp.ones((Dv // NUM_HEADS,), jnp.float32), 'Wo': _xavier(ks[7], Dv, D)}
    _L1_attn_in = _L1_attn_setup()

    def _L1_ffn_setup():
        import jax, jax.numpy as jnp
        import numpy as np
        B, S, D, F, E = (8, 128, 128, 512, 8)
        EPS = 1e-05
        key = jax.random.key(seed)
        ks = jax.random.split(key, 4)
        s = 0.02
        return {'input_features': jax.random.normal(ks[0], (B, S, D), jnp.float32), 'centroids': jax.random.normal(ks[1], (E, D), jnp.float32) * 0.1, 'ln_g': jnp.ones((E, D), jnp.float32), 'ln_b': jnp.zeros((E, D), jnp.float32), 'w1': jax.random.normal(ks[2], (E, D, F), jnp.float32) * s, 'b1': jnp.zeros((E, F), jnp.float32), 'w2': jax.random.normal(ks[3], (E, F, D), jnp.float32) * s, 'b2': jnp.zeros((E, D), jnp.float32)}
    _L1_ffn_in = _L1_ffn_setup()
    _d = {'L0_attn_x': _L0_attn_in['x'], 'L0_attn_norm_w': _L0_attn_in['norm_w'], 'L0_attn_norm_b': _L0_attn_in['norm_b'], 'L0_attn_in_w': _L0_attn_in['in_w'], 'L0_attn_in_b': _L0_attn_in['in_b'], 'L0_attn_conv_w': _L0_attn_in['conv_w'], 'L0_attn_conv_b': _L0_attn_in['conv_b'], 'L0_attn_bc_w': _L0_attn_in['bc_w'], 'L0_attn_bc_b': _L0_attn_in['bc_b'], 'L0_attn_dtr_w': _L0_attn_in['dtr_w'], 'L0_attn_dtr_b': _L0_attn_in['dtr_b'], 'L0_attn_dt_w': _L0_attn_in['dt_w'], 'L0_attn_dt_b': _L0_attn_in['dt_b'], 'L0_attn_out_w': _L0_attn_in['out_w'], 'L0_attn_out_b': _L0_attn_in['out_b'], 'L0_ffn_w_g': _L0_ffn_in['w_g'], 'L0_ffn_c_fc': _L0_ffn_in['c_fc'], 'L0_ffn_c_proj': _L0_ffn_in['c_proj'], 'L1_attn_Wq': _L1_attn_in['Wq'], 'L1_attn_Wk': _L1_attn_in['Wk'], 'L1_attn_Wv': _L1_attn_in['Wv'], 'L1_attn_Wg': _L1_attn_in['Wg'], 'L1_attn_gk_w1': _L1_attn_in['gk_w1'], 'L1_attn_gk_w2': _L1_attn_in['gk_w2'], 'L1_attn_gk_b2': _L1_attn_in['gk_b2'], 'L1_attn_g_norm_w': _L1_attn_in['g_norm_w'], 'L1_attn_Wo': _L1_attn_in['Wo'], 'L1_ffn_centroids': _L1_ffn_in['centroids'], 'L1_ffn_ln_g': _L1_ffn_in['ln_g'], 'L1_ffn_ln_b': _L1_ffn_in['ln_b'], 'L1_ffn_w1': _L1_ffn_in['w1'], 'L1_ffn_b1': _L1_ffn_in['b1'], 'L1_ffn_w2': _L1_ffn_in['w2'], 'L1_ffn_b2': _L1_ffn_in['b2']}
    _x0 = _d['L0_attn_x']
    _d['L0_attn_x'] = jax.random.normal(jax.random.fold_in(jax.random.key(seed), 1), (4, 1024, 128), dtype=_x0.dtype)
    del _x0
    return _d

def reference(L0_attn_x, L0_attn_norm_w, L0_attn_norm_b, L0_attn_in_w, L0_attn_in_b, L0_attn_conv_w, L0_attn_conv_b, L0_attn_bc_w, L0_attn_bc_b, L0_attn_dtr_w, L0_attn_dtr_b, L0_attn_dt_w, L0_attn_dt_b, L0_attn_out_w, L0_attn_out_b, L0_ffn_w_g, L0_ffn_c_fc, L0_ffn_c_proj, L1_attn_Wq, L1_attn_Wk, L1_attn_Wv, L1_attn_Wg, L1_attn_gk_w1, L1_attn_gk_w2, L1_attn_gk_b2, L1_attn_g_norm_w, L1_attn_Wo, L1_ffn_centroids, L1_ffn_ln_g, L1_ffn_ln_b, L1_ffn_w1, L1_ffn_b1, L1_ffn_w2, L1_ffn_b2):

    def _L0_attn_ref(x, norm_w, norm_b, in_w, in_b, conv_w, conv_b, bc_w, bc_b, dtr_w, dtr_b, dt_w, dt_b, out_w, out_b):
        import jax, jax.numpy as jnp
        import numpy as np
        H, EXP, N, CONV = (128, 2, 16, 4)
        INNER = H * EXP
        DTR = max(H // 16, 1)
        BATCH, SEQ = (2, 128)

        def _forward(x, norm_w, norm_b, in_w, in_b, conv_w, conv_b, bc_w, bc_b, dtr_w, dtr_b, dt_w, dt_b, out_w, out_b):
            B, L, _ = x.shape
            mu = x.mean(-1, keepdims=True)
            var = ((x - mu) ** 2).mean(-1, keepdims=True)
            normed = (x - mu) * jax.lax.rsqrt(var + 1e-05) * norm_w + norm_b
            xz = normed @ in_w + in_b
            xb, z = (xz[..., :INNER], xz[..., INNER:])
            xp = jnp.pad(xb, ((0, 0), (CONV - 1, 0), (0, 0)))
            xc = sum((xp[:, k:k + L, :] * conv_w[:, k] for k in range(CONV))) + conv_b
            xa = jax.nn.silu(xc)
            bc = xa @ bc_w + bc_b
            Bm, Cm = (bc[..., :N], bc[..., N:])
            dt = jax.nn.softplus((xa @ dtr_w + dtr_b) @ dt_w + dt_b)
            dt = jnp.clip(dt, 0.001, 0.1)
            a_diag = -(jnp.arange(N, dtype=jnp.float32) + 1.0)
            a_bar = jnp.exp(dt[..., None] * a_diag)
            dt_mean = dt.mean(axis=2, keepdims=True)[..., None]
            bx = dt_mean * Bm[:, :, None, :] * xa[..., None]

            def step(h, ts):
                a_t, bx_t, c_t = ts
                h = a_t * h + bx_t
                y = jnp.einsum('bdn,bn->bd', h, c_t)
                return (h, y)
            h0 = jnp.zeros((B, INNER, N), x.dtype)
            _, ys = jax.lax.scan(step, h0, (a_bar.transpose(1, 0, 2, 3), bx.transpose(1, 0, 2, 3), Cm.transpose(1, 0, 2)))
            ssm_out = ys.transpose(1, 0, 2)
            gated = ssm_out * jax.nn.silu(z)
            return gated @ out_w + out_b
        return _forward(x, norm_w, norm_b, in_w, in_b, conv_w, conv_b, bc_w, bc_b, dtr_w, dtr_b, dt_w, dt_b, out_w, out_b)

    def _L0_ffn_ref(x, w_g, c_fc, c_proj):
        import jax, jax.numpy as jnp
        import numpy as np
        import math
        N_EXP = 8
        TOP_K = 2
        CAPACITY_FACTOR = 1.25

        def _capacity(num_tokens):
            cap = math.floor(TOP_K * CAPACITY_FACTOR * num_tokens / N_EXP)
            cap += cap % 2
            return int(cap)
        B, C, d = x.shape
        T = B * C
        cap = _capacity(T)
        xt = x.reshape(T, d)
        logits = xt @ w_g
        top_v, top_i = jax.lax.top_k(logits, TOP_K)
        full = jnp.full_like(logits, -jnp.inf)
        full = full.at[jnp.arange(T)[:, None], top_i].set(top_v)
        probs = jax.nn.softmax(full, axis=-1)
        exp_mask = jax.nn.one_hot(top_i, N_EXP, dtype=jnp.int32)
        exp_mask = jnp.transpose(exp_mask, (1, 0, 2))
        exp_rank = jnp.cumsum(exp_mask.reshape(TOP_K * T, N_EXP), axis=0) - 1
        exp_rank = exp_rank.reshape(TOP_K, T, N_EXP)
        exp_mask = exp_mask * (exp_rank < cap).astype(jnp.int32)
        exp_rank = jnp.sum(exp_mask * exp_rank, axis=-1)
        exp_weights = exp_mask.astype(x.dtype) * probs[None]
        rank_oh = jax.nn.one_hot(exp_rank, cap, dtype=x.dtype)
        cb_weight = jnp.einsum('kte,ktc->tec', exp_weights, rank_oh)
        sec_mask = (cb_weight != 0).astype(x.dtype)
        exp_batches = jnp.einsum('tec,td->ecd', sec_mask, xt)
        h = jax.nn.gelu(jnp.einsum('ecd,edf->ecf', exp_batches, c_fc), approximate=False)
        exp_out = jnp.einsum('ecf,efd->ecd', h, c_proj)
        out = cb_weight.reshape(T, N_EXP * cap) @ exp_out.reshape(N_EXP * cap, d)
        return out.reshape(B, C, d)

    def _L1_attn_ref(x, Wq, Wk, Wv, Wg, gk_w1, gk_w2, gk_b2, g_norm_w, Wo):
        import jax, jax.numpy as jnp
        import numpy as np
        NUM_HEADS = 4
        CHUNK = 64
        GATE_NORM = 16.0
        EPS = 1e-05

        def _xavier(key, fan_in, fan_out):
            gain = 2.0 ** (-2.5)
            limit = gain * np.sqrt(6.0 / (fan_in + fan_out))
            return jax.random.uniform(key, (fan_in, fan_out), jnp.float32, -limit, limit)

        def _to_chunks(t, B, H, NC, C):
            d = t.shape[-1]
            return t.reshape(B, H, NC, C, d).transpose(2, 0, 1, 3, 4)

        def _gla_forward(x, Wq, Wk, Wv, Wg, gk_w1, gk_w2, gk_b2, g_norm_w, Wo):
            B, L, D = x.shape
            H = NUM_HEADS
            C = CHUNK
            NC = L // C
            q = x @ Wq
            k = x @ Wk
            v = x @ Wv
            gk = jax.nn.log_sigmoid(x @ gk_w1 @ gk_w2 + gk_b2) / GATE_NORM

            def split_heads(t):
                return t.reshape(B, L, H, -1).transpose(0, 2, 1, 3)
            q, k, v, gk = map(split_heads, (q, k, v, gk))
            dk = q.shape[-1]
            scale = dk ** (-0.5)
            qc = _to_chunks(q, B, H, NC, C)
            kc = _to_chunks(k, B, H, NC, C)
            vc = _to_chunks(v, B, H, NC, C)
            gc = _to_chunks(gk, B, H, NC, C)
            Bcum = jnp.cumsum(gc, axis=3)
            causal = jnp.tril(jnp.ones((C, C), jnp.float32))

            def step(Hst, inp):
                qi, ki, vi, bi = inp
                qg = qi * jnp.exp(bi) * scale
                kg = ki * jnp.exp(-bi)
                o_inter = jnp.einsum('bhcd,bhde->bhce', qg, Hst)
                A = jnp.einsum('bhtd,bhsd->bhts', qg, kg) * causal
                o_intra = jnp.einsum('bhts,bhse->bhte', A, vi)
                b_last = bi[:, :, -1:, :]
                kH = ki * jnp.exp(b_last - bi)
                H_new = jnp.exp(b_last).transpose(0, 1, 3, 2) * Hst + jnp.einsum('bhcd,bhce->bhde', kH, vi)
                return (H_new, o_inter + o_intra)
            dv = v.shape[-1]
            H0 = jnp.zeros((B, H, dk, dv), jnp.float32)
            _, oc = jax.lax.scan(step, H0, (qc, kc, vc, Bcum))
            o = oc.transpose(1, 2, 0, 3, 4).reshape(B, H, L, dv)
            o = o.transpose(0, 2, 1, 3)
            rms = jnp.sqrt(jnp.mean(o * o, axis=-1, keepdims=True) + EPS)
            o_n = o / rms * g_norm_w
            g = (x @ Wg).reshape(B, L, H, dv)
            o = o_n * g * jax.nn.sigmoid(g)
            return o.reshape(B, L, H * dv) @ Wo
        return _gla_forward(x, Wq, Wk, Wv, Wg, gk_w1, gk_w2, gk_b2, g_norm_w, Wo)

    def _L1_ffn_ref(input_features, centroids, ln_g, ln_b, w1, b1, w2, b2):
        import jax, jax.numpy as jnp
        import numpy as np
        B, S, D, F, E = (8, 128, 128, 512, 8)
        EPS = 1e-05
        x = input_features.reshape(-1, D)
        aff = jax.lax.stop_gradient(x @ centroids.T)
        eid = jnp.argmax(aff, axis=-1)
        alpha = jax.nn.sigmoid(jnp.sum(x * centroids[eid], axis=-1, keepdims=True))
        mu = jnp.mean(x, axis=-1, keepdims=True)
        var = jnp.mean((x - mu) ** 2, axis=-1, keepdims=True)
        xn = (x - mu) * jax.lax.rsqrt(var + EPS)
        xln = xn * ln_g[eid] + ln_b[eid]
        onehot = jax.nn.one_hot(eid, E, dtype=x.dtype)
        ffn = jnp.zeros_like(x)
        for e in range(E):
            h = jax.nn.relu(xln @ w1[e] + b1[e])
            ffn = ffn + onehot[:, e:e + 1] * (h @ w2[e] + b2[e])
        out = x + alpha * ffn
        return out.reshape(input_features.shape)
    x = L0_attn_x
    x = _layernorm(x + _L0_attn_ref(x, L0_attn_norm_w, L0_attn_norm_b, L0_attn_in_w, L0_attn_in_b, L0_attn_conv_w, L0_attn_conv_b, L0_attn_bc_w, L0_attn_bc_b, L0_attn_dtr_w, L0_attn_dtr_b, L0_attn_dt_w, L0_attn_dt_b, L0_attn_out_w, L0_attn_out_b), axis=-1)
    x = _layernorm(x + _L0_ffn_ref(x, L0_ffn_w_g, L0_ffn_c_fc, L0_ffn_c_proj), axis=-1)
    x = _layernorm(x + _L1_attn_ref(x, L1_attn_Wq, L1_attn_Wk, L1_attn_Wv, L1_attn_Wg, L1_attn_gk_w1, L1_attn_gk_w2, L1_attn_gk_b2, L1_attn_g_norm_w, L1_attn_Wo), axis=-1)
    x = _layernorm(x + _L1_ffn_ref(x, L1_ffn_centroids, L1_ffn_ln_g, L1_ffn_ln_b, L1_ffn_w1, L1_ffn_b1, L1_ffn_w2, L1_ffn_b2), axis=-1)
    return x

_drawn_inputs = setup_inputs


def setup_inputs(seed=0):
    import zlib

    import numpy as np

    out = dict(_drawn_inputs(seed))
    spreads = {'L0_attn_norm_w': (1.0, 0.6),
     'L0_attn_norm_b': (0.0, 0.8),
     'L0_attn_in_b': (0.0, 0.8),
     'L0_attn_conv_b': (0.0, 0.8),
     'L0_attn_bc_b': (0.0, 0.8),
     'L0_attn_dtr_b': (0.0, 0.1),
     'L0_attn_dt_b': (0.0, 0.1),
     'L0_attn_out_b': (0.0, 0.8),
     'L1_attn_gk_b2': (0.0, 0.8),
     'L1_attn_g_norm_w': (1.0, 0.6),
     'L1_ffn_ln_g': (1.0, 0.6),
     'L1_ffn_ln_b': (0.0, 2.0),
     'L1_ffn_b1': (0.0, 0.619),
     'L1_ffn_b2': (0.0, 0.1)}
    factors = {'L0_attn_in_w': 8.0,
     'L0_attn_conv_w': 8.0,
     'L0_attn_bc_w': 8.0,
     'L0_attn_out_w': 8.0,
     'L1_attn_Wq': 3.336,
     'L1_attn_Wk': 3.28,
     'L1_attn_Wv': 3.292,
     'L1_attn_Wg': 3.34,
     'L1_attn_gk_w1': 8.0,
     'L1_attn_gk_w2': 8.0,
     'L1_attn_Wo': 3.298}
    for name, (base, spread) in spreads.items():
        noise = np.random.default_rng([zlib.crc32(name.encode()), seed]).standard_normal(out[name].shape)
        drawn = base * np.exp(spread * noise) if base else spread * noise
        out[name] = jnp.asarray(drawn.astype(out[name].dtype))
    for name, factor in factors.items():
        out[name] = (out[name] * factor).astype(out[name].dtype)
    return out
```

```python
from contextlib import ExitStack

import concourse.bass as bass
from concourse import mybir

ALU = mybir.AluOpType
ACT = mybir.ActivationFunctionType
AX = mybir.AxisListType
F32 = mybir.dt.float32
BF16 = mybir.dt.bfloat16
I32 = mybir.dt.int32
U32 = mybir.dt.uint32

P = 128
EPS = 1e-5
LN_EXP = "natural_log_exp_and_others"


class Buffers:
    pass


class Space:

    def __init__(self, nc, ctx, stage):
        self.nc, self.ctx, self.stage, self.sems = nc, ctx, stage, []
        ctx.callback(self.end)

    def sb(self, name, shape, dtype=F32):
        return self.ctx.enter_context(self.nc.sbuf_tensor(f"{self.stage}_{name}", shape, dtype))

    def ps(self, name, shape, dtype=F32):
        return self.ctx.enter_context(self.nc.psum_tensor(f"{self.stage}_{name}", shape, dtype))

    def sem(self, name):
        self.sems.append(self.nc.alloc_semaphore(f"{self.stage}_{name}"))
        return self.sems[-1]

    def end(self):
        self.nc.clear_and_free_semaphores(self.sems)
        self.nc.all_engine_barrier()

    def block(self):
        return self.ctx.enter_context(self.nc.Block())


def constants(nc, keep):
    with ExitStack() as ctx:
        s = Space(nc, ctx, "const")
        filled, done = s.sem("filled"), s.sem("done")
        block = s.block()

        @block.vector
        def _(dve):
            dve.memset(keep.ident[:], 0.0).then_inc(filled, 1)
            dve.memset(keep.ones[:], 1.0).then_inc(filled, 1)
            dve.memset(keep.before[:], 1.0).then_inc(filled, 1)
            dve.memset(keep.eps[:], EPS).then_inc(filled, 1)

        @block.gpsimd
        def _(pool):
            pool.wait_ge(filled, 4)
            pool.affine_select(out=keep.ident[:], in_=keep.ident[:], compare_op=ALU.not_equal, fill=1.0, base=0,
                               pattern=[[-1, P]], channel_multiplier=1).then_inc(done, 1)
            pool.affine_select(out=keep.before[:], in_=keep.before[:], compare_op=ALU.is_gt, fill=0.0, base=0,
                               pattern=[[1, P]], channel_multiplier=-1).then_inc(done, 1)
            pool.wait_ge(done, 2)


def run_chunks(chunks, slots, loop, steps, scan, start=None):
    most = max([ahead for _, ahead, _ in steps] + [0])
    least = -min([ahead for _, ahead, _ in steps] + [0])
    in_order = sorted(steps, key=lambda step: step[0])

    def alone(q):
        for slot, ahead, work in in_order:
            if 0 <= q + ahead < chunks:
                work(q + ahead, (q + ahead) % 2)

    def chunk(q, par):
        for n in range(slots):
            for at in (n, n + 0.5):
                for slot, ahead, work in steps:
                    if slot == at and (not isinstance(q, int) or 0 <= q + ahead < chunks):
                        work(q + ahead, (par + ahead) % 2)
                if at == n:
                    scan(q, par, n)

    for q in range(-most, 0):
        alone(q)
    if start:
        start()
    head = max(least, 1)
    pairs = (chunks - head - most) // 2
    for q in range(head):
        chunk(q, q % 2)
    with loop(0, pairs) as i:
        chunk(2 * i + head, head % 2)
        chunk(2 * i + head + 1, 1 - head % 2)
    for q in range(head + 2 * pairs, chunks):
        chunk(q, q % 2)
    for q in range(chunks, chunks + least):
        alone(q)


def at_chunk(tiles, q):
    return tiles[q] if isinstance(q, int) else tiles[bass.ds(q, 1)].rearrange("a p s d -> (a p) s d")


def later(q, n):
    return not isinstance(q, int) or q >= n


def mamba(nc, keep, x, norm_w, norm_b, in_w, in_b, conv_w, conv_b, bc_w, bc_b, dtr_w, dtr_b, dt_w, dt_b, out_w, out_b):
    B, L, D = x.shape
    INNER = out_w.shape[0]
    J = INNER // P
    N = bc_w.shape[1] // 2
    CONV = conv_w.shape[1]
    R = dtr_w.shape[1]
    C = 512
    DEEP = 4
    S = C // P
    Q = B * L // C
    HALVES = L // C
    assert (J, N, HALVES, D) == (2, 16, 2, P)
    x_tiles = x.rearrange("b (c s p) d -> (b c) p s d", s=S, p=P)
    x1_tiles = keep.x1.rearrange("(q s p) d -> q p s d", s=S, p=P)

    with ExitStack() as ctx:
        m = Space(nc, ctx, "ssm")
        w_in = m.sb("w_in", [P, 2 * INNER])
        w_bcd = m.sb("w_bcd", [P, J, 2 * N + R])
        w_dt = m.sb("w_dt", [2 * N + R, INNER])
        w_out = m.sb("w_out", [P, J, D])
        out_bias = m.sb("out_bias", [P, D])
        nw, nb = m.sb("nw", [P, 1]), m.sb("nb", [P, 1])
        b_in = m.sb("b_in", [P, 2 * J])
        b_conv, b_dt = m.sb("b_conv", [P, J]), m.sb("b_dt", [P, J])
        minus_b_dt = m.sb("minus_b_dt", [P, J])
        b_bc = m.sb("b_bc", [2 * N, 1])
        b_dtr = m.sb("b_dtr", [2 * N + R, 1])
        taps = m.sb("taps", [P, J, CONV])
        eps = m.sb("eps", [P, 1])
        mean_w = m.sb("mean_w", [P, 2 * N])
        is_c = m.sb("is_c", [2 * N, 1])
        pick = m.sb("pick", [P, 2 * N, P], BF16)

        xin = m.sb("xin", [P, 2, S, D])
        stats, moments = m.sb("stats", [P, S, 6]), m.sb("moments", [P, S, 2])
        lnvar, rstd = m.sb("lnvar", [P, S]), m.sb("rstd", [P, S])
        xn = m.sb("xn", [P, S, D])
        nT = m.sb("nT", [P, C])
        xb = m.sb("xb", [P, J, CONV - 1 + C])
        conv = m.sb("conv", [P, J, 2, C])
        zs = m.sb("zs", [P, 2, J, C])
        xa = m.sb("xa", [P, 2, J, C])
        dt = m.sb("dt", [P, 2, J, C])
        dtn = m.sb("dtn", [P, J, C])
        dte = m.sb("dte", [P, J, C])
        dtl = m.sb("dtl", [P, J, C])
        dtr = m.sb("dtr", [2 * N + R, C])
        bcs = m.sb("bcs", [2 * N, C])
        bc = m.sb("bc", [2 * N, C])
        mid = m.sb("mid", [2 * N, C], BF16)
        rest1, rest2 = m.sb("rest1", [2 * N, C]), m.sb("rest2", [2 * N, C])
        parts = m.sb("parts", [P, 2, C], BF16)
        b_all = m.sb("b_all", [P, DEEP, C])
        decay = m.sb("decay", [P, DEEP, J, C])
        drive = m.sb("drive", [P, DEEP, J, C])
        h = m.sb("h", [P, 2, J, C])
        hc = m.sb("hc", [P, DEEP, J, C])
        h_end = m.sb("h_end", [P, N, J, 1])
        gated = m.sb("gated", [P, J, C])
        xob = m.sb("xob", [P, 2, S, D])
        x1 = m.sb("x1", [P, 2, S, D])
        s_x1out = [m.sem(f"x1_stored{i}") for i in range(2)]
        res = m.sb("res", [P, S, D])
        ostats, omoments = m.sb("ostats", [P, S, 6]), m.sb("omoments", [P, S, 2])
        olnvar, orstd = m.sb("olnvar", [P, S]), m.sb("orstd", [P, S])

        p_y = m.ps("p_y", [P, J, C])
        p_b = m.ps("p_b", [P, C])
        p_c = m.ps("p_c", [P, 2, C])
        p_mm = [m.ps(f"p_mm{i}", [P, C]) for i in range(3)]

        s_w = m.sem("weights_loaded")
        s_zero, s_cst, s_pick = m.sem("zeroed"), m.sem("constants_made"), m.sem("pick_made")
        s_turn, s_sp_turn = m.sem("vector_steps"), m.sem("sync_steps")
        s_edge = m.sem("xb_edge_made")
        s_x = [m.sem(f"x_loaded{i}") for i in range(2)]
        s_xr = [m.sem(f"x_reloaded{i}") for i in range(2)]
        s_st, s_mom = m.sem("stats_made"), m.sem("moments_made")
        s_lnv, s_rstd = m.sem("lnvar_made"), m.sem("rstd_made")
        s_xn, s_xT, s_nT = m.sem("x_normed"), m.sem("x_transposed"), m.sem("nT_made")
        s_in, s_xb, s_z = m.sem("in_product"), m.sem("xb_made"), m.sem("z_made")
        s_conv, s_xa = m.sem("conv_steps"), m.sem("xa_made")
        s_bcd, s_bcs, s_dtr = m.sem("bcd_product"), m.sem("bcs_made"), m.sem("dtr_made")
        s_dtp, s_dtn, s_dte, s_dtl, s_dt = (m.sem("dt_product"), m.sem("dt_negated"), m.sem("dt_exp"),
                                            m.sem("dt_log"), m.sem("dt_made"))
        s_mean, s_bc, s_split, s_parts = m.sem("dt_mean"), m.sem("bc_made"), m.sem("split_steps"), m.sem("parts_made")
        s_pb, s_pc, s_ball = m.sem("b_spread"), m.sem("c_spread"), m.sem("b_copied")
        s_decay, s_drive, s_h, s_hc, s_y = (m.sem("decay_made"), m.sem("drive_made"), m.sem("h_made"),
                                            m.sem("hc_made"), m.sem("y_summed"))
        s_hend = m.sem("h_end_kept")
        s_g, s_o, s_xob, s_res = m.sem("gated_made"), m.sem("out_product"), m.sem("x_plus_bias"), m.sem("residual_made")
        s_ost, s_omom, s_olnv, s_orstd, s_x1 = (m.sem("out_stats"), m.sem("out_moments"), m.sem("out_lnvar"),
                                                m.sem("out_rstd"), m.sem("x1_made"))
        WEIGHTS = 14 * 16
        block = m.block()

        @block.sync
        def _(sp):
            col = lambda v, a: v.rearrange("(a p) -> p a", p=P)
            sp.dma_start(xin[:, 0], x_tiles[0]).then_inc(s_x[0], 16)
            sp.dma_start(w_in[:], in_w).then_inc(s_w, 16)
            sp.dma_start(w_bcd[:, :, 0:2 * N], bc_w.rearrange("(j p) n -> p j n", p=P)).then_inc(s_w, 16)
            sp.dma_start(w_bcd[:, :, 2 * N:], dtr_w.rearrange("(j p) n -> p j n", p=P)).then_inc(s_w, 16)
            sp.dma_start(w_dt[2 * N:, :], dt_w).then_inc(s_w, 16)
            sp.dma_start(w_out[:], out_w.rearrange("(j p) n -> p j n", p=P)).then_inc(s_w, 16)
            sp.dma_start(nw[:], col(norm_w, 1)).then_inc(s_w, 16)
            sp.dma_start(nb[:], col(norm_b, 1)).then_inc(s_w, 16)
            sp.dma_start(b_in[:], col(in_b, 2 * J), allow_slow_non_contiguous=True).then_inc(s_w, 16)
            sp.dma_start(b_conv[:], col(conv_b, J), allow_slow_non_contiguous=True).then_inc(s_w, 16)
            sp.dma_start(b_dt[:], col(dt_b, J), allow_slow_non_contiguous=True).then_inc(s_w, 16)
            sp.dma_start(b_bc[:], bc_b.rearrange("(n a) -> n a", a=1)).then_inc(s_w, 16)
            sp.dma_start(b_dtr[2 * N:, :], dtr_b.rearrange("(n a) -> n a", a=1)).then_inc(s_w, 16)
            sp.dma_start(taps[:], conv_w.rearrange("(j p) k -> p j k", p=P)).then_inc(s_w, 16)
            sp.dma_start(out_bias[:], out_b.rearrange("(a d) -> a d", a=1).broadcast_to((P, D))).then_inc(s_w, 16)
            sp.dma_start(xin[:, 1], x_tiles[1]).then_inc(s_x[1], 16)
            for q in range(2):
                sp.dma_start(xob[:, q], x_tiles[q]).then_inc(s_xr[q], 16)
            for q in range(2, 4):
                sp.wait_ge(s_xn, S * (q - 1))
                sp.dma_start(xin[:, q % 2], x_tiles[q]).then_inc(s_x[q % 2], 16)

            def during(q, par):
                known = isinstance(q, int)
                if not known or q + 3 < Q:
                    sp.wait_ge(s_xn, S * (q + 2))
                    sp.sem_inc(s_sp_turn, 1)
                    sp.dma_start(xin[:, 1 - par], at_chunk(x_tiles, q + 3)).then_inc(s_x[1 - par], 16)
                if not known or q + 1 < Q:
                    sp.wait_ge(s_res, q)
                    sp.sem_inc(s_sp_turn, 1)
                    sp.dma_start(xob[:, 1 - par], at_chunk(x_tiles, q + 1)).then_inc(s_xr[1 - par], 16)
                sp.wait_ge(s_x1, S * q)
                sp.sem_inc(s_sp_turn, 1)
                sp.dma_start(at_chunk(x1_tiles, q - 1), x1[:, 1 - par]).then_inc(s_x1out[1 - par], 16)

            with sp.Fori(0, (Q - 4) // 2) as i:
                during(2 * i + 1, 1)
                during(2 * i + 2, 0)
            for q in range(Q - 3, Q + 1):
                during(q, q % 2)
            for par in range(2):
                sp.wait_ge(s_x1out[par], 16 * (Q // 2))

        @block.vector
        def _(dve):
            dve.memset(eps[:], EPS).then_inc(s_zero, 1)
            dve.memset(pick[:], 0.0).then_inc(s_zero, 1)
            dve.memset(is_c[:], 1.0).then_inc(s_zero, 1)
            dve.memset(mean_w[:], 0.0).then_inc(s_zero, 1)
            dve.memset(parts[:], 0.0).then_inc(s_zero, 1)
            dve.wait_ge(s_zero, 5)
            dve.memset(is_c[0:N, :], 0.0).then_inc(s_cst, 1)
            dve.memset(mean_w[:, 0:N], 1.0 / INNER).then_inc(s_cst, 1)
            dve.wait_ge(s_w, WEIGHTS)
            dve.tensor_scalar(minus_b_dt[:], b_dt[:], -1.0, None, ALU.mult).then_inc(s_cst, 1)

            def x_moments(q, par):
                dve.wait_ge(s_x[par], 8 * (q - par) + 16)
                for s in range(S):
                    dve.bn_stats(stats[:, s], xin[:, par, s]).then_inc(s_st, 1)
                dve.wait_ge(s_st, S * (q + 1))
                dve.sem_inc(s_turn, 1)
                for s in range(S):
                    dve.bn_aggr(moments[:, s], stats[:, s]).then_inc(s_mom, 1)

            def norm_x(q, par):
                dve.wait_ge(s_rstd, q + 1)
                dve.wait_ge(s_mom, S * (q + 1))
                dve.wait_ge(s_xT, q)
                for s in range(S):
                    dve.tensor_scalar(xn[:, s], xin[:, par, s], moments[:, s, 0:1], rstd[:, s:s + 1],
                                      ALU.subtract, ALU.mult).then_inc(s_xn, 1)

            def scale_x(q, par):
                dve.wait_ge(s_xT, q + 1)
                dve.wait_ge(s_in, 2 * J * q)
                dve.tensor_scalar(nT[:], p_mm[0][:], nw[:], nb[:], ALU.mult, ALU.add).then_inc(s_nT, 1)

            def convolve(q, j):
                dve.wait_ge(s_xb, J * q + j + 1)
                dve.wait_ge(s_xa, J * q)
                dve.tensor_scalar(conv[:, j, 0], xb[:, j, 0:C], taps[:, j, 0:1], None, ALU.mult).then_inc(s_conv, 1)
                for k in range(1, CONV):
                    dve.wait_ge(s_conv, CONV * (J * q + j) + k)
                    dve.scalar_tensor_tensor(out=conv[:, j, k % 2], in0=xb[:, j, k:k + C], scalar=taps[:, j, k:k + 1],
                                             in1=conv[:, j, 1 - k % 2], op0=ALU.mult, op1=ALU.add).then_inc(s_conv, 1)

            def clip_dt(q, par):
                dve.wait_ge(s_dtl, q + 1)
                dve.tensor_scalar(dt[:, par], dtl[:], 0.001, 0.1, ALU.max, ALU.min).then_inc(s_dt, 1)

            def split_bc(q, par):
                dve.wait_ge(s_mean, q + 1)
                dve.wait_ge(s_bcs, q + 1)
                dve.wait_ge(s_split, 4 * q)
                dve.scalar_tensor_tensor(out=bc[:], in0=p_mm[1][0:2 * N, :], scalar=is_c[:], in1=bcs[:],
                                         op0=ALU.add, op1=ALU.mult).then_inc(s_bc, 1)
                dve.wait_ge(s_bc, q + 1)
                if later(q, 2):
                    dve.wait_ge(s_pc, N * (q - 1))
                dve.tensor_copy(parts[0:2 * N, par], bc[:]).then_inc(s_split, 1)
                dve.wait_ge(s_split, 4 * q + 1)
                dve.tensor_tensor(rest1[:], bc[:], parts[0:2 * N, par], ALU.subtract).then_inc(s_split, 1)
                dve.wait_ge(s_split, 4 * q + 2)
                dve.wait_ge(s_parts, 2 * q)
                dve.tensor_copy(mid[:], rest1[:]).then_inc(s_split, 1)
                dve.wait_ge(s_split, 4 * q + 3)
                dve.tensor_tensor(rest2[:], rest1[:], mid[:], ALU.subtract).then_inc(s_split, 1)

            def scan(q, par, n):
                first = par == 0
                k, deep = n % 2, n % DEEP
                done = N * q + n
                dve.wait_ge(s_decay, done + 1)
                dve.wait_ge(s_drive, done + 1)
                if not first:
                    dve.wait_ge(s_hend, (q + 1) * (N // 2))
                if later(q, 1) or n >= 2:
                    dve.wait_ge(s_hc, done - 1)
                for j in range(J):
                    dve.tensor_tensor_scan(h[:, k, j], decay[:, deep, j], drive[:, deep, j],
                                           0.0 if first else h_end[:, n, j], ALU.mult, ALU.add).then_inc(s_h, 1)
                dve.wait_ge(s_h, 2 * done + 2)
                dve.wait_ge(s_pc, done + 1)
                if later(q, 1) or n >= DEEP:
                    dve.wait_ge(s_y, done + 1 - DEEP)
                if first:
                    dve.tensor_copy(h_end[:, n], h[:, k, :, C - 1:C]).then_inc(s_hend, 1)
                dve.tensor_tensor(hc[:, deep], h[:, k], p_c[:, k:k + 1].broadcast_to((P, J, C)),
                                  ALU.mult).then_inc(s_hc, 1)

            def gate(q, par):
                dve.wait_ge(s_y, N * (q + 1))
                dve.wait_ge(s_z, J * (q + 1))
                dve.wait_ge(s_o, q)
                dve.tensor_tensor(gated[:], p_y[:], zs[:, par], ALU.mult).then_inc(s_g, 1)

            def residual(q, par):
                dve.wait_ge(s_o, q + 1)
                dve.wait_ge(s_xob, q + 1)
                dve.wait_ge(s_x1, S * q)
                dve.tensor_tensor(res[:], p_mm[0][:].rearrange("p (s d) -> p s d", s=S), xob[:, par],
                                  ALU.add).then_inc(s_res, 1)
                dve.wait_ge(s_res, q + 1)
                for s in range(S):
                    dve.bn_stats(ostats[:, s], res[:, s]).then_inc(s_ost, 1)
                dve.wait_ge(s_ost, S * (q + 1))
                dve.sem_inc(s_turn, 1)
                for s in range(S):
                    dve.bn_aggr(omoments[:, s], ostats[:, s]).then_inc(s_omom, 1)

            def norm_out(q, par):
                dve.wait_ge(s_orstd, q + 1)
                dve.wait_ge(s_omom, S * (q + 1))
                if later(q, 2):
                    dve.wait_ge(s_x1out[par], 8 * (q - par))
                for s in range(S):
                    dve.tensor_scalar(x1[:, par, s], res[:, s], omoments[:, s, 0:1], orstd[:, s:s + 1],
                                      ALU.subtract, ALU.mult).then_inc(s_x1, 1)

            run_chunks(Q, N, dve.Fori, [
                (1, -1, gate), (3, -1, residual), (5, -1, norm_out),
                (2, 1, lambda q, par: convolve(q, 0)), (3, 1, lambda q, par: convolve(q, 1)),
                (6, 2, x_moments), (8, 2, norm_x), (10, 2, scale_x), (10, 1, clip_dt), (12, 1, split_bc)], scan)

        @block.gpsimd
        def _(pool):
            pool.wait_ge(s_zero, 5)
            for part in range(3):
                pool.affine_select(out=pick[:], in_=pick[:], compare_op=ALU.not_equal, fill=1.0,
                                   base=-2 * N * part, pattern=[[-1, 2 * N], [0, P]],
                                   channel_multiplier=1).then_inc(s_pick, 1)
                pool.wait_ge(s_pick, part + 1)

            def add_out_bias(q, par):
                pool.wait_ge(s_xr[par], 8 * (q - par) + 16)
                pool.tensor_tensor(xob[:, par], xob[:, par], out_bias[:, None, :].broadcast_to((P, S, D)),
                                   ALU.add).then_inc(s_xob, 1)

            def scan(q, par, n):
                done = N * q + n
                pool.wait_ge(s_xa, J * (q + 1))
                pool.wait_ge(s_ball, done + 1)
                if later(q, 1) or n >= DEEP:
                    pool.wait_ge(s_h, J * (done + 1 - DEEP))
                pool.tensor_tensor(drive[:, n % DEEP], xa[:, par], b_all[:, n % DEEP, None, :].broadcast_to((P, J, C)),
                                   ALU.mult).then_inc(s_drive, 1)

            pool.wait_ge(s_w, WEIGHTS)
            run_chunks(Q, N, pool.Fori, [(8, 0, add_out_bias)], scan)

        @block.scalar
        def _(act):
            act.preload_act_table_set(LN_EXP)
            act.wait_ge(s_w, WEIGHTS)
            act.wait_ge(s_zero, 5)
            act.wait_ge(s_cst, 3)

            def x_rstd(q, par):
                act.wait_ge(s_mom, S * (q + 1))
                act.activation(lnvar[:], moments[:, :, 1], ACT.Ln, bias=eps[:]).then_inc(s_lnv, 1)
                act.wait_ge(s_lnv, q + 1)
                act.wait_ge(s_xn, S * q)
                act.activation(rstd[:], lnvar[:], ACT.Exp, scale=-0.5).then_inc(s_rstd, 1)

            def take_xb(q, par):
                for j in range(J):
                    act.wait_ge(s_in, 2 * J * q + j + 1)
                    act.wait_ge(s_conv, J * CONV * q)
                    if par == 0:
                        act.activation(xb[:, j, 0:CONV - 1], keep.ident[:, 0:CONV - 1], ACT.Copy,
                                       scale=0.0).then_inc(s_edge, 1)
                    else:
                        act.activation(xb[:, j, 0:CONV - 1], xb[:, j, C:C + CONV - 1], ACT.Copy).then_inc(s_edge, 1)
                    act.wait_ge(s_edge, J * q + j + 1)
                    act.activation(xb[:, j, CONV - 1:], p_mm[j + 1][:], ACT.Identity,
                                   bias=b_in[:, j:j + 1]).then_inc(s_xb, 1)

            def take_z(q, par):
                for j in range(J):
                    act.wait_ge(s_in, 2 * J * q + J + j + 1)
                    if later(q, 2):
                        act.wait_ge(s_g, q - 1)
                    act.activation(zs[:, par, j], p_mm[j + 1][:], ACT.Silu,
                                   bias=b_in[:, J + j:J + j + 1]).then_inc(s_z, 1)

            def take_xa(q, par):
                for j in range(J):
                    act.wait_ge(s_conv, CONV * (J * q + j + 1))
                    if later(q, 2):
                        act.wait_ge(s_drive, N * (q - 1))
                        act.wait_ge(s_bcd, q - 1)
                    act.activation(xa[:, par, j], conv[:, j, 1], ACT.Silu, bias=b_conv[:, j:j + 1]).then_inc(s_xa, 1)
                act.preload_act_table_set(LN_EXP)

            def take_bcd(q, par):
                act.wait_ge(s_bcd, q + 1)
                act.wait_ge(s_dtp, J * q)
                act.activation(dtr[2 * N:, :], p_mm[0][2 * N:2 * N + R, :], ACT.Identity,
                               bias=b_dtr[2 * N:, :]).then_inc(s_dtr, 1)
                act.wait_ge(s_bc, q)
                act.activation(bcs[:], p_mm[0][0:2 * N, :], ACT.Identity, bias=b_bc[:]).then_inc(s_bcs, 1)

            def dt_exp(q, par):
                act.wait_ge(s_dte, q)
                for j in range(J):
                    act.wait_ge(s_dtp, J * q + j + 1)
                    act.activation(dtn[:, j], p_mm[j + 1][:], ACT.Relu, scale=-1.0,
                                   bias=minus_b_dt[:, j:j + 1]).then_inc(s_dtn, 1)
                act.wait_ge(s_dtn, J * (q + 1))
                act.wait_ge(s_dtl, q)
                act.activation(dte[:], dtn[:], ACT.Exp, scale=-1.0).then_inc(s_dte, 1)

            def dt_log(q, par):
                act.wait_ge(s_dte, q + 1)
                act.wait_ge(s_dt, q)
                act.activation(dtl[:], dte[:], ACT.Ln, bias=1.0).then_inc(s_dtl, 1)

            def place_parts(q, par):
                act.wait_ge(s_split, 4 * q + 3)
                act.activation(parts[2 * N:4 * N, par], mid[:], ACT.Copy).then_inc(s_parts, 1)
                act.wait_ge(s_split, 4 * q + 4)
                act.activation(parts[4 * N:6 * N, par], rest2[:], ACT.Copy).then_inc(s_parts, 1)

            def copy_b(q, n):
                act.wait_ge(s_pb, N * q + n + 1)
                if later(q, 1) or n >= DEEP:
                    act.wait_ge(s_drive, N * q + n + 1 - DEEP)
                act.activation(b_all[:, n % DEEP], p_b[:], ACT.Copy).then_inc(s_ball, 1)

            def scan(q, par, n):
                done = N * q + n
                if n == 0:
                    act.wait_ge(s_dt, q + 1)
                if later(q, 1) or n >= DEEP:
                    act.wait_ge(s_h, J * (done + 1 - DEEP))
                act.activation(decay[:, n % DEEP], dt[:, par], ACT.Exp, scale=-(n + 1.0)).then_inc(s_decay, 1)
                if n + 1 < N:
                    copy_b(q, n + 1)
                elif not isinstance(q, int) or q + 1 < Q:
                    copy_b(q + 1, 0)

            def out_rstd(q, par):
                act.wait_ge(s_omom, S * (q + 1))
                act.activation(olnvar[:], omoments[:, :, 1], ACT.Ln, bias=eps[:]).then_inc(s_olnv, 1)
                act.wait_ge(s_olnv, q + 1)
                act.wait_ge(s_x1, S * q)
                act.activation(orstd[:], olnvar[:], ACT.Exp, scale=-0.5).then_inc(s_orstd, 1)

            run_chunks(Q, N, act.Fori, [
                (5, -1, out_rstd), (0, 1, take_xb), (5, 1, take_z), (5, 1, take_xa), (8, 2, x_rstd), (7, 1, take_bcd),
                (9, 1, dt_exp), (9, 1, dt_log), (13, 1, place_parts)], scan, start=lambda: copy_b(0, 0))

        @block.tensor
        def _(pe):
            pe.wait_ge(s_w, WEIGHTS)
            pe.wait_ge(s_cst, 3)
            pe.wait_ge(s_pick, 3)

            def turn_x(q, par):
                pe.wait_ge(s_xn, S * (q + 1))
                if later(q, 1):
                    pe.wait_ge(s_bcs, q)
                for s in range(S):
                    t = pe.transpose(p_mm[0][:, P * s:P * s + P], xn[:, s], keep.ident[:])
                t.then_inc(s_xT, 1)

            def project_in(q, c):
                pe.wait_ge(s_nT, q + 1)
                if c == 0:
                    pe.wait_ge(s_bc, q)
                if c == 1:
                    pe.wait_ge(s_dtn, J * q)
                if c >= J:
                    pe.wait_ge(s_xb, J * q + c - J + 1)
                pe.matmul(p_mm[c % J + 1][:], w_in[:, P * c:P * c + P], nT[:], start=True, stop=True).then_inc(s_in, 1)

            def project_bcd(q, par):
                pe.wait_ge(s_xa, J * (q + 1))
                if later(q, 1):
                    pe.wait_ge(s_res, q - 1)
                for j in range(J):
                    t = pe.matmul(p_mm[0][0:2 * N + R, :], w_bcd[:, j], xa[:, par, j], start=(j == 0), stop=(j == J - 1))
                t.then_inc(s_bcd, 1)

            def project_dt(q, par):
                pe.wait_ge(s_dtr, q + 1)
                pe.wait_ge(s_z, J * (q + 1))
                for j in range(J):
                    pe.matmul(p_mm[j + 1][:], w_dt[2 * N:, P * j:P * j + P], dtr[2 * N:, :], start=True,
                              stop=True).then_inc(s_dtp, 1)

            def mean_dt(q, par):
                pe.wait_ge(s_dt, q + 1)
                pe.wait_ge(s_dtn, J * (q + 1))
                for j in range(J):
                    t = pe.matmul(p_mm[1][0:2 * N, :], mean_w[:], dt[:, par, j], start=(j == 0), stop=(j == J - 1))
                t.then_inc(s_mean, 1)

            def spread_b(q, par, n):
                if n == 0:
                    pe.wait_ge(s_parts, 2 * q + 2)
                if later(q, 1) or n:
                    pe.wait_ge(s_ball, N * q + n)
                pe.matmul(p_b[:], pick[:, n], parts[:, par], start=True, stop=True).then_inc(s_pb, 1)

            def spread_c(q, par, n):
                if later(q, 1) or n >= 2:
                    pe.wait_ge(s_hc, N * q + n - 1)
                pe.matmul(p_c[:, n % 2], pick[:, N + n], parts[:, par], start=True, stop=True).then_inc(s_pc, 1)

            def ahead(spread, q, par, n):
                if n < N:
                    spread(q, par, n)
                elif not isinstance(q, int) or q + 1 < Q:
                    spread(q + 1, 1 - par, n - N)

            def sum_state(q, par, n):
                pe.wait_ge(s_hc, N * q + n + 1)
                if n == 0 and later(q, 1):
                    pe.wait_ge(s_g, q)
                for j in range(J):
                    t = pe.matmul(p_y[:, j], keep.ident[:], hc[:, n % DEEP, j], start=(n == 0), stop=(n == N - 1))
                t.then_inc(s_y, 1)

            def scan(q, par, n):
                ahead(spread_b, q, par, n + 2)
                ahead(spread_c, q, par, n + 1)
                if n > 0:
                    sum_state(q, par, n - 1)

            def project_out(q, par):
                pe.wait_ge(s_g, q + 1)
                if not isinstance(q, int) or q + 2 < Q:
                    pe.wait_ge(s_nT, q + 3)
                for s in range(S):
                    for j in range(J):
                        t = pe.matmul(p_mm[0][:, P * s:P * s + P], gated[:, j, P * s:P * s + P], w_out[:, j],
                                      start=(j == 0), stop=(j == J - 1))
                t.then_inc(s_o, 1)

            def start():
                for n in range(2):
                    spread_b(0, 0, n)
                spread_c(0, 0, 0)

            run_chunks(Q, N, pe.Fori, [
                (0, -1, lambda q, par: sum_state(q, par, N - 1)), (2, -1, project_out),
                (14, 2, lambda q, par: project_in(q, 0)), (15, 2, lambda q, par: project_in(q, 1)),
                (1, 1, lambda q, par: project_in(q, 2)), (1, 1, lambda q, par: project_in(q, 3)),
                (6, 1, project_bcd), (8, 1, project_dt), (9, 2, turn_x), (11, 1, mean_dt)], scan, start=start)


FAR = 1.0e6


def moe(nc, keep, w_g, c_fc, c_proj):
    T = keep.x1.shape[0]
    D, E = w_g.shape
    F = c_fc.shape[2]
    FB = F // P
    NT = T // P
    K = 2
    CAP = K * 5 * T // (4 * E)
    CAP += CAP % 2
    CT = CAP // P
    S = 4
    G = NT // S
    assert D == P and CAP % P == 0
    x1_tiles = keep.x1.rearrange("(q s p) d -> q p s d", s=S, p=P)

    with ExitStack() as outer:
        k = Space(nc, outer, "moe")
        weight, from_slot = keep.weight, keep.from_slot
        to_slot = k.sb("to_slot", [P, K, NT], I32)

        with ExitStack() as ctx:
            m = Space(nc, ctx, "route")
            wg = m.sb("wg", [P, E])
            zero = m.sb("zero", [P, CT, D])
            x1 = m.sb("x1", [P, 2, S, D])
            xT = m.sb("xT", [P, 2, S * P])
            logits = m.sb("logits", [P, NT, E])
            rest = m.sb("rest", [P, NT, E])
            first_of = m.sb("first_of", [P, 1, E])
            base = m.sb("base", [P, 1, E])
            hit, cand = m.sb("hit", [P, NT, E]), m.sb("cand", [P, NT, E])
            best, pref = m.sb("best", [P, K, NT]), m.sb("pref", [P, K, NT])
            chosen = m.sb("chosen", [P, K, NT, E])
            gap, ratio, den, p1 = (m.sb(n, [P, NT]) for n in ("gap", "ratio", "den", "p1"))
            upto, rank, ranke, picked = (m.sb(n, [P, K * NT, E]) for n in ("upto", "rank", "ranke", "picked"))
            rk, row, valid, over, far, near = (m.sb(n, [P, K * NT]) for n in ("rk", "row", "valid", "over", "far", "near"))
            p_t = [m.ps(f"p_t{i}", [P, S * P]) for i in range(2)]
            p_l = [m.ps(f"p_l{i}", [P, S, E]) for i in range(2)]
            p_in = m.ps("p_in", [P, K * NT * E])
            p_all = m.ps("p_all", [P, K * NT * E])
            s_wg, s_zeroed = m.sem("wg_loaded"), m.sem("zero_made")
            s_x = [m.sem(f"x1_loaded{i}") for i in range(2)]
            s_clear = m.sem("rows_cleared")
            s_t, s_xT, s_l, s_log = m.sem("transposed"), m.sem("xT_made"), m.sem("logit_product"), m.sem("logits_made")
            s_iota = m.sem("iota_made")
            s_r, s_ratio, s_cum = m.sem("routing_steps"), m.sem("ratio_made"), m.sem("rank_products")
            block = m.block()

            @block.sync
            def _(sp):
                sp.dma_start(wg[:], w_g).then_inc(s_wg, 16)
                for par in range(2):
                    sp.dma_start(x1[:, par], x1_tiles[par]).then_inc(s_x[par], 16)
                with sp.Fori(1, G // 2) as i:
                    for par in range(2):
                        sp.wait_ge(s_t, 2 * i + par - 1)
                        sp.wait_ge(s_wg, 16)
                        sp.dma_start(x1[:, par], at_chunk(x1_tiles, 2 * i + par)).then_inc(s_x[par], 16)
                sp.wait_ge(s_zeroed, 1)
                for e in range(E):
                    sp.dma_start(keep.xe[e * CAP:(e + 1) * CAP, :].rearrange("(c p) d -> p c d", p=P),
                                 zero[:]).then_inc(s_clear, 16)
                sp.wait_ge(s_clear, 16 * E)

            @block.tensor
            def _(pe):
                pe.wait_ge(s_wg, 16)

                def logit(g, par):
                    pe.wait_ge(s_xT, g + 1)
                    if later(g, 2):
                        pe.wait_ge(s_log, g - 1)
                    for s in range(S):
                        t = pe.matmul(p_l[par][:, s], xT[:, par, P * s:P * s + P], wg[:], start=True, stop=True)
                    t.then_inc(s_l, 1)

                def turn(g, par):
                    pe.wait_ge(s_x[par], 8 * (g - par) + 16)
                    if later(g, 2):
                        pe.wait_ge(s_xT, g - 1)
                    for s in range(S):
                        t = pe.transpose(p_t[par][:, P * s:P * s + P], x1[:, par, s], keep.ident[:])
                    t.then_inc(s_t, 1)

                turn(0, 0)
                turn(1, 1)
                logit(0, 0)
                with pe.Fori(1, G // 2) as i:
                    turn(2 * i, 0)
                    logit(2 * i - 1, 1)
                    turn(2 * i + 1, 1)
                    logit(2 * i, 0)
                logit(G - 1, 1)
                pe.wait_ge(s_r, 13)
                flat = chosen[:].rearrange("p k t e -> p (k t e)")
                pe.matmul(p_all[:], keep.ones[:], flat, start=True, stop=True).then_inc(s_cum, 1)
                pe.matmul(p_in[:], keep.before[:], flat, start=True, stop=True).then_inc(s_cum, 1)

            @block.gpsimd
            def _(pool):
                pool.iota(first_of[:, 0], pattern=[[-1, E]], base=E, channel_multiplier=0,
                          allow_small_or_imprecise_dtypes=True).then_inc(s_iota, 1)
                pool.iota(base[:, 0], pattern=[[CAP, E]], base=0, channel_multiplier=0,
                          allow_small_or_imprecise_dtypes=True).then_inc(s_iota, 1)
                pool.memset(zero[:], 0.0).then_inc(s_zeroed, 1)

            @block.scalar
            def _(act):
                def copy_l(g, par):
                    act.wait_ge(s_l, g + 1)
                    at = logits[:, S * g:S * g + S] if isinstance(g, int) else logits[:, bass.ds(S * g, S)]
                    act.activation(at, p_l[par][:], ACT.Copy).then_inc(s_log, 1)

                act.preload_act_table_set(LN_EXP)
                with act.Fori(0, G // 2) as i:
                    for par in range(2):
                        copy_l(2 * i + par, par)
                act.wait_ge(s_r, 14)
                act.activation(ratio[:], gap[:], ACT.Exp).then_inc(s_ratio, 1)

            @block.vector
            def _(dve):
                with dve.Fori(0, G // 2) as i:
                    for par in range(2):
                        g = 2 * i + par
                        dve.wait_ge(s_t, g + 1)
                        if par == 0:
                            dve.wait_ge(s_l, g - 1 + 1)
                        else:
                            dve.wait_ge(s_l, g)
                        dve.tensor_copy(xT[:, par], p_t[par][:]).then_inc(s_xT, 1)
                steps = [0]

                def step(ins):
                    ins.then_inc(s_r, 1)
                    steps[0] += 1
                    dve.wait_ge(s_r, steps[0])

                wide = lambda v: v[:, :, None].broadcast_to((P, NT, E))
                step(dve.memset(over[:, 0:1], 0.0))
                dve.wait_ge(s_log, G)
                dve.wait_ge(s_iota, 2)
                for c in range(K):
                    src = rest if c else logits
                    step(dve.tensor_reduce(best[:, c], src[:], AX.X, ALU.max))
                    step(dve.tensor_tensor(hit[:], src[:], wide(best[:, c]), ALU.is_equal))
                    step(dve.tensor_tensor(cand[:], hit[:], first_of[:].broadcast_to((P, NT, E)), ALU.mult))
                    step(dve.tensor_reduce(pref[:, c], cand[:], AX.X, ALU.max))
                    step(dve.tensor_tensor(chosen[:, c], cand[:], wide(pref[:, c]), ALU.is_equal))
                    if c == 0:
                        step(dve.scalar_tensor_tensor(out=rest[:].rearrange("p t e -> p (t e)"),
                                                      in0=chosen[:, 0].rearrange("p t e -> p (t e)"), scalar=-3.0e38,
                                                      in1=logits[:].rearrange("p t e -> p (t e)"), op0=ALU.mult,
                                                      op1=ALU.add))
                step(dve.memset(over[:, 0:1], 0.0))
                step(dve.tensor_tensor(gap[:], best[:, 1], best[:, 0], ALU.subtract))
                dve.wait_ge(s_cum, 1)
                tiles = p_all[:].rearrange("p (t e) -> p t e", e=E)
                for e in range(E):
                    step(dve.tensor_tensor_scan(upto[:, :, e], keep.ones[:, 0:K * NT], tiles[:, :, e], 0.0,
                                                ALU.mult, ALU.add))
                step(dve.tensor_tensor(rank[:], upto[:], tiles, ALU.subtract))
                dve.wait_ge(s_cum, 2)
                step(dve.tensor_tensor(rank[:], rank[:], p_in[:].rearrange("p (t e) -> p t e", e=E), ALU.add))
                both = chosen[:].rearrange("p k t e -> p (k t) e")
                step(dve.tensor_tensor(picked[:], rank[:], both, ALU.mult))
                step(dve.tensor_reduce(rk[:], picked[:], AX.X, ALU.add))
                step(dve.tensor_tensor(ranke[:], rank[:], base[:].broadcast_to((P, K * NT, E)), ALU.add))
                step(dve.tensor_tensor(picked[:], ranke[:], both, ALU.mult))
                step(dve.tensor_reduce(row[:], picked[:], AX.X, ALU.add))
                step(dve.tensor_scalar(valid[:], rk[:], float(CAP), None, ALU.is_lt))
                step(dve.tensor_scalar(over[:], rk[:], float(CAP), FAR, ALU.is_ge, ALU.mult))
                step(dve.tensor_tensor(far[:], over[:], row[:], ALU.add))
                step(dve.tensor_tensor(near[:], valid[:], row[:], ALU.mult))
                step(dve.tensor_copy(to_slot[:].rearrange("p k t -> p (k t)"), far[:]))
                step(dve.tensor_copy(from_slot[:].rearrange("p k t -> p (k t)"), near[:]))
                dve.wait_ge(s_ratio, 1)
                step(dve.tensor_scalar(den[:], ratio[:], 1.0, None, ALU.add))
                step(dve.reciprocal(p1[:], den[:]))
                v = valid[:].rearrange("p (k t) -> p k t", k=K)
                step(dve.tensor_tensor(weight[:, 0], p1[:], v[:, 0], ALU.mult))
                step(dve.tensor_tensor(den[:], p1[:], ratio[:], ALU.mult))
                step(dve.tensor_tensor(weight[:, 1], den[:], v[:, 1], ALU.mult))

        with ExitStack() as ctx:
            m = Space(nc, ctx, "send")
            x1 = m.sb("x1", [P, 2, S, D])
            ix = m.sb("ix", [P, 2, K, S], I32)
            s_x = [m.sem(f"x1_loaded{i}") for i in range(2)]
            s_ix = m.sem("ix_made")
            s_turn = m.sem("pool_steps")
            s_sent = [m.sem(f"rows_sent{i}") for i in range(2)]
            block = m.block()
            ROUND = 16 * K * S

            @block.sync
            def _(sp):
                for par in range(2):
                    sp.dma_start(x1[:, par], x1_tiles[par]).then_inc(s_x[par], 16)
                with sp.Fori(1, G // 2) as i:
                    for par in range(2):
                        sp.wait_ge(s_sent[par], ROUND * i)
                        sp.wait_ge(s_x[0], 16)
                        sp.dma_start(x1[:, par], at_chunk(x1_tiles, 2 * i + par)).then_inc(s_x[par], 16)

            @block.vector
            def _(dve):
                with dve.Fori(0, G // 2) as i:
                    for par in range(2):
                        dve.wait_ge(s_sent[par], ROUND * i)
                        dve.tensor_copy(ix[:, par], to_slot[:, :, bass.ds(S * (2 * i + par), S)]).then_inc(s_ix, 1)

            @block.gpsimd
            def _(pool):
                with pool.Fori(0, G // 2) as i:
                    for par in range(2):
                        pool.wait_ge(s_ix, 2 * i + par + 1)
                        pool.wait_ge(s_x[par], 16 * i + 16)
                        pool.sem_inc(s_turn, 1)
                        for c in range(K):
                            for s in range(S):
                                pool.indirect_dma_start(
                                    out=keep.xe, out_offset=bass.IndirectOffsetOnAxis(ap=ix[:, par, c, s:s + 1], axis=0),
                                    in_=x1[:, par, s], in_offset=None, bounds_check=E * CAP - 1,
                                    oob_is_err=False).then_inc(s_sent[par], 16)
                for par in range(2):
                    pool.wait_ge(s_sent[par], ROUND * (G // 2))

        with ExitStack() as ctx:
            m = Space(nc, ctx, "expert")
            w1, w2 = m.sb("w1", [P, 2, F]), m.sb("w2", [P, 2, FB, D])
            xe, xT = m.sb("xe", [P, 2, CT, D]), m.sb("xT", [P, CAP])
            hT = m.sb("hT", [P, FB, CAP])
            ye = m.sb("ye", [P, 2, CT, D])
            p_t = [m.ps(f"p_t{i}", [P, 4 * P]) for i in range(2)]
            p_h = [m.ps(f"p_h{i}", [P, 4 * P]) for i in range(4)]
            p_o = [m.ps(f"p_o{i}", [P, 4, D]) for i in range(2)]
            s_in = [m.sem(f"expert_loaded{i}") for i in range(2)]
            s_t, s_xT, s_h, s_g, s_o, s_y = (m.sem("transposed"), m.sem("xT_made"), m.sem("h_product"),
                                             m.sem("gelu_made"), m.sem("out_product"), m.sem("y_copied"))
            s_out = [m.sem(f"y_stored{i}") for i in range(2)]
            block = m.block()
            groups = [(a, min(a + 4, CT)) for a in range(0, CT, 4)]
            NG = len(groups)
            xe_rows = keep.xe.rearrange("(e c p) d -> e p c d", e=E, p=P)
            ye_rows = keep.ye.rearrange("(e c p) d -> e p c d", e=E, p=P)
            w2_rows = c_proj.rearrange("e (c p) d -> e p c d", p=P)

            @block.sync
            def _(sp):
                def load(e, par):
                    if isinstance(e, int):
                        a, b, c = xe_rows[e], c_fc[e], w2_rows[e]
                    else:
                        a, b, c = at_chunk(xe_rows, e), c_fc[bass.ds(e, 1)].rearrange("a p f -> (a p) f"), at_chunk(w2_rows, e)
                    sp.dma_start(xe[:, par], a).then_inc(s_in[par], 16)
                    sp.dma_start(w1[:, par], b).then_inc(s_in[par], 16)
                    sp.dma_start(w2[:, par], c).then_inc(s_in[par], 16)

                def store(e, par):
                    sp.wait_ge(s_y, NG * (e + 1))
                    sp.wait_ge(s_y, 1)
                    sp.dma_start(at_chunk(ye_rows, e), ye[:, par]).then_inc(s_out[par], 16)

                load(0, 0)
                load(1, 1)
                with sp.Fori(1, E // 2) as i:
                    for par in range(2):
                        store(2 * i + par - 2, par)
                        load(2 * i + par, par)
                for par in range(2):
                    store(E - 2 + par, par)
                for par in range(2):
                    sp.wait_ge(s_out[par], 16 * (E // 2))

            @block.tensor
            def _(pe):
                with pe.Fori(0, E // 2) as i:
                    for par in range(2):
                        e = 2 * i + par
                        pe.wait_ge(s_in[par], 48 * i + 48)
                        for n, (a, b) in enumerate(groups):
                            k_ = (NG * par + n) % 2
                            if NG * par + n >= 2:
                                pe.wait_ge(s_xT, NG * e + n - 1)
                            else:
                                pe.wait_ge(s_xT, NG * e)
                            for c in range(a, b):
                                t = pe.transpose(p_t[k_][:, P * (c - a):P * (c - a) + P], xe[:, par, c], keep.ident[:])
                            t.then_inc(s_t, 1)

                        def out(n):
                            a, b = groups[n]
                            k_ = (NG * par + n) % 2
                            pe.wait_ge(s_g, FB * (NG * e + n + 1))
                            if NG * par + n >= 2:
                                pe.wait_ge(s_y, NG * e + n - 1)
                            else:
                                pe.wait_ge(s_y, NG * e)
                            for c in range(a, b):
                                for f in range(FB):
                                    t = pe.matmul(p_o[k_][:, c - a], hT[:, f, P * c:P * c + P], w2[:, par, f],
                                                  start=(f == 0), stop=(f == FB - 1))
                            t.then_inc(s_o, 1)

                        for n, (a, b) in enumerate(groups):
                            pe.wait_ge(s_xT, NG * e + n + 1)
                            for f in range(FB):
                                done = FB * (NG * e + n) + f
                                if NG * par + n == 0:
                                    pe.wait_ge(s_g, FB * NG * e)
                                else:
                                    pe.wait_ge(s_g, done - FB + 1)
                                pe.matmul(p_h[f][:, 0:P * (b - a)], w1[:, par, P * f:P * f + P], xT[:, P * a:P * b],
                                          start=True, stop=True).then_inc(s_h, 1)
                            if n:
                                out(n - 1)
                        out(NG - 1)

            @block.scalar
            def _(act):
                with act.Fori(0, E // 2) as i:
                    for par in range(2):
                        e = 2 * i + par
                        act.wait_ge(s_o, NG * e)
                        for n, (a, b) in enumerate(groups):
                            for f in range(FB):
                                act.wait_ge(s_h, FB * (NG * e + n) + f + 1)
                                act.activation(hT[:, f, P * a:P * b], p_h[f][:, 0:P * (b - a)],
                                               ACT.Gelu).then_inc(s_g, 1)

            @block.vector
            def _(dve):
                with dve.Fori(0, E // 2) as i:
                    for par in range(2):
                        e = 2 * i + par
                        dve.wait_ge(s_h, FB * NG * e)
                        for n, (a, b) in enumerate(groups):
                            k_ = (NG * par + n) % 2
                            dve.wait_ge(s_t, NG * e + n + 1)
                            dve.tensor_copy(xT[:, P * a:P * b], p_t[k_][:, 0:P * (b - a)]).then_inc(s_xT, 1)
                        dve.wait_ge(s_out[par], 16 * i)
                        for n, (a, b) in enumerate(groups):
                            k_ = (NG * par + n) % 2
                            dve.wait_ge(s_o, NG * e + n + 1)
                            dve.tensor_copy(ye[:, par, a:b], p_o[k_][:, 0:b - a]).then_inc(s_y, 1)


def gla(nc, keep, Wq, Wk, Wv, Wg, gk_w1, gk_w2, gk_b2, g_norm_w, Wo, ffn):
    T = keep.x1.shape[0]
    D, DK = Wq.shape
    DV = Wv.shape[1]
    R = gk_w1.shape[1]
    HEADS = 4
    DH, VH = DK // HEADS, DV // HEADS
    CH = 64
    S = 4
    C = S * P
    NC = C // CH
    Q = T // C
    SCALE = DH ** -0.5
    GATE = 16.0
    assert (D, DK, DV) == (P, P, 2 * P)
    K = 2
    E = ffn.centroids.shape[0]
    ROUND, PLACES = 16 * S, 16 * S
    x1_tiles = keep.x1.rearrange("(q s p) d -> q p s d", s=S, p=P)

    with ExitStack() as ctx:
        m = Space(nc, ctx, "gla")
        wq, wk = m.sb("wq", [P, DK]), m.sb("wk", [P, DK])
        wvg = m.sb("wvg", [P, 2 * DV])
        w1, w2, b2 = m.sb("w1", [P, R]), m.sb("w2", [R, DK]), m.sb("b2", [P, 1])
        nb2 = m.sb("nb2", [P, 1])
        gnw = m.sb("gnw", [P, 1])
        wo_in, wo = m.sb("wo_in", [P, 2, D]), m.sb("wo", [P, 2, D])
        eps = keep.eps
        lnc = m.sb("lnc", [E, 3, D])
        causal = m.sb("causal", [P, 1, P])
        inside = m.sb("inside", [P, NC, CH])
        x1, y = m.sb("x1", [P, 2, S, D]), m.sb("y", [P, 2, K, S, D])
        ix, w = m.sb("ix", [P, 2, K, S], I32), m.sb("w", [P, 2, K, S])
        sum2, x2, x2r = m.sb("sum2", [P, S, D]), m.sb("x2", [P, 2, S, D]), m.sb("x2r", [P, 2, S, D])
        stats2, moments2 = m.sb("stats2", [P, S, 6]), m.sb("moments2", [P, S, 2])
        lnvar2, rstd2 = m.sb("lnvar2", [P, S]), m.sb("rstd2", [P, S])
        xT = m.sb("xT", [P, C])
        v, sg = m.sb("v", [P, 2, S, DV]), m.sb("sg", [P, 2, S, DV])
        low = m.sb("low", [R, C])
        mag, em, lm, neg = (m.sb(n, [P, C]) for n in ("mag", "em", "lm", "neg"))
        rate, cum, left = m.sb("rate", [P, C]), m.sb("cum", [P, NC, CH]), m.sb("left", [P, NC, CH])
        eq, ek, eh = m.sb("eq", [P, 2, NC, CH]), m.sb("ek", [P, C]), m.sb("eh", [P, C])
        qg, kg, khT = m.sb("qg", [P, 2, C]), m.sb("kg", [P, 1, C]), m.sb("khT", [P, C])
        kgh = m.sb("kgh", [P, 2, HEADS, C])
        of_head = m.sb("of_head", [P, HEADS, 1])
        own = m.sb("own", [P, 1, DV])
        kvm = m.sb("kvm", [P, 2, DV])
        kh = m.sb("kh", [P, 2, 2, S, DK])
        state = m.sb("state", [P, NC, DV])
        am = m.sb("am", [P, 2, HEADS, P])
        o, sq = m.sb("o", [P, S, DV]), m.sb("sq", [P, S, HEADS, VH])
        ss, lss, ri = (m.sb(n, [P, S * HEADS]) for n in ("ss", "lss", "ri"))
        on, og = (m.sb(n, [P, S * HEADS, VH]) for n in ("on", "og"))
        ogT = m.sb("ogT", [P, S, 2, P])
        res = m.sb("res", [P, S, D])
        row3 = m.sb("row3", [P, 2, S, keep.WIDE])
        numbers = m.sb("numbers", [P, 1, T // P])
        x3T = m.sb("x3T", [P, C])
        first_of = m.sb("first_of", [P, 1, E])
        hit, cand, rank, picked = (m.sb(n, [P, S, E]) for n in ("hit", "cand", "rank", "picked"))
        chosen = m.sb("chosen", [P, S + 1, E])
        pref, place = m.sb("pref", [P, S]), m.sb("place", [P, S])
        ix3 = m.sb("ix3", [P, 2, S], I32)
        stats, moments = m.sb("stats", [P, S, 6]), m.sb("moments", [P, S, 2])
        lnvar, rstd = m.sb("lnvar", [P, S]), m.sb("rstd", [P, S])
        p_a = m.ps("p_a", [P, C])
        p_q, p_k = m.ps("p_q", [P, C]), m.ps("p_k", [P, C])
        p_f = m.ps("p_f", [P, C])
        p_r = m.ps("p_r", [P, C])
        p_near = p_r[:, 0:S * E].rearrange("p (s e) -> p s e", e=E)
        p_rank = p_r[:, S * E:(2 * S + 1) * E].rearrange("p (s e) -> p s e", e=E)
        p_kv = m.ps("p_kv", [P, 2, DV])
        p_s = m.ps("p_s", [P, HEADS, P])
        p_o = m.ps("p_o", [P, DV])

        s_w, s_zero, s_mask = m.sem("weights_loaded"), m.sem("zeroed"), m.sem("masks_made")
        s_x = [m.sem(f"x1_loaded{i}") for i in range(2)]
        s_y = [[m.sem(f"rows_fetched{i}{c}") for c in range(K)] for i in range(2)]
        s_ix, s_sum2, s_st2, s_mom2, s_lnv2, s_rstd2, s_x2, s_x2r = (m.sem(n) for n in (
            "ix_made", "sum_steps", "stats2_made", "moments2_made", "lnvar2_made", "rstd2_made", "x2_made", "x2_kept"))
        s_wo, s_iota, s_wT, s_cT = m.sem("wo_scaled"), m.sem("iota_made"), m.sem("small_transposed"), m.sem("cT_made")
        s_t3, s_x3T, s_near, s_route, s_ranks = (m.sem(n) for n in (
            "x3_transposed", "x3T_made", "affinity_product", "routing_steps", "rank_products"))
        s_number, s_placed = m.sem("numbered"), [m.sem(f"rows_placed{i}") for i in range(2)]
        (s_t, s_xT, s_low, s_lows, s_vg, s_v, s_sg, s_u, s_q, s_gate, s_neg, s_lm, s_rate, s_cum, s_left, s_eq, s_ek, s_eh,
         s_qk, s_kht, s_kh) = (m.sem(n) for n in (
             "x_transposed", "xT_made", "low_product", "low_made", "vg_product", "v_made", "silu_g_made", "u_product",
             "qk_product", "gate_steps", "neg_made", "lm_made", "rate_made", "cum_made", "left_made", "eq_made",
             "ek_made", "eh_made", "qk_scaled", "kh_transposed", "kh_made"))
        s_kv, s_s, s_state, s_am, s_o = (m.sem(n) for n in ("kv_product", "score_product", "state_made", "scores_masked",
                                                            "o_product"))
        s_oo = m.sem("o_kept")
        s_sq, s_ss, s_lss, s_ri, s_on, s_og, s_ogt, s_ogT, s_out = (m.sem(n) for n in (
            "squares_made", "sums_made", "ln_sums_made", "rms_made", "o_normed", "o_gated",
            "og_transposed", "ogT_made", "out_product"))
        s_res, s_st, s_mom, s_lnv, s_rstd, s_x3 = (m.sem(n) for n in (
            "residual_made", "stats_made", "moments_made", "lnvar_made", "rstd_made", "x3_made"))
        s_kgh, s_kvm = m.sem("kg_by_head"), m.sem("kv_masked")
        s_inside = m.sem("inside_made")
        s_turn, s_sp_turn, s_pool_turn = m.sem("vector_steps"), m.sem("sync_steps"), m.sem("pool_steps")
        block = m.block()
        WEIGHTS = 16 * 13

        @block.sync
        def _(sp):
            for par in range(2):
                sp.dma_start(x1[:, par], x1_tiles[par]).then_inc(s_x[par], 16)
            sp.dma_start(wq[:], Wq).then_inc(s_w, 16)
            sp.dma_start(wk[:], Wk).then_inc(s_w, 16)
            sp.dma_start(wvg[:, 0:DV], Wv).then_inc(s_w, 16)
            sp.dma_start(wvg[:, DV:], Wg).then_inc(s_w, 16)
            sp.dma_start(w1[:], gk_w1).then_inc(s_w, 16)
            sp.dma_start(w2[:], gk_w2).then_inc(s_w, 16)
            sp.dma_start(b2[:], gk_b2.rearrange("(p a) -> p a", a=1)).then_inc(s_w, 16)
            for h in range(2):
                sp.dma_start(gnw[VH * h:VH * h + VH], g_norm_w.rearrange("(p a) -> p a", a=1)).then_inc(s_w, 16)
            sp.dma_start(wo_in[:], Wo.rearrange("(j p) n -> p j n", p=P)).then_inc(s_w, 16)
            for n, v in enumerate((ffn.centroids, ffn.ln_g, ffn.ln_b)):
                sp.dma_start(lnc[:, n], v).then_inc(s_w, 16)
            for q in range(2, 4):
                sp.wait_ge(s_sum2, 2 * S * (q - 1))
                sp.dma_start(x1[:, q % 2], x1_tiles[q]).then_inc(s_x[q % 2], 16)
            sp.dma_start(keep.w1s[:], ffn.w1.rearrange("e p f -> p e f")).then_inc(keep.s_big, 16)
            for e in range(E):
                sp.dma_start(keep.w2s[:, e], ffn.w2[e].rearrange("(c p) d -> p c d", p=P)).then_inc(keep.s_big, 16)
            sp.dma_start(keep.b1s[:], ffn.b1.rearrange("(a e) f -> a e f", a=1).broadcast_to(keep.b1s.shape)).then_inc(keep.s_big, 16)
            sp.dma_start(keep.b2s[:], ffn.b2.rearrange("(a e) d -> a e d", a=1)).then_inc(keep.s_big, 16)
            with sp.Fori(2, Q // 2) as i:
                for par in range(2):
                    q = 2 * i + par
                    sp.wait_ge(s_sum2, 2 * S * (q - 1))
                    sp.sem_inc(s_sp_turn, 1)
                    sp.dma_start(x1[:, par], at_chunk(x1_tiles, q)).then_inc(s_x[par], 16)

        @block.gpsimd
        def _(pool):
            pool.iota(first_of[:, 0], pattern=[[-1, E]], base=E, channel_multiplier=0,
                      allow_small_or_imprecise_dtypes=True).then_inc(s_iota, 1)
            pool.iota(numbers[:, 0], pattern=[[P, T // P]], base=0, channel_multiplier=1,
                      allow_small_or_imprecise_dtypes=True).then_inc(s_iota, 1)
            pool.iota(keep.base[:, 0], pattern=[[T, E]], base=0, channel_multiplier=0,
                      allow_small_or_imprecise_dtypes=True).then_inc(s_iota, 1)
            pool.wait_ge(s_zero, 6)
            pool.affine_select(out=causal[:, 0], in_=causal[:, 0], compare_op=ALU.is_ge, fill=0.0, base=0,
                               pattern=[[1, P]], channel_multiplier=-1).then_inc(s_mask, 1)
            pool.wait_ge(s_mask, 1)
            pool.affine_select(out=causal[:, 0, CH:], in_=causal[:, 0, CH:], compare_op=ALU.is_ge, fill=0.0, base=-CH,
                               pattern=[[0, CH]], channel_multiplier=1).then_inc(s_mask, 1)
            for n, (tile, width) in enumerate(((of_head, 1), (own, VH))):
                view = tile[:].rearrange("p h a -> p (h a)").rearrange("p (h e) -> p h e", h=HEADS)
                pool.affine_select(out=view, in_=view, compare_op=ALU.is_ge, fill=0.0, base=0,
                                   pattern=[[-DH, HEADS], [0, width]], channel_multiplier=1).then_inc(s_mask, 1)
                pool.wait_ge(s_mask, 3 + 2 * n)
                pool.affine_select(out=view, in_=view, compare_op=ALU.is_ge, fill=0.0, base=DH - 1,
                                   pattern=[[DH, HEADS], [0, width]], channel_multiplier=-1).then_inc(s_mask, 1)
            pool.wait_ge(s_mask, 6)

            def fetch(q, par, c):
                pool.wait_ge(s_ix, 2 * (q + 1))
                if later(q, 2):
                    pool.wait_ge(s_sum2, 2 * S * (q - 1))
                pool.sem_inc(s_pool_turn, 1)
                for s in range(S):
                    pool.indirect_dma_start(
                        out=y[:, par, c, s], out_offset=None, in_=keep.ye,
                        in_offset=bass.IndirectOffsetOnAxis(ap=ix[:, par, c, s:s + 1], axis=0),
                        bounds_check=keep.ye.shape[0] - 1, oob_is_err=False).then_inc(s_y[par][c], 16)

            def gate_o(q, par):
                pool.wait_ge(s_on, q + 1)
                pool.wait_ge(s_sg, S * (q + 1))
                pool.wait_ge(s_ogt, 2 * q)
                pool.tensor_tensor(og[:], on[:], sg[:, par].rearrange("p s (h e) -> p (s h) e", h=HEADS),
                                   ALU.mult).then_inc(s_og, 1)

            def add_rate(q, par):
                pool.wait_ge(s_lm, q + 1)
                pool.wait_ge(s_neg, q + 1)
                pool.wait_ge(s_cum, q)
                pool.tensor_tensor(rate[:], neg[:], lm[:], ALU.add).then_inc(s_rate, 1)

            def rate_left(q, par):
                pool.wait_ge(s_cum, q + 1)
                pool.wait_ge(s_eh, q)
                pool.tensor_tensor(left[:], cum[:, :, CH - 1:CH].broadcast_to((P, NC, CH)), cum[:],
                                   ALU.subtract).then_inc(s_left, 1)

            def send(q, par):
                pool.wait_ge(s_route, 10 * (q + 1))
                pool.sem_inc(s_pool_turn, 1)
                pool.wait_ge(s_number, q + 1)
                pool.sem_inc(s_pool_turn, 1)
                for s in range(S):
                    pool.indirect_dma_start(
                        out=keep.xs, out_offset=bass.IndirectOffsetOnAxis(ap=ix3[:, par, s:s + 1], axis=0),
                        in_=row3[:, par, s], in_offset=None, bounds_check=E * T - 1,
                        oob_is_err=False).then_inc(s_placed[par], 16)

            run_chunks(Q, 2 * S, pool.Fori, [
                (0, 2, lambda q, par: fetch(q, par, 0)), (2, -1, gate_o), (3, 2, lambda q, par: fetch(q, par, 1)),
                (4, 1, add_rate), (4, 1, rate_left), (7.5, -2, send)], lambda q, par, n: None)
            for par in range(2):
                pool.wait_ge(s_placed[par], PLACES * (Q // 2))

        @block.scalar
        def _(act):
            act.preload_act_table_set(LN_EXP)
            act.wait_ge(s_w, WEIGHTS)
            act.activation(nb2[:], b2[:], ACT.Copy, scale=-1.0).then_inc(s_gate, 1)
            for j in range(2):
                act.activation(wo[:, j], wo_in[:, j], ACT.Copy, scale=gnw[:]).then_inc(s_wo, 1)
            act.wait_ge(s_gate, 1)
            act.wait_ge(s_zero, 6)
            act.wait_ge(s_iota, 3)
            act.wait_ge(s_mask, 6)

            def rstd_of(q, moments, lnvar, rstd, s_mom, s_lnv, s_rstd, s_used):
                act.wait_ge(s_mom, S * (q + 1))
                act.activation(lnvar[:], moments[:, :, 1], ACT.Ln, bias=eps[:]).then_inc(s_lnv, 1)
                act.wait_ge(s_lnv, q + 1)
                act.wait_ge(s_used, S * q)
                act.activation(rstd[:], lnvar[:], ACT.Exp, scale=-0.5).then_inc(s_rstd, 1)

            def x2_rstd(q, par):
                rstd_of(q, moments2, lnvar2, rstd2, s_mom2, s_lnv2, s_rstd2, s_x2)

            def x3_rstd(q, par):
                rstd_of(q, moments, lnvar, rstd, s_mom, s_lnv, s_rstd, s_x3)

            def take_x2(q, par):
                act.wait_ge(s_t, q + 1)
                act.wait_ge(s_vg, S * q)
                act.wait_ge(s_q, 2 * q)
                act.activation(xT[:], p_a[:], ACT.Copy).then_inc(s_xT, 1)

            def keep_x2(q, par):
                act.wait_ge(s_x2, S * (q + 1))
                if later(q, 2):
                    act.wait_ge(s_res, q - 1)
                act.activation(x2r[:, par], x2[:, par], ACT.Copy).then_inc(s_x2r, 1)

            def take_low(q, par):
                act.wait_ge(s_low, q + 1)
                act.wait_ge(s_u, q)
                act.activation(low[:], p_a[0:R, :], ACT.Copy).then_inc(s_lows, 1)

            def take_vg(q, par, tiles):
                if later(q, 2):
                    act.wait_ge(s_o, S * (q - 1))
                    act.wait_ge(s_og, q - 1)
                for s in tiles:
                    p = (p_q, p_k)[s % 2]
                    act.wait_ge(s_vg, S * q + s + 1)
                    act.activation(sg[:, par, s], p[:, DV:], ACT.Silu).then_inc(s_sg, 1)
                    act.activation(v[:, par, s], p[:, 0:DV], ACT.Copy).then_inc(s_v, 1)
                if S - 1 in tiles:
                    act.preload_act_table_set(LN_EXP)

            def gate(q, par):
                act.wait_ge(s_u, q + 1)
                act.activation(mag[:], p_a[:], ACT.Abs, bias=b2[:]).then_inc(s_gate, 1)
                act.wait_ge(s_rate, q)
                act.activation(neg[:], p_a[:], ACT.Relu, scale=-1.0, bias=nb2[:]).then_inc(s_neg, 1)
                act.wait_ge(s_gate, 2 * q + 2)
                act.activation(em[:], mag[:], ACT.Exp, scale=-1.0).then_inc(s_gate, 1)
                act.wait_ge(s_gate, 2 * q + 3)
                act.activation(lm[:], em[:], ACT.Ln, bias=1.0).then_inc(s_lm, 1)

            def decays(q, par):
                flat = cum[:].rearrange("p c t -> p (c t)")
                act.wait_ge(s_cum, q + 1)
                if later(q, 2):
                    act.wait_ge(s_state, NC * (q - 1))
                act.activation(eq[:, par].rearrange("p c t -> p (c t)"), flat, ACT.Exp, scale=-1 / GATE).then_inc(s_eq, 1)
                act.wait_ge(s_qk, 3 * q)
                act.activation(ek[:], flat, ACT.Exp, scale=1 / GATE).then_inc(s_ek, 1)
                act.wait_ge(s_left, q + 1)
                act.activation(eh[:], left[:].rearrange("p c t -> p (c t)"), ACT.Exp, scale=-1 / GATE).then_inc(s_eh, 1)

            def keys_by_head(q, par):
                act.wait_ge(s_qk, 3 * q + 2)
                if later(q, 2):
                    act.wait_ge(s_s, S * (q - 1))
                for h in range(HEADS):
                    act.activation(kgh[:, par, h], kg[:, 0], ACT.Copy, scale=of_head[:, h]).then_inc(s_kgh, 1)

            def take_kh(q, par):
                act.wait_ge(s_kht, q + 1)
                if later(q, 2):
                    act.wait_ge(s_kv, S * (q - 1))
                for c in range(2):
                    part = slice(CH * c, CH * c + CH)
                    act.activation(kh[part, par, c], p_a[part, :].rearrange("p (s d) -> p s d", s=S),
                                   ACT.Copy).then_inc(s_kh, 1)

            def take_o(q, s):
                act.wait_ge(s_o, S * q + s + 1)
                act.wait_ge(s_on, q)
                act.activation(o[:, s], p_o[:], ACT.Copy).then_inc(s_oo, 1)
                act.wait_ge(s_oo, S * q + s + 1)
                act.wait_ge(s_ss, q)
                act.activation(sq[:, s].rearrange("p h e -> p (h e)"), o[:, s], ACT.Square).then_inc(s_sq, 1)

            def o_rms(q, par):
                act.wait_ge(s_ss, q + 1)
                act.activation(lss[:], ss[:], ACT.Ln, scale=1.0 / VH, bias=eps[:]).then_inc(s_lss, 1)
                act.wait_ge(s_lss, q + 1)
                act.wait_ge(s_on, q)
                act.activation(ri[:], lss[:], ACT.Exp, scale=-0.5).then_inc(s_ri, 1)

            def take_x3(q, par):
                act.wait_ge(s_t3, q + 1)
                act.wait_ge(s_near, q)
                act.activation(x3T[:], p_r[:], ACT.Copy).then_inc(s_x3T, 1)
                if later(q, 2):
                    act.wait_ge(s_placed[par], PLACES // 2 * (q - par))
                at = slice(S * q, S * q + S) if isinstance(q, int) else bass.ds(S * q, S)
                act.activation(row3[:, par, :, D + 1], numbers[:, 0, at], ACT.Copy).then_inc(s_number, 1)

            run_chunks(Q, 2 * S, act.Fori, [
                (0, -1, lambda q, par: take_o(q, 3)), (0, 1, take_x2), (1, -1, o_rms), (1, 1, take_low),
                (2, 0, lambda q, par: take_o(q, 0)), (2, -2, x3_rstd), (2, 1, gate), (3, 0, keep_x2),
                (3, 1, lambda q, par: take_vg(q, par, (0, 1))), (4, 0, lambda q, par: take_o(q, 1)),
                (4, 1, lambda q, par: take_vg(q, par, (2, 3))), (5, 1, decays), (5, -2, take_x3), (5, 2, x2_rstd),
                (6, 0, lambda q, par: take_o(q, 2)), (6, 1, keys_by_head), (7, 1, take_kh)], lambda q, par, n: None)

        @block.vector
        def _(dve):
            dve.memset(causal[:], 1.0).then_inc(s_zero, 1)
            dve.memset(inside[:], 1.0).then_inc(s_zero, 1)
            dve.memset(of_head[:], 1.0).then_inc(s_zero, 1)
            dve.memset(own[:], 1.0).then_inc(s_zero, 1)
            dve.memset(kh[:], 0.0).then_inc(s_zero, 1)
            dve.memset(chosen[:], 0.0).then_inc(s_zero, 1)
            dve.wait_ge(s_zero, 6)
            dve.memset(inside[:, :, 0:1], 0.0).then_inc(s_inside, 1)
            dve.wait_ge(s_inside, 1)
            dve.wait_ge(s_mask, 6)
            dve.wait_ge(s_iota, 3)
            dve.wait_ge(s_wT, 1)
            for n, tile in enumerate((keep.cT, keep.gT, keep.bT)):
                dve.tensor_copy(tile[:], p_kv[:, 0, E * n:E * n + E]).then_inc(s_cT, 1)

            def moments_of(q, src, stats, moments, s_st, s_mom):
                for s in range(S):
                    dve.bn_stats(stats[:, s], src[:, s]).then_inc(s_st, 1)
                dve.wait_ge(s_st, S * (q + 1))
                dve.sem_inc(s_turn, 1)
                for s in range(S):
                    dve.bn_aggr(moments[:, s], stats[:, s]).then_inc(s_mom, 1)

            def indices(q, par):
                at = slice(S * q, S * q + S) if isinstance(q, int) else bass.ds(S * q, S)
                if later(q, 2):
                    for c in range(K):
                        dve.wait_ge(s_y[par][c], ROUND // 2 * (q - par))
                dve.tensor_copy(ix[:, par], keep.from_slot[:, :, at]).then_inc(s_ix, 1)
                dve.tensor_copy(w[:, par], keep.weight[:, :, at]).then_inc(s_ix, 1)

            def sum_expert(q, par, c):
                dve.wait_ge(s_ix, 2 * q + 2)
                if c == 0:
                    dve.wait_ge(s_x[par], 8 * (q - par) + 16)
                    dve.wait_ge(s_x2, S * q)
                else:
                    dve.wait_ge(s_sum2, 2 * S * q + S)
                dve.wait_ge(s_y[par][c], ROUND // 2 * (q - par) + ROUND)
                for s in range(S):
                    dve.scalar_tensor_tensor(out=sum2[:, s], in0=y[:, par, c, s], scalar=w[:, par, c, s:s + 1],
                                             in1=sum2[:, s] if c else x1[:, par, s], op0=ALU.mult,
                                             op1=ALU.add).then_inc(s_sum2, 1)
                if c == K - 1:
                    dve.wait_ge(s_sum2, 2 * S * q + 2 * S)
                    moments_of(q, sum2, stats2, moments2, s_st2, s_mom2)

            def norm_x2(q, par):
                dve.wait_ge(s_rstd2, q + 1)
                dve.wait_ge(s_mom2, S * (q + 1))
                if later(q, 2):
                    dve.wait_ge(s_t, q - 1)
                    dve.wait_ge(s_x2r, q - 1)
                for s in range(S):
                    dve.tensor_scalar(x2[:, par, s], sum2[:, s], moments2[:, s, 0:1], rstd2[:, s:s + 1],
                                      ALU.subtract, ALU.mult).then_inc(s_x2, 1)

            def cumulate(q, par):
                dve.wait_ge(s_rate, q + 1)
                dve.wait_ge(s_ek, q)
                dve.wait_ge(s_left, q)
                dve.tensor_tensor_scan(cum[:].rearrange("p c t -> p (c t)"), inside[:].rearrange("p c t -> p (c t)"),
                                       rate[:], 0.0, ALU.mult, ALU.add).then_inc(s_cum, 1)

            def scale_qk(q, par):
                dve.wait_ge(s_q, 2 * q + 2)
                dve.wait_ge(s_ek, q + 1)
                dve.wait_ge(s_kgh, HEADS * q)
                dve.tensor_tensor(kg[:, 0], p_k[:], ek[:], ALU.mult).then_inc(s_qk, 1)
                dve.wait_ge(s_eq, q + 1)
                if later(q, 2):
                    dve.wait_ge(s_o, S * (q - 1))
                dve.scalar_tensor_tensor(out=qg[:, par], in0=p_q[:], scalar=SCALE,
                                         in1=eq[:, par].rearrange("p c t -> p (c t)"), op0=ALU.mult,
                                         op1=ALU.mult).then_inc(s_qk, 1)
                dve.wait_ge(s_eh, q + 1)
                dve.wait_ge(s_kht, q)
                dve.tensor_tensor(khT[:], p_k[:], eh[:], ALU.mult).then_inc(s_qk, 1)

            def attend(q, par, n):
                if n % 2 == 0:
                    return
                s = n // 2
                dve.wait_ge(s_kv, S * q + s + 1)
                if later(q, 1) or s >= 1:
                    dve.wait_ge(s_state, NC * q + 2 * s)
                dve.tensor_tensor(kvm[:], p_kv[:], own[:].broadcast_to((P, 2, DV)), ALU.mult).then_inc(s_kvm, 1)
                dve.wait_ge(s_kvm, S * q + s + 1)
                if later(q, 1) or s >= 3:
                    dve.wait_ge(s_o, S * q + s - 2)
                for c in range(2):
                    i = 2 * s + c
                    if par == 0 and i == 0:
                        dve.tensor_copy(state[:, 1], kvm[:, 0]).then_inc(s_state, 1)
                        continue
                    dve.wait_ge(s_state, NC * q + i)
                    dve.scalar_tensor_tensor(out=state[:, (i + 1) % NC], in0=state[:, i % NC],
                                             scalar=eq[:, par, i, CH - 1:CH], in1=kvm[:, c], op0=ALU.mult,
                                             op1=ALU.add).then_inc(s_state, 1)
                dve.wait_ge(s_s, S * q + s + 1)
                if later(q, 1) or s >= 2:
                    dve.wait_ge(s_o, S * q + s - 1)
                dve.tensor_tensor(am[:, s % 2], p_s[:], causal[:].broadcast_to((P, HEADS, P)), ALU.mult).then_inc(s_am, 1)

            def sum_squares(q, par):
                dve.wait_ge(s_sq, S * (q + 1))
                dve.wait_ge(s_lss, q)
                dve.tensor_reduce(ss[:], sq[:].rearrange("p s h e -> p (s h) e"), AX.X, ALU.add).then_inc(s_ss, 1)

            def norm_o(q, par):
                dve.wait_ge(s_ri, q + 1)
                dve.wait_ge(s_oo, S * (q + 1))
                dve.wait_ge(s_og, q)
                dve.tensor_tensor(on[:], o[:].rearrange("p s (h e) -> p (s h) e", h=HEADS),
                                  ri[:, :, None].broadcast_to((P, S * HEADS, VH)), ALU.mult).then_inc(s_on, 1)

            def take_og(q, g):
                dve.wait_ge(s_ogt, 2 * q + g + 1)
                dve.wait_ge(s_out, q)
                dve.tensor_copy(ogT[:, 2 * g:2 * g + 2].rearrange("p s j t -> p (s j t)"), p_f[:]).then_inc(s_ogT, 1)

            def residual(q, par):
                dve.wait_ge(s_out, q + 1)
                dve.wait_ge(s_x3, S * q)
                dve.wait_ge(s_x2r, q + 1)
                dve.tensor_tensor(res[:], p_f[:].rearrange("p (s d) -> p s d", s=S), x2r[:, par],
                                  ALU.add).then_inc(s_res, 1)
                dve.wait_ge(s_res, q + 1)
                moments_of(q, res, stats, moments, s_st, s_mom)

            def norm_x3(q, par):
                dve.wait_ge(s_rstd, q + 1)
                dve.wait_ge(s_mom, S * (q + 1))
                if later(q, 2):
                    dve.wait_ge(s_placed[par], PLACES // 2 * (q - par))
                for s in range(S):
                    dve.tensor_scalar(row3[:, par, s, 0:D], res[:, s], moments[:, s, 0:1], rstd[:, s:s + 1],
                                      ALU.subtract, ALU.mult).then_inc(s_x3, 1)

            def step(q, n, ins):
                ins.then_inc(s_route, 1)
                dve.wait_ge(s_route, 10 * q + n)

            def choose(q, par):
                best = row3[:, par, :, D:D + 1]
                wide = (P, S, E)
                dve.wait_ge(s_near, q + 1)
                if later(q, 2):
                    dve.wait_ge(s_placed[par], PLACES // 2 * (q - par))
                step(q, 1, dve.tensor_reduce(best, p_near, AX.X, ALU.max))
                step(q, 2, dve.tensor_tensor(hit[:], p_near, best.broadcast_to(wide), ALU.is_equal))
                step(q, 3, dve.tensor_tensor(cand[:], hit[:], first_of[:].broadcast_to(wide), ALU.mult))
                step(q, 4, dve.tensor_reduce(pref[:], cand[:], AX.X, ALU.max))
                dve.wait_ge(s_ranks, q)
                step(q, 5, dve.tensor_tensor(chosen[:, 0:S], cand[:], pref[:, :, None].broadcast_to(wide), ALU.is_equal))

            def locate(q, par):
                dve.wait_ge(s_ranks, q + 1)
                step(q, 6, dve.tensor_tensor(rank[:], p_rank[:, 0:S], keep.base[:].broadcast_to((P, S, E)), ALU.add))
                step(q, 7, dve.tensor_tensor(keep.base[:], p_rank[:, S:S + 1], keep.base[:], ALU.add))
                step(q, 8, dve.tensor_tensor(picked[:], rank[:], chosen[:, 0:S], ALU.mult))
                step(q, 9, dve.tensor_reduce(place[:], picked[:], AX.X, ALU.add))
                step(q, 10, dve.tensor_copy(ix3[:, par], place[:]))

            run_chunks(Q, 2 * S, dve.Fori, [
                (0, -1, sum_squares), (0, 2, indices), (1, -2, residual), (2, -1, norm_o), (3, -2, norm_x3),
                (3, 2, lambda q, par: sum_expert(q, par, 0)), (4, 1, cumulate), (5, 2, lambda q, par: sum_expert(q, par, 1)),
                (5, -1, lambda q, par: take_og(q, 0)), (6, 1, scale_qk), (6, -2, choose), (6, 2, norm_x2),
                (7, -1, lambda q, par: take_og(q, 1)), (7.5, -2, locate)], attend)

        @block.tensor
        def _(pe):
            pe.wait_ge(s_w, WEIGHTS)
            for n in range(3):
                t = pe.transpose(p_kv[:, 0, E * n:E * n + E], lnc[:, n], keep.ident[0:E, 0:E])
            t.then_inc(s_wT, 1)
            pe.wait_ge(s_cT, 3)
            pe.wait_ge(s_wo, 2)

            def turn_x2(q, par):
                pe.wait_ge(s_x2, S * (q + 1))
                pe.wait_ge(s_kh, 2 * q)
                for s in range(S):
                    t = pe.transpose(p_a[:, P * s:P * s + P], x2[:, par, s], keep.ident[:])
                t.then_inc(s_t, 1)

            def project_low(q, par):
                pe.wait_ge(s_xT, q + 1)
                pe.matmul(p_a[0:R, :], w1[:], xT[:], start=True, stop=True).then_inc(s_low, 1)

            def project_vg(q, par, tiles):
                pe.wait_ge(s_qk, 3 * q)
                for s in tiles:
                    if s >= 2:
                        pe.wait_ge(s_v, S * q + s - 1)
                    pe.matmul((p_q, p_k)[s % 2][:], xT[:, P * s:P * s + P], wvg[:], start=True,
                              stop=True).then_inc(s_vg, 1)

            def project_u(q, par):
                pe.wait_ge(s_lows, q + 1)
                pe.matmul(p_a[:], w2[:], low[:], start=True, stop=True).then_inc(s_u, 1)

            def project_qk(q, par):
                pe.wait_ge(s_v, S * (q + 1))
                pe.matmul(p_q[:], wq[:], xT[:], start=True, stop=True).then_inc(s_q, 1)
                pe.matmul(p_k[:], wk[:], xT[:], start=True, stop=True).then_inc(s_q, 1)

            def turn_kh(q, par):
                pe.wait_ge(s_qk, 3 * q + 3)
                pe.wait_ge(s_neg, q + 1)
                pe.wait_ge(s_gate, 2 * q + 3)
                for s in range(S):
                    t = pe.transpose(p_a[:, P * s:P * s + P], khT[:, P * s:P * s + P], keep.ident[:])
                t.then_inc(s_kht, 1)

            def products(q, par, s):
                pe.wait_ge(s_kgh, HEADS * (q + 1))
                if later(q, 1) or s:
                    pe.wait_ge(s_am, S * q + s)
                cols = slice(P * s, P * s + P)
                for h in range(HEADS):
                    t = pe.matmul(p_s[:, h], kgh[:, par, h, cols], qg[:, par, cols], start=True, stop=True)
                t.then_inc(s_s, 1)
                pe.wait_ge(s_kh, 2 * q + 2)
                if later(q, 1) or s:
                    pe.wait_ge(s_kvm, S * q + s)
                for c in range(2):
                    t = pe.matmul(p_kv[:, c], kh[:, par, c, s], v[:, par, s], start=True, stop=True)
                t.then_inc(s_kv, 1)

            def output(q, par, s):
                if later(q, 1) or s >= 1:
                    pe.wait_ge(s_oo, S * q + s)
                pe.wait_ge(s_am, S * q + s + 1)
                pe.wait_ge(s_state, NC * q + 2 * s + 1)
                for h in range(HEADS):
                    out = slice(VH * h, VH * h + VH)
                    pe.matmul(p_o[:, out], am[:, s % 2, h], v[:, par, s, out], start=(h == 0), stop=False,
                              skip_group_check=True)
                for c in range(2):
                    i = 2 * s + c
                    if par == 0 and i == 0:
                        continue
                    cols = slice(P * s + CH * c, P * s + CH * c + CH)
                    t = pe.matmul(p_o[CH * c:CH * c + CH, :], qg[:, par, cols], state[:, i % NC],
                                  start=False, stop=(c == 1), skip_group_check=True)
                t.then_inc(s_o, 1)

            def attend(q, par, n):
                if n % 2 == 0:
                    products(q, par, n // 2)
                else:
                    output(q, par, n // 2)

            def turn_og(q, g):
                pe.wait_ge(s_og, q + 1)
                if g:
                    pe.wait_ge(s_ogT, 2 * q + 1)
                elif later(q, 1):
                    pe.wait_ge(s_res, q)
                for s in range(2):
                    for j in range(2):
                        at = P * (2 * s + j)
                        src = og[:, HEADS * (2 * g + s) + 2 * j:HEADS * (2 * g + s) + 2 * j + 2]
                        t = pe.transpose(p_f[:, at:at + P], src.rearrange("p h e -> p (h e)"), keep.ident[:])
                t.then_inc(s_ogt, 1)

            def project_out(q, par):
                pe.wait_ge(s_ogT, 2 * q + 2)
                for s in range(S):
                    for j in range(2):
                        t = pe.matmul(p_f[:, P * s:P * s + P], ogT[:, s, j], wo[:, j], start=(j == 0), stop=(j == 1))
                t.then_inc(s_out, 1)

            def turn_x3(q, par):
                pe.wait_ge(s_x3, S * (q + 1))
                if later(q, 1):
                    pe.wait_ge(s_route, 10 * q)
                for s in range(S):
                    t = pe.transpose(p_r[:, P * s:P * s + P], row3[:, par, s, 0:D], keep.ident[:])
                t.then_inc(s_t3, 1)

            def affinities(q, par):
                pe.wait_ge(s_x3T, q + 1)
                for s in range(S):
                    t = pe.matmul(p_near[:, s], x3T[:, P * s:P * s + P], keep.cT[:], start=True, stop=True)
                t.then_inc(s_near, 1)

            def ranks(q, par):
                pe.wait_ge(s_route, 10 * q + 5)
                flat = p_rank.rearrange("p s e -> p (s e)")
                pe.matmul(flat, keep.before[:], chosen[:].rearrange("p s e -> p (s e)"), start=True, stop=True)
                for back in range(1, S + 1):
                    t = pe.matmul(flat[:, E * back:], keep.ones[:],
                                  chosen[:, 0:S + 1 - back].rearrange("p s e -> p (s e)"), start=False, stop=True,
                                  skip_group_check=True)
                t.then_inc(s_ranks, 1)

            run_chunks(Q, 2 * S, pe.Fori, [
                (0, 1, turn_x2), (0, -2, project_out), (1, 1, project_low), (2, 1, project_u),
                (3, 1, lambda q, par: project_vg(q, par, (0, 1))), (4, 1, lambda q, par: project_vg(q, par, (2, 3))),
                (4, -1, lambda q, par: turn_og(q, 0)), (4, -2, turn_x3), (5, 1, project_qk), (5, -2, affinities),
                (6, -1, lambda q, par: turn_og(q, 1)), (7, -2, ranks), (7, 1, turn_kh)], attend)


def routed_ffn(nc, keep, ffn, out):
    T = keep.x1.shape[0]
    E, D = ffn.centroids.shape
    F = ffn.w1.shape[2]
    FB = F // P
    NT = T // P
    TILES = NT + E
    NONE = 4.0 * E * T
    WIDE = keep.WIDE
    out_rows = out.rearrange("b l d -> (b l) d")
    w1s, w2s, b1s, gT, bT, eps = keep.w1s, keep.w2s, keep.b1s, keep.gT, keep.bT, keep.eps

    with ExitStack() as outer:
        k = Space(nc, outer, "ffn")
        owner = k.sb("owner", [P, TILES], I32)
        start = k.sb("start", [P, TILES], I32)

        with ExitStack() as ctx:
            m = Space(nc, ctx, "cut")
            full = m.sb("full", [P, 1, NT])
            order = m.sb("order", [P, TILES, 1])
            first_row = m.sb("first_row", [P, E])
            lane = m.sb("lane", [P, 1])
            count = m.sb("count", [P, E])
            more = m.sb("more", [P, E, NT])
            size, end, spare = m.sb("size", [P, E]), m.sb("end", [P, E]), m.sb("spare", [P, 1, E])
            passed, skip = m.sb("passed", [P, TILES, E]), m.sb("skip", [P, TILES, E])
            who, at = m.sb("who", [P, TILES]), m.sb("at", [P, TILES])
            row, limit, over = m.sb("row", [P, E]), m.sb("limit", [P, E]), m.sb("over", [P, E])
            pad_at = m.sb("pad_at", [P, E], I32)
            pad = m.sb("pad", [P, WIDE])
            s_iota, s_r, s_pad, s_padded = m.sem("iota_made"), m.sem("cutting_steps"), m.sem("pad_made"), m.sem("padded")
            s_last = m.sem("last_tile_padded")
            block = m.block()
            PADS = 10

            @block.sync
            def _(sp):
                sp.wait_ge(s_pad, 2)
                sp.dma_start(keep.xs[E * T:E * T + P, :], pad[:]).then_inc(s_last, 16)
                sp.wait_ge(s_last, 16)

            @block.gpsimd
            def _(pool):
                for tile, step, base in ((full[:, 0], P, 0), (order[:, :, 0], 1, 0), (first_row[:], T, 0)):
                    pool.iota(tile, pattern=[[step, tile.shape[1]]], base=base, channel_multiplier=0,
                              allow_small_or_imprecise_dtypes=True).then_inc(s_iota, 1)
                pool.iota(lane[:], pattern=[[1, 1]], base=0, channel_multiplier=1,
                          allow_small_or_imprecise_dtypes=True).then_inc(s_iota, 1)
                pool.wait_ge(s_r, PADS)
                pool.wait_ge(s_pad, 2)
                for e in range(E):
                    pool.indirect_dma_start(
                        out=keep.xs, out_offset=bass.IndirectOffsetOnAxis(ap=pad_at[:, e:e + 1], axis=0),
                        in_=pad[:], in_offset=None, bounds_check=E * T - 1, oob_is_err=False).then_inc(s_padded, 16)
                pool.wait_ge(s_padded, 16 * E)

            @block.vector
            def _(dve):
                steps = [0]

                def step(ins):
                    ins.then_inc(s_r, 1)
                    steps[0] += 1
                    dve.wait_ge(s_r, steps[0])

                dve.memset(pad[:, 0:D + 1], 0.0).then_inc(s_pad, 1)
                dve.memset(pad[:, D + 1:], NONE).then_inc(s_pad, 1)
                dve.wait_ge(s_iota, 4)
                step(dve.tensor_tensor(count[:], keep.base[:, 0], first_row[:], ALU.subtract))
                step(dve.tensor_tensor(more[:], count[:, :, None].broadcast_to((P, E, NT)),
                                       full[:].broadcast_to((P, E, NT)), ALU.is_gt))
                step(dve.tensor_reduce(size[:], more[:], AX.X, ALU.add))
                step(dve.tensor_scalar(limit[:], size[:], float(P), None, ALU.mult))
                step(dve.tensor_tensor(limit[:], limit[:], first_row[:], ALU.add))
                step(dve.tensor_scalar(row[:], keep.base[:, 0], lane[:], None, ALU.add))
                step(dve.tensor_tensor(over[:], row[:], limit[:], ALU.is_ge))
                step(dve.tensor_scalar(over[:], over[:], NONE, None, ALU.mult))
                step(dve.tensor_tensor(row[:], row[:], over[:], ALU.add))
                step(dve.tensor_copy(pad_at[:], row[:]))
                step(dve.tensor_tensor_scan(end[:], keep.ones[:, 0:E], size[:], 0.0, ALU.mult, ALU.add))
                step(dve.tensor_tensor(passed[:], order[:].broadcast_to((P, TILES, E)),
                                       end[:, None, :].broadcast_to((P, TILES, E)), ALU.is_ge))
                step(dve.tensor_reduce(who[:], passed[:], AX.X, ALU.add))
                step(dve.tensor_scalar(who[:], who[:], float(E - 1), None, ALU.min))
                step(dve.tensor_copy(owner[:], who[:]))
                step(dve.tensor_scalar(spare[:, 0], size[:], -1.0, float(NT), ALU.mult, ALU.add))
                step(dve.tensor_tensor(skip[:], passed[:], spare[:].broadcast_to((P, TILES, E)), ALU.mult))
                step(dve.tensor_reduce(at[:], skip[:], AX.X, ALU.add))
                step(dve.tensor_tensor(at[:], at[:], order[:, :, 0], ALU.add))
                step(dve.tensor_scalar(at[:], at[:], float(E * NT), float(P), ALU.min, ALU.mult))
                step(dve.tensor_copy(start[:], at[:]))

        with ExitStack() as ctx:
            m = Space(nc, ctx, "tiles")
            DEEP = 4
            rows = m.sb("rows", [P, DEEP, WIDE])
            twice = m.sb("twice", [P, DEEP, WIDE])
            stats, moments = m.sb("stats", [P, DEEP, 6]), m.sb("moments", [P, DEEP, 2])
            lnvar, rstd = m.sb("lnvar", [P, DEEP]), m.sb("rstd", [P, DEEP])
            xn, xT = m.sb("xn", [P, 2, D]), m.sb("xT", [P, 2, P])
            h, hT = m.sb("h", [P, 2, F]), m.sb("hT", [P, 2, F])
            away, alpha = m.sb("away", [P, DEEP]), m.sb("alpha", [P, DEEP])
            token = m.sb("token", [P, DEEP], I32)
            res = m.sb("res", [P, DEEP, D])
            ostats, omoments = m.sb("ostats", [P, DEEP, 6]), m.sb("omoments", [P, DEEP, 2])
            olnvar, orstd = m.sb("olnvar", [P, DEEP]), m.sb("orstd", [P, DEEP])
            done = m.sb("done", [P, DEEP, D])
            p_t = [m.ps(f"p_t{i}", [P, 512]) for i in range(2)]
            p_h = [m.ps(f"p_h{i}", [P, F]) for i in range(2)]
            p_r = [m.ps(f"p_r{i}", [P, F]) for i in range(2)]
            p_y = [m.ps(f"p_y{i}", [P, 512]) for i in range(2)]
            s_in = [m.sem(f"rows_loaded{i}") for i in range(DEEP)]
            s_out = [m.sem(f"rows_sent{i}") for i in range(DEEP)]
            s_st, s_mom, s_lnv, s_rstd, s_xn, s_twice = (m.sem(n) for n in (
                "stats_made", "moments_made", "lnvar_made", "rstd_made", "xn_made", "doubled"))
            s_t, s_xT, s_h, s_hs, s_r, s_hT, s_yp = (m.sem(n) for n in (
                "transposed", "xT_made", "h_product", "h_made", "h_transposed", "hT_made", "y_product"))
            s_exp, s_one, s_alpha, s_token, s_res = (m.sem(n) for n in (
                "exp_made", "one_added", "alpha_made", "token_made", "residual_made"))
            s_ost, s_omom, s_olnv, s_orstd, s_done = (m.sem(n) for n in (
                "out_stats", "out_moments", "out_lnvar", "out_rstd", "output_made"))
            s_turn, s_sp_turn, s_pool_turn = m.sem("vector_steps"), m.sem("sync_steps"), m.sem("pool_steps")
            block = m.block()
            WEIGHTS = 16 * (E + 3)

            def pipeline(eng, *stages):
                depth = max(stage[0] for stage in stages) + 1
                looked_up = [stage for stage in stages if len(stage) == 3]

                def turns(first):
                    known = isinstance(first, int)
                    entry = {}
                    if looked_up:
                        table = looked_up[0][2]
                        late, early = max(s[0] for s in looked_up), min(s[0] for s in looked_up)
                        for d in range(-late, DEEP - early):
                            j = first + d
                            if not known or 0 <= j < TILES:
                                entry[d] = eng.value_load(table[0:1, j:j + 1] if known else table[0:1, bass.ds(j, 1)],
                                                          min_val=0, max_val=E * T if table is start else E - 1)
                    for b in range(DEEP):
                        for n, work, *tables in stages:
                            j = first + b - n
                            if not known or 0 <= j < TILES:
                                work(j, (b - n) % DEEP, *(entry[b - n] for _ in tables))

                head = (-(-depth // DEEP) + 1) * DEEP
                for first in range(0, head, DEEP):
                    turns(first)
                with eng.Fori(0, (TILES - head) // DEEP) as i:
                    turns(DEEP * i + head)
                for first in range(TILES, TILES + depth - 1, DEEP):
                    turns(first)

            def rounds(j, b):
                return (j - b) * (16 // DEEP)

            @block.sync
            def _(sp):
                def load(j, b, first):
                    if later(j, DEEP):
                        sp.wait_ge(s_twice, j + 1 - DEEP)
                        sp.sem_inc(s_sp_turn, 1)
                        sp.wait_ge(s_xn, j + 1 - DEEP)
                        sp.sem_inc(s_sp_turn, 1)
                    sp.dma_start(rows[:, b], keep.xs[bass.ds(first, P), :]).then_inc(s_in[b], 16)

                pipeline(sp, (0, load, start))

            @block.tensor
            def _(pe):
                pe.wait_ge(keep.s_big, WEIGHTS)

                def turn_x(j, b):
                    par = b % 2
                    pe.wait_ge(s_xn, j + 1)
                    if later(j, 2):
                        pe.wait_ge(s_xT, j - 1)
                    pe.transpose(p_t[par][:, 0:P], xn[:, par], keep.ident[:]).then_inc(s_t, 1)

                def up(j, b, e):
                    par = b % 2
                    pe.wait_ge(s_xT, j + 1)
                    if later(j, 2):
                        pe.wait_ge(s_hs, j - 1)
                    pe.matmul(p_h[par][:], xT[:, par], w1s[:, bass.ds(e, 1), :].rearrange("p a f -> p (a f)"),
                              start=True, stop=True).then_inc(s_h, 1)

                def turn_h(j, b):
                    par = b % 2
                    pe.wait_ge(s_hs, j + 1)
                    if later(j, 2):
                        pe.wait_ge(s_hT, j - 1)
                    for f in range(FB):
                        t = pe.transpose(p_r[par][:, P * f:P * f + P], h[:, par, P * f:P * f + P], keep.ident[:])
                    t.then_inc(s_r, 1)

                def down(j, b, e):
                    par = b % 2
                    pe.wait_ge(s_hT, j + 1)
                    if later(j, 2):
                        pe.wait_ge(s_res, j - 1)
                    for f in range(FB):
                        t = pe.matmul(p_y[par][:, 0:D], hT[:, par, P * f:P * f + P],
                                      w2s[:, bass.ds(e, 1), f, :].rearrange("p a d -> p (a d)"),
                                      start=(f == 0), stop=False)
                    t = pe.matmul(p_y[par][:, 0:D], keep.ones[0:1, :],
                                  keep.b2s[0:1, bass.ds(e, 1), :].rearrange("p a d -> p (a d)"), start=False, stop=True)
                    t.then_inc(s_yp, 1)

                pipeline(pe, (5, down, owner), (4, turn_h), (3, up, owner), (2, turn_x))

            @block.vector
            def _(dve):
                dve.wait_ge(keep.s_big, WEIGHTS)

                def x_stats(j, b):
                    dve.wait_ge(s_in[b], rounds(j, b) + 16)
                    if later(j, DEEP):
                        dve.wait_ge(s_mom, j + 1 - DEEP)
                    dve.bn_stats(stats[:, b], rows[:, b, 0:D]).then_inc(s_st, 1)

                def x_moments(j, b):
                    if later(j, DEEP):
                        dve.wait_ge(s_xn, j + 1 - DEEP)
                        dve.wait_ge(s_lnv, j + 1 - DEEP)
                    dve.wait_ge(s_st, j + 1)
                    dve.sem_inc(s_turn, 1)
                    dve.bn_aggr(moments[:, b], stats[:, b]).then_inc(s_mom, 1)

                def norm_x(j, b):
                    dve.wait_ge(s_rstd, j + 1)
                    dve.wait_ge(s_mom, j + 1)
                    if later(j, 2):
                        dve.wait_ge(s_t, j - 1)
                    dve.tensor_scalar(xn[:, b % 2], rows[:, b, 0:D], moments[:, b, 0:1], rstd[:, b:b + 1],
                                      ALU.subtract, ALU.mult).then_inc(s_xn, 1)

                def affine(j, b, e):
                    par = b % 2
                    dve.wait_ge(s_t, j + 1)
                    if later(j, 2):
                        dve.wait_ge(s_h, j - 1)
                    dve.tensor_scalar(xT[:, par], p_t[par][:, 0:P], gT[:, bass.ds(e, 1)], bT[:, bass.ds(e, 1)],
                                      ALU.mult, ALU.add).then_inc(s_xT, 1)

                def bias_h(j, b, e):
                    par = b % 2
                    dve.wait_ge(s_h, j + 1)
                    if later(j, 2):
                        dve.wait_ge(s_r, j - 1)
                    dve.tensor_tensor(h[:, par], p_h[par][:], b1s[:, bass.ds(e, 1), :].rearrange("p a f -> p (a f)"),
                                      ALU.add).then_inc(s_hs, 1)

                def weigh(j, b):
                    dve.wait_ge(s_exp, j + 1)
                    dve.tensor_scalar(away[:, b:b + 1], away[:, b:b + 1], 1.0, None, ALU.add).then_inc(s_one, 1)
                    if later(j, DEEP):
                        dve.wait_ge(s_res, j + 1 - DEEP)
                        dve.wait_ge(s_out[b], rounds(j, b))
                    dve.tensor_scalar(token[:, b:b + 1], twice[:, b, D + 1:D + 2], 0.5, None, ALU.mult).then_inc(s_token, 1)
                    dve.wait_ge(s_one, j + 1)
                    dve.reciprocal(alpha[:, b:b + 1], away[:, b:b + 1]).then_inc(s_alpha, 1)

                def residual(j, b):
                    dve.wait_ge(s_yp, j + 1)
                    dve.wait_ge(s_alpha, j + 1)
                    if later(j, DEEP):
                        dve.wait_ge(s_done, j + 1 - DEEP)
                    dve.scalar_tensor_tensor(out=res[:, b], in0=p_y[b % 2][:, 0:D], scalar=alpha[:, b:b + 1],
                                             in1=twice[:, b, 0:D], op0=ALU.mult, op1=ALU.add).then_inc(s_res, 1)

                def out_stats(j, b):
                    dve.wait_ge(s_res, j + 1)
                    if later(j, DEEP):
                        dve.wait_ge(s_omom, j + 1 - DEEP)
                    dve.bn_stats(ostats[:, b], res[:, b]).then_inc(s_ost, 1)

                def out_moments(j, b):
                    if later(j, DEEP):
                        dve.wait_ge(s_olnv, j + 1 - DEEP)
                    dve.wait_ge(s_ost, j + 1)
                    dve.sem_inc(s_turn, 1)
                    dve.bn_aggr(omoments[:, b], ostats[:, b]).then_inc(s_omom, 1)

                def norm_out(j, b):
                    dve.wait_ge(s_orstd, j + 1)
                    dve.wait_ge(s_omom, j + 1)
                    if later(j, DEEP):
                        dve.wait_ge(s_out[b], rounds(j, b))
                    dve.tensor_scalar(done[:, b], res[:, b], omoments[:, b, 0:1], orstd[:, b:b + 1],
                                      ALU.subtract, ALU.mult).then_inc(s_done, 1)

                pipeline(dve, (2, norm_x), (1, x_stats), (6, residual), (1, x_moments), (5, weigh), (6, out_stats),
                         (4, bias_h, owner), (6, out_moments), (7, norm_out), (3, affine, owner))

            @block.scalar
            def _(act):
                act.preload_act_table_set(LN_EXP)

                def x_rstd(j, b):
                    act.wait_ge(s_mom, j + 1)
                    if later(j, DEEP):
                        act.wait_ge(s_rstd, j + 1 - DEEP)
                    act.activation(lnvar[:, b:b + 1], moments[:, b, 1:2], ACT.Ln, bias=eps[:]).then_inc(s_lnv, 1)
                    act.wait_ge(s_lnv, j + 1)
                    if later(j, DEEP):
                        act.wait_ge(s_xn, j + 1 - DEEP)
                    act.activation(rstd[:, b:b + 1], lnvar[:, b:b + 1], ACT.Exp, scale=-0.5).then_inc(s_rstd, 1)

                def double(j, b):
                    act.wait_ge(s_in[b], rounds(j, b) + 16)
                    if later(j, DEEP):
                        act.wait_ge(s_res, j + 1 - DEEP)
                        act.wait_ge(s_token, j + 1 - DEEP)
                    act.activation(twice[:, b], rows[:, b], ACT.Copy, scale=2.0).then_inc(s_twice, 1)
                    act.wait_ge(s_twice, j + 1)
                    if later(j, DEEP):
                        act.wait_ge(s_alpha, j + 1 - DEEP)
                    act.activation(away[:, b:b + 1], twice[:, b, D:D + 1], ACT.Exp, scale=-0.5).then_inc(s_exp, 1)

                def rectify(j, b):
                    act.wait_ge(s_r, j + 1)
                    if later(j, 2):
                        act.wait_ge(s_yp, j - 1)
                    act.activation(hT[:, b % 2], p_r[b % 2][:], ACT.Relu).then_inc(s_hT, 1)

                def out_rstd(j, b):
                    act.wait_ge(s_omom, j + 1)
                    if later(j, DEEP):
                        act.wait_ge(s_orstd, j + 1 - DEEP)
                    act.activation(olnvar[:, b:b + 1], omoments[:, b, 1:2], ACT.Ln, bias=eps[:]).then_inc(s_olnv, 1)
                    act.wait_ge(s_olnv, j + 1)
                    if later(j, DEEP):
                        act.wait_ge(s_done, j + 1 - DEEP)
                    act.activation(orstd[:, b:b + 1], olnvar[:, b:b + 1], ACT.Exp, scale=-0.5).then_inc(s_orstd, 1)

                pipeline(act, (1, x_rstd), (6, out_rstd), (3, double), (4, rectify))

            @block.gpsimd
            def _(pool):
                def send(j, b):
                    pool.wait_ge(s_token, j + 1)
                    pool.sem_inc(s_pool_turn, 1)
                    pool.wait_ge(s_done, j + 1)
                    pool.sem_inc(s_pool_turn, 1)
                    pool.indirect_dma_start(
                        out=out_rows, out_offset=bass.IndirectOffsetOnAxis(ap=token[:, b:b + 1], axis=0),
                        in_=done[:, b], in_offset=None, bounds_check=T - 1, oob_is_err=False).then_inc(s_out[b], 16)

                pipeline(pool, (8, send))
                for b in range(DEEP):
                    pool.wait_ge(s_out[b], 16 * (TILES // DEEP))


def network(nc, a, out):
    T = a["L0_attn_x"].shape[0] * a["L0_attn_x"].shape[1]
    with ExitStack() as ctx:
        s = Space(nc, ctx, "keep")
        keep = Buffers()
        keep.ident = s.sb("ident", [P, P])
        keep.ones = s.sb("ones", [P, P])
        keep.before = s.sb("before", [P, P])
        keep.eps = s.sb("eps", [P, 1])
        keep.weight, keep.from_slot = s.sb("weight", [P, 2, T // P]), s.sb("from_slot", [P, 2, T // P], I32)
        ffn = Buffers()
        ffn.centroids, ffn.ln_g, ffn.ln_b, ffn.w1, ffn.b1, ffn.w2, ffn.b2 = (
            a["L1_ffn_" + n] for n in ("centroids", "ln_g", "ln_b", "w1", "b1", "w2", "b2"))
        E, _, F = ffn.w1.shape
        keep.WIDE = P + 2
        rows = lambda name, n, width: nc.dram_tensor(name, (n, width), F32, kind="Internal").ap()
        keep.x1 = rows("x1_rows", T, P)
        keep.xe, keep.ye = rows("expert_in_rows", 5 * T // 2, P), rows("expert_out_rows", 5 * T // 2, P)
        keep.xs = rows("rows_by_centroid", E * T + P, keep.WIDE)
        constants(nc, keep)
        mamba(nc, keep, *(a["L0_attn_" + n] for n in (
            "x", "norm_w", "norm_b", "in_w", "in_b", "conv_w", "conv_b", "bc_w", "bc_b", "dtr_w", "dtr_b", "dt_w",
            "dt_b", "out_w", "out_b")))
        moe(nc, keep, *(a["L0_ffn_" + n] for n in ("w_g", "c_fc", "c_proj")))

        s = Space(nc, ctx, "layer1")
        keep.base = s.sb("base", [P, 1, E])
        keep.cT, keep.gT, keep.bT = (s.sb(n, [P, E]) for n in ("cT", "gT", "bT"))
        keep.w1s, keep.w2s = s.sb("w1s", [P, E, F]), s.sb("w2s", [P, E, F // P, P])
        keep.b1s, keep.b2s = s.sb("b1s", [P, E, F]), s.sb("b2s", [1, E, P])
        keep.s_big = s.sem("ffn_weights_loaded")
        gla(nc, keep, *(a["L1_attn_" + n] for n in (
            "Wq", "Wk", "Wv", "Wg", "gk_w1", "gk_w2", "gk_b2", "g_norm_w", "Wo")), ffn)
        routed_ffn(nc, keep, ffn, out)


def kernel(**inputs):
    import numpy as np
    import concourse.bacc as bacc
    from concourse.bass_utils import run_bass_kernel_spmd

    nc = bacc.Bacc("TRN2", target_bir_lowering=False, num_devices=1)
    arrays, views = {}, {}
    for name, value in inputs.items():
        arrays[f"in_{name}"] = np.ascontiguousarray(value)
        views[name] = nc.dram_tensor(f"in_{name}", value.shape, mybir.dt.from_np(arrays[f"in_{name}"].dtype),
                                     kind="ExternalInput").ap()
    out = nc.dram_tensor("out", inputs["L0_attn_x"].shape, F32, kind="ExternalOutput").ap()
    network(nc, views, out)
    return run_bass_kernel_spmd(nc, [arrays], core_ids=[0]).results[0]["out"]
```

```python
from contextlib import ExitStack

import concourse.bass as bass
from concourse import mybir

ALU = mybir.AluOpType
ACT = mybir.ActivationFunctionType
AX = mybir.AxisListType
F32 = mybir.dt.float32
BF16 = mybir.dt.bfloat16
I32 = mybir.dt.int32
U32 = mybir.dt.uint32

P = 128
EPS = 1e-5
FAR = 1.0e6
LN_EXP = "natural_log_exp_and_others"


class Buffers:
    pass


class Space:

    def __init__(self, nc, ctx, stage):
        self.nc, self.ctx, self.stage, self.sems = nc, ctx, stage, []
        ctx.callback(self.end)

    def sb(self, name, shape, dtype=F32):
        return self.ctx.enter_context(self.nc.sbuf_tensor(f"{self.stage}_{name}", shape, dtype))

    def ps(self, name, shape, dtype=F32):
        return self.ctx.enter_context(self.nc.psum_tensor(f"{self.stage}_{name}", shape, dtype))

    def sem(self, name):
        self.sems.append(self.nc.alloc_semaphore(f"{self.stage}_{name}"))
        return self.sems[-1]

    def end(self):
        self.nc.clear_and_free_semaphores(self.sems)
        self.nc.all_engine_barrier()

    def block(self):
        return self.ctx.enter_context(self.nc.Block())


def constants(nc, keep):
    with ExitStack() as ctx:
        s = Space(nc, ctx, "const")
        filled, done = s.sem("filled"), s.sem("done")
        block = s.block()

        @block.vector
        def _(dve):
            dve.memset(keep.ident[:], 0.0).then_inc(filled, 1)
            dve.memset(keep.ones[:], 1.0).then_inc(filled, 1)
            dve.memset(keep.before[:], 1.0).then_inc(filled, 1)
            dve.memset(keep.eps[:], EPS).then_inc(filled, 1)

        @block.gpsimd
        def _(pool):
            pool.wait_ge(filled, 4)
            pool.affine_select(out=keep.ident[:], in_=keep.ident[:], compare_op=ALU.not_equal, fill=1.0, base=0,
                               pattern=[[-1, P]], channel_multiplier=1).then_inc(done, 1)
            pool.affine_select(out=keep.before[:], in_=keep.before[:], compare_op=ALU.is_gt, fill=0.0, base=0,
                               pattern=[[1, P]], channel_multiplier=-1).then_inc(done, 1)
            pool.wait_ge(done, 2)


def run_chunks(chunks, slots, loop, steps, scan, start=None):
    most = max([ahead for _, ahead, _ in steps] + [0])
    least = -min([ahead for _, ahead, _ in steps] + [0])
    in_order = sorted(steps, key=lambda step: step[0])

    def alone(q):
        for slot, ahead, work in in_order:
            if 0 <= q + ahead < chunks:
                work(q + ahead, (q + ahead) % 2)

    def chunk(q, par):
        for n in range(slots):
            for at in (n, n + 0.5):
                for slot, ahead, work in steps:
                    if slot == at and (not isinstance(q, int) or 0 <= q + ahead < chunks):
                        work(q + ahead, (par + ahead) % 2)
                if at == n:
                    scan(q, par, n)

    for q in range(-most, 0):
        alone(q)
    if start:
        start()
    head = max(least, 1)
    pairs = (chunks - head - most) // 2
    for q in range(head):
        chunk(q, q % 2)
    with loop(0, pairs) as i:
        chunk(2 * i + head, head % 2)
        chunk(2 * i + head + 1, 1 - head % 2)
    for q in range(head + 2 * pairs, chunks):
        chunk(q, q % 2)
    for q in range(chunks, chunks + least):
        alone(q)


def at_chunk(tiles, q):
    return tiles[q] if isinstance(q, int) else tiles[bass.ds(q, 1)].rearrange("a p s d -> (a p) s d")


def later(q, n):
    return not isinstance(q, int) or q >= n


def mamba(nc, keep, x, norm_w, norm_b, in_w, in_b, conv_w, conv_b, bc_w, bc_b, dtr_w, dtr_b, dt_w, dt_b, out_w, out_b, w_g):
    B, L, D = x.shape
    INNER = out_w.shape[0]
    J = INNER // P
    N = bc_w.shape[1] // 2
    CONV = conv_w.shape[1]
    R = dtr_w.shape[1]
    C = 512
    DEEP = 4
    S = C // P
    Q = B * L // C
    HALVES = L // C
    assert (J, N, HALVES, D) == (2, 16, 2, P)
    x_tiles = x.rearrange("b (c s p) d -> (b c) p s d", s=S, p=P)
    x1_tiles = keep.x1.rearrange("(q s p) d -> q p s d", s=S, p=P)
    STEPS, RANKED = 21, 13
    CONSTS = 3 + CONV
    K, E, CAP = keep.K, w_g.shape[1], keep.CAP
    CT = CAP // P
    SENT = 16 * K * S

    with ExitStack() as ctx:
        m = Space(nc, ctx, "ssm")
        w_in = m.sb("w_in", [P, 2 * INNER])
        w_bcd = m.sb("w_bcd", [P, J, 2 * N + R])
        w_dt = m.sb("w_dt", [2 * N + R, INNER])
        w_out = m.sb("w_out", [P, J, D])
        out_bias = m.sb("out_bias", [P, D])
        nw, nb = m.sb("nw", [P, 1]), m.sb("nb", [P, 1])
        b_in = m.sb("b_in", [P, 2 * J])
        b_conv, b_dt = m.sb("b_conv", [P, J]), m.sb("b_dt", [P, J])
        minus_b_dt = m.sb("minus_b_dt", [P, J])
        b_bc = m.sb("b_bc", [2 * N, 1])
        b_dtr = m.sb("b_dtr", [2 * N + R, 1])
        taps = m.sb("taps", [P, J, CONV])
        tap_diag = m.sb("tap_diag", [P, CONV, P])
        eps = m.sb("eps", [P, 1])
        mean_w = m.sb("mean_w", [P, 2 * N])
        is_c = m.sb("is_c", [2 * N, 1])
        pick1 = m.sb("pick1", [P, 2 * N, 1])
        pick = m.sb("pick", [P, 2 * N, P], BF16)

        wg = m.sb("wg", [P, E])
        zero = m.sb("zero", [P, 1, D])
        first_of = m.sb("first_of", [P, 1, E])
        x1T = m.sb("x1T", [P, C])
        logits, rest = m.sb("logits", [P, S, E]), m.sb("rest", [P, S, E])
        hit, cand = m.sb("hit", [P, S, E]), m.sb("cand", [P, S, E])
        chosen = m.sb("chosen", [P, S + 1, K, E])
        rank, picked = m.sb("rank", [P, S, K, E]), m.sb("picked", [P, S, K, E])
        rk, at, over = (m.sb(n, [P, S, K]) for n in ("rk", "at", "over"))
        ix = m.sb("ix", [P, 2, S, K], I32)
        xin = m.sb("xin", [P, 2, S, D])
        stats, moments = m.sb("stats", [P, S, 6]), m.sb("moments", [P, S, 2])
        lnvar, rstd, minus, shift = (m.sb(n, [P, S]) for n in ("lnvar", "rstd", "minus", "shift"))
        xn = m.sb("xn", [P, S, D])
        nT = m.sb("nT", [P, C])
        xb = m.sb("xb", [P, J, CONV - 1 + C])
        conv = m.sb("conv", [P, J, 2, C])
        zs = m.sb("zs", [P, 2, J, C])
        xa = m.sb("xa", [P, 2, J, C])
        dt = m.sb("dt", [P, 2, J, C])
        dtn = m.sb("dtn", [P, J, C])
        dte = m.sb("dte", [P, J, C])
        dtl = m.sb("dtl", [P, J, C])
        dtr = m.sb("dtr", [2 * N + R, C])
        bcs = m.sb("bcs", [2 * N, C])
        bc = m.sb("bc", [2 * N, C])
        mid = m.sb("mid", [2 * N, C], BF16)
        rest1, rest2 = m.sb("rest1", [2 * N, C]), m.sb("rest2", [2 * N, C])
        parts = m.sb("parts", [P, 2, C], BF16)
        b_all = m.sb("b_all", [P, DEEP, C])
        decay = m.sb("decay", [P, DEEP, J, C])
        drive = m.sb("drive", [P, DEEP, J, C])
        h = m.sb("h", [P, 2, J, C])
        hc = m.sb("hc", [P, DEEP, J, C])
        h_end = m.sb("h_end", [P, N, J, 1])
        gated = m.sb("gated", [P, J, C])
        xob = m.sb("xob", [P, 2, S, D])
        x1 = m.sb("x1", [P, 2, S, D])
        s_x1out = [m.sem(f"x1_stored{i}") for i in range(2)]
        res = m.sb("res", [P, S, D])
        ostats, omoments = m.sb("ostats", [P, S, 6]), m.sb("omoments", [P, S, 2])
        olnvar, orstd, ominus, oshift = (m.sb(n, [P, S]) for n in ("olnvar", "orstd", "ominus", "oshift"))

        p_y = m.ps("p_y", [P, J, C])
        p_b = m.ps("p_b", [P, C])
        p_c = m.ps("p_c", [P, 2, C])
        p_mm = [m.ps(f"p_mm{i}", [P, C]) for i in range(3)]

        p_logits = p_mm[2][:, 0:S * E].rearrange("p (s e) -> p s e", e=E)
        p_rank = p_mm[0][:, 0:(S + 1) * K * E].rearrange("p (s k e) -> p s k e", k=K, e=E)

        s_w = m.sem("weights_loaded")
        s_zero, s_cst, s_pick = m.sem("zeroed"), m.sem("constants_made"), m.sem("pick_made")
        s_turn, s_sp_turn = m.sem("vector_steps"), m.sem("sync_steps")
        s_edge = m.sem("xb_edge_made")
        s_iota, s_clear, s_minus, s_shift, s_ominus, s_oshift = (m.sem(n) for n in (
            "iota_made", "rows_cleared", "minus_mean", "shift_made", "minus_out_mean", "out_shift_made"))
        s_x1t, s_x1T, s_lp, s_logits, s_route, s_ranks = (m.sem(n) for n in (
            "x1_transposed", "x1T_made", "logit_product", "logits_made", "routing_steps", "rank_products"))
        s_sent = [m.sem(f"rows_sent{i}") for i in range(2)]
        s_pool_turn = m.sem("pool_steps")
        s_x = [m.sem(f"x_loaded{i}") for i in range(2)]
        s_xr = [m.sem(f"x_reloaded{i}") for i in range(2)]
        s_st, s_mom = m.sem("stats_made"), m.sem("moments_made")
        s_lnv, s_rstd = m.sem("lnvar_made"), m.sem("rstd_made")
        s_xn, s_xT, s_nT = m.sem("x_normed"), m.sem("x_transposed"), m.sem("nT_made")
        s_in, s_xb, s_z = m.sem("in_product"), m.sem("xb_made"), m.sem("z_made")
        s_conv, s_xa = m.sem("conv_steps"), m.sem("xa_made")
        s_conv_product, s_conv_taken = m.sem("conv_product"), m.sem("conv_taken")
        s_bcd, s_bcs, s_dtr = m.sem("bcd_product"), m.sem("bcs_made"), m.sem("dtr_made")
        s_dtp, s_dtn, s_dte, s_dtl, s_dt = (m.sem("dt_product"), m.sem("dt_negated"), m.sem("dt_exp"),
                                            m.sem("dt_log"), m.sem("dt_made"))
        s_mean, s_bc, s_split, s_parts = m.sem("dt_mean"), m.sem("bc_made"), m.sem("split_steps"), m.sem("parts_made")
        s_pb, s_pc, s_ball = m.sem("b_spread"), m.sem("c_spread"), m.sem("b_copied")
        s_decay, s_drive, s_h, s_hc, s_y = (m.sem("decay_made"), m.sem("drive_made"), m.sem("h_made"),
                                            m.sem("hc_made"), m.sem("y_summed"))
        s_hend = m.sem("h_end_kept")
        s_g, s_o, s_xob, s_res = m.sem("gated_made"), m.sem("out_product"), m.sem("x_plus_bias"), m.sem("residual_made")
        s_ost, s_omom, s_olnv, s_orstd, s_x1 = (m.sem("out_stats"), m.sem("out_moments"), m.sem("out_lnvar"),
                                                m.sem("out_rstd"), m.sem("x1_made"))
        WEIGHTS = 15 * 16
        block = m.block()

        @block.sync
        def _(sp):
            col = lambda v, a: v.rearrange("(a p) -> p a", p=P)
            sp.dma_start(xin[:, 0], x_tiles[0]).then_inc(s_x[0], 16)
            sp.dma_start(w_in[:], in_w).then_inc(s_w, 16)
            sp.dma_start(w_bcd[:, :, 0:2 * N], bc_w.rearrange("(j p) n -> p j n", p=P)).then_inc(s_w, 16)
            sp.dma_start(w_bcd[:, :, 2 * N:], dtr_w.rearrange("(j p) n -> p j n", p=P)).then_inc(s_w, 16)
            sp.dma_start(w_dt[2 * N:, :], dt_w).then_inc(s_w, 16)
            sp.dma_start(w_out[:], out_w.rearrange("(j p) n -> p j n", p=P)).then_inc(s_w, 16)
            sp.dma_start(nw[:], col(norm_w, 1)).then_inc(s_w, 16)
            sp.dma_start(nb[:], col(norm_b, 1)).then_inc(s_w, 16)
            sp.dma_start(b_in[:], col(in_b, 2 * J), allow_slow_non_contiguous=True).then_inc(s_w, 16)
            sp.dma_start(b_conv[:], col(conv_b, J), allow_slow_non_contiguous=True).then_inc(s_w, 16)
            sp.dma_start(b_dt[:], col(dt_b, J), allow_slow_non_contiguous=True).then_inc(s_w, 16)
            sp.dma_start(b_bc[:], bc_b.rearrange("(n a) -> n a", a=1)).then_inc(s_w, 16)
            sp.dma_start(b_dtr[2 * N:, :], dtr_b.rearrange("(n a) -> n a", a=1)).then_inc(s_w, 16)
            sp.dma_start(taps[:], conv_w.rearrange("(j p) k -> p j k", p=P)).then_inc(s_w, 16)
            sp.dma_start(out_bias[:], out_b.rearrange("(a d) -> a d", a=1).broadcast_to((P, D))).then_inc(s_w, 16)
            sp.dma_start(wg[:], w_g).then_inc(s_w, 16)
            sp.dma_start(xin[:, 1], x_tiles[1]).then_inc(s_x[1], 16)
            for q in range(2):
                sp.dma_start(xob[:, q], x_tiles[q]).then_inc(s_xr[q], 16)
            sp.wait_ge(s_zero, 8)
            for e in range(E):
                sp.dma_start(keep.xe[(2 * e + 1) * CAP:(2 * e + 2) * CAP, :].rearrange("(c p) d -> p c d", p=P),
                             zero[:].broadcast_to((P, CT, D))).then_inc(s_clear, 16)
            for q in range(2, 4):
                sp.wait_ge(s_xn, S * (q - 1))
                sp.dma_start(xin[:, q % 2], x_tiles[q]).then_inc(s_x[q % 2], 16)

            def during(q, par):
                known = isinstance(q, int)
                if not known or q + 3 < Q:
                    sp.wait_ge(s_xn, S * (q + 2))
                    sp.sem_inc(s_sp_turn, 1)
                    sp.dma_start(xin[:, 1 - par], at_chunk(x_tiles, q + 3)).then_inc(s_x[1 - par], 16)
                if not known or q + 1 < Q:
                    sp.wait_ge(s_res, q)
                    sp.sem_inc(s_sp_turn, 1)
                    sp.dma_start(xob[:, 1 - par], at_chunk(x_tiles, q + 1)).then_inc(s_xr[1 - par], 16)
                sp.wait_ge(s_x1, S * q)
                sp.sem_inc(s_sp_turn, 1)
                sp.dma_start(at_chunk(x1_tiles, q - 1), x1[:, 1 - par]).then_inc(s_x1out[1 - par], 16)

            with sp.Fori(0, (Q - 4) // 2) as i:
                during(2 * i + 1, 1)
                during(2 * i + 2, 0)
            for q in range(Q - 3, Q + 1):
                during(q, q % 2)
            for par in range(2):
                sp.wait_ge(s_x1out[par], 16 * (Q // 2))

        @block.vector
        def _(dve):
            dve.memset(eps[:], EPS).then_inc(s_zero, 1)
            dve.memset(pick1[:], 0.0).then_inc(s_zero, 1)
            dve.memset(is_c[:], 1.0).then_inc(s_zero, 1)
            dve.memset(mean_w[:], 0.0).then_inc(s_zero, 1)
            dve.memset(parts[:], 0.0).then_inc(s_zero, 1)
            dve.memset(zero[:], 0.0).then_inc(s_zero, 1)
            dve.memset(chosen[:], 0.0).then_inc(s_zero, 1)
            dve.memset(keep.count[:], 0.0).then_inc(s_zero, 1)
            dve.wait_ge(s_zero, 8)
            dve.memset(is_c[0:N, :], 0.0).then_inc(s_cst, 1)
            dve.memset(mean_w[:, 0:N], 1.0 / INNER).then_inc(s_cst, 1)
            dve.wait_ge(s_w, WEIGHTS)
            dve.tensor_scalar(minus_b_dt[:], b_dt[:], -1.0, None, ALU.mult).then_inc(s_cst, 1)
            for k in range(CONV):
                dve.tensor_scalar(tap_diag[:, k], keep.ident[:], taps[:, 0, k:k + 1], None, ALU.mult).then_inc(s_cst, 1)
            dve.wait_ge(s_iota, 1)
            dve.wait_ge(s_pick, 3)
            dve.tensor_copy(pick[:], pick1[:].broadcast_to((P, 2 * N, P))).then_inc(s_pick, 1)

            def x_moments(q, par):
                dve.wait_ge(s_x[par], 8 * (q - par) + 16)
                for s in range(S):
                    dve.bn_stats(stats[:, s], xin[:, par, s]).then_inc(s_st, 1)
                dve.wait_ge(s_st, S * (q + 1))
                dve.sem_inc(s_turn, 1)
                for s in range(S):
                    dve.bn_aggr(moments[:, s], stats[:, s]).then_inc(s_mom, 1)

            def convolve(q, par):
                dve.wait_ge(s_xb, J * (q + 1))
                dve.wait_ge(s_xa, J * q)
                for j in range(1, J):
                    dve.tensor_scalar(conv[:, j, 0], xb[:, j, 0:C], taps[:, j, 0:1], None, ALU.mult).then_inc(s_conv, 1)
                    for k in range(1, CONV):
                        dve.wait_ge(s_conv, CONV * ((J - 1) * q + j - 1) + k)
                        dve.scalar_tensor_tensor(out=conv[:, j, k % 2], in0=xb[:, j, k:k + C],
                                                 scalar=taps[:, j, k:k + 1], in1=conv[:, j, 1 - k % 2],
                                                 op0=ALU.mult, op1=ALU.add).then_inc(s_conv, 1)

            def clip_dt(q, par):
                dve.wait_ge(s_dtl, q + 1)
                dve.tensor_scalar(dt[:, par], dtl[:], 0.001, 0.1, ALU.max, ALU.min).then_inc(s_dt, 1)

            def split_bc(q, par):
                dve.wait_ge(s_mean, q + 1)
                dve.wait_ge(s_bcs, q + 1)
                dve.wait_ge(s_split, 4 * q)
                dve.scalar_tensor_tensor(out=bc[:], in0=p_mm[1][0:2 * N, :], scalar=is_c[:], in1=bcs[:],
                                         op0=ALU.add, op1=ALU.mult).then_inc(s_bc, 1)
                dve.wait_ge(s_bc, q + 1)
                if later(q, 2):
                    dve.wait_ge(s_pc, N * (q - 1))
                dve.tensor_copy(parts[0:2 * N, par], bc[:]).then_inc(s_split, 1)
                dve.wait_ge(s_split, 4 * q + 1)
                dve.tensor_tensor(rest1[:], bc[:], parts[0:2 * N, par], ALU.subtract).then_inc(s_split, 1)
                dve.wait_ge(s_split, 4 * q + 2)
                dve.wait_ge(s_parts, 2 * q)
                dve.tensor_copy(mid[:], rest1[:]).then_inc(s_split, 1)
                dve.wait_ge(s_split, 4 * q + 3)
                dve.tensor_tensor(rest2[:], rest1[:], mid[:], ALU.subtract).then_inc(s_split, 1)

            def scan(q, par, n):
                first = par == 0
                k, deep = n % 2, n % DEEP
                done = N * q + n
                dve.wait_ge(s_decay, done + 1)
                dve.wait_ge(s_drive, done + 1)
                if not first:
                    dve.wait_ge(s_hend, (q + 1) * (N // 2))
                if later(q, 1) or n >= 2:
                    dve.wait_ge(s_hc, done - 1)
                for j in range(J):
                    dve.tensor_tensor_scan(h[:, k, j], decay[:, deep, j], drive[:, deep, j],
                                           0.0 if first else h_end[:, n, j], ALU.mult, ALU.add).then_inc(s_h, 1)
                dve.wait_ge(s_h, 2 * done + 2)
                dve.wait_ge(s_pc, done + 1)
                if later(q, 1) or n >= DEEP:
                    dve.wait_ge(s_y, done + 1 - DEEP)
                if first:
                    dve.tensor_copy(h_end[:, n], h[:, k, :, C - 1:C]).then_inc(s_hend, 1)
                dve.tensor_tensor(hc[:, deep], h[:, k], p_c[:, k:k + 1].broadcast_to((P, J, C)),
                                  ALU.mult).then_inc(s_hc, 1)

            def gate(q, par):
                dve.wait_ge(s_y, N * (q + 1))
                dve.wait_ge(s_z, J * (q + 1))
                dve.wait_ge(s_o, q)
                dve.tensor_tensor(gated[:], p_y[:], zs[:, par], ALU.mult).then_inc(s_g, 1)

            def residual(q, par):
                dve.wait_ge(s_o, q + 1)
                dve.wait_ge(s_xob, q + 1)
                dve.wait_ge(s_x1, S * q)
                dve.tensor_tensor(res[:], p_mm[0][:].rearrange("p (s d) -> p s d", s=S), xob[:, par],
                                  ALU.add).then_inc(s_res, 1)
                dve.wait_ge(s_res, q + 1)
                for s in range(S):
                    dve.bn_stats(ostats[:, s], res[:, s]).then_inc(s_ost, 1)
                dve.wait_ge(s_ost, S * (q + 1))
                dve.sem_inc(s_turn, 1)
                for s in range(S):
                    dve.bn_aggr(omoments[:, s], ostats[:, s]).then_inc(s_omom, 1)

            def step(q, n, ins):
                ins.then_inc(s_route, 1)
                dve.wait_ge(s_route, STEPS * q + n)

            def of_chunk(q):
                return slice(S * q, S * q + S) if isinstance(q, int) else bass.ds(S * q, S)

            def choose(q, par, c):
                wide = (P, S, E)
                if c == 0:
                    dve.wait_ge(s_logits, q + 1)
                    if later(q, 1):
                        dve.wait_ge(s_ranks, q)
                src = rest if c else logits
                best, pref = (v[:, of_chunk(q), c:c + 1] for v in (keep.best, keep.pref))
                n = 6 * c
                step(q, n + 1, dve.tensor_reduce(best, src[:], AX.X, ALU.max))
                step(q, n + 2, dve.tensor_tensor(hit[:], src[:], best.broadcast_to(wide), ALU.is_equal))
                step(q, n + 3, dve.tensor_tensor(cand[:], hit[:], first_of[:].broadcast_to(wide), ALU.mult))
                step(q, n + 4, dve.tensor_reduce(pref, cand[:], AX.X, ALU.max))
                step(q, n + 5, dve.tensor_tensor(chosen[:, 0:S, c], cand[:], pref.broadcast_to(wide), ALU.is_equal))
                if c == 0:
                    step(q, 6, dve.scalar_tensor_tensor(out=rest[:], in0=chosen[:, 0:S, 0], scalar=-3.0e38,
                                                        in1=logits[:], op0=ALU.mult, op1=ALU.add))

            def locate(q, par):
                dve.wait_ge(s_ranks, q + 1)
                step(q, 12, dve.tensor_tensor(rank[:], p_rank[:, 0:S], keep.count[:].broadcast_to((P, S, K, E)), ALU.add))
                step(q, 13, dve.tensor_tensor(keep.count[:], p_rank[:, S:S + 1], keep.count[:], ALU.add))
                step(q, 14, dve.tensor_tensor(picked[:], rank[:], chosen[:, 0:S], ALU.mult))
                step(q, 15, dve.tensor_reduce(rk[:], picked[:], AX.X, ALU.add))

            def locate_rows(q, par):
                step(q, 16, dve.tensor_scalar(at[:], keep.pref[:, of_chunk(q)], -2.0 * CAP, float(2 * CAP * E + CAP),
                                              ALU.mult, ALU.add))
                row = keep.row[:, of_chunk(q)]
                step(q, 17, dve.scalar_tensor_tensor(out=row[:, :, 0:1], in0=at[:, :, 0:1], scalar=-1.0,
                                                     in1=rk[:, :, 0:1], op0=ALU.add, op1=ALU.subtract))
                step(q, 18, dve.tensor_tensor(row[:, :, 1:2], at[:, :, 1:2], rk[:, :, 1:2], ALU.add))
                step(q, 19, dve.tensor_scalar(over[:], rk[:], float(CAP), FAR, ALU.is_ge, ALU.mult))
                step(q, 20, dve.tensor_tensor(over[:], over[:], row, ALU.add))
                if later(q, 2):
                    dve.wait_ge(s_sent[par], SENT // 2 * (q - par))
                step(q, 21, dve.tensor_copy(ix[:, par], over[:]))

            run_chunks(Q, N, dve.Fori, [
                (1, -1, gate), (3, -1, residual), (14, -1, lambda q, par: choose(q, par, 0)),
                (15, -1, lambda q, par: choose(q, par, 1)), (5, -2, locate), (6, -2, locate_rows),
                (2, 1, convolve), (4, 2, x_moments), (10, 1, clip_dt), (12, 1, split_bc)], scan)

        @block.gpsimd
        def _(pool):
            pool.iota(first_of[:, 0], pattern=[[-1, E]], base=E, channel_multiplier=0,
                      allow_small_or_imprecise_dtypes=True).then_inc(s_iota, 1)
            pool.wait_ge(s_zero, 8)
            for part in range(3):
                pool.affine_select(out=pick1[:, :, 0], in_=pick1[:, :, 0], compare_op=ALU.not_equal, fill=1.0,
                                   base=-2 * N * part, pattern=[[-1, 2 * N]],
                                   channel_multiplier=1).then_inc(s_pick, 1)
                pool.wait_ge(s_pick, part + 1)

            def x_shift(q, par):
                pool.wait_ge(s_rstd, q + 1)
                pool.wait_ge(s_minus, q + 1)
                pool.wait_ge(s_xn, S * q)
                pool.tensor_tensor(shift[:], minus[:], rstd[:], ALU.mult).then_inc(s_shift, 1)

            def out_shift(q, par):
                pool.wait_ge(s_orstd, q + 1)
                pool.wait_ge(s_ominus, q + 1)
                pool.wait_ge(s_x1, S * q)
                pool.tensor_tensor(oshift[:], ominus[:], orstd[:], ALU.mult).then_inc(s_oshift, 1)

            def send(q, par, c):
                pool.wait_ge(s_route, STEPS * (q + 1))
                pool.sem_inc(s_pool_turn, 1)
                pool.wait_ge(s_x1, S * (q + 1))
                pool.sem_inc(s_pool_turn, 1)
                if isinstance(q, int) and q == 0 and c == 0:
                    pool.wait_ge(s_clear, 16 * E)
                for s in range(S):
                    pool.indirect_dma_start(
                        out=keep.xe, out_offset=bass.IndirectOffsetOnAxis(ap=ix[:, par, s, c:c + 1], axis=0),
                        in_=x1[:, par, s], in_offset=None, bounds_check=2 * E * CAP - 1,
                        oob_is_err=False).then_inc(s_sent[par], 16)

            def add_out_bias(q, par):
                pool.wait_ge(s_xr[par], 8 * (q - par) + 16)
                pool.tensor_tensor(xob[:, par], xob[:, par], out_bias[:, None, :].broadcast_to((P, S, D)),
                                   ALU.add).then_inc(s_xob, 1)

            def scan(q, par, n):
                done = N * q + n
                pool.wait_ge(s_xa, J * (q + 1))
                pool.wait_ge(s_ball, done + 1)
                if later(q, 1) or n >= DEEP:
                    pool.wait_ge(s_h, J * (done + 1 - DEEP))
                pool.tensor_tensor(drive[:, n % DEEP], xa[:, par], b_all[:, n % DEEP, None, :].broadcast_to((P, J, C)),
                                   ALU.mult).then_inc(s_drive, 1)

            pool.wait_ge(s_w, WEIGHTS)
            run_chunks(Q, N, pool.Fori, [
                (9, -2, lambda q, par: send(q, par, 0)), (8, -1, out_shift), (9, 2, x_shift), (10, 0, add_out_bias),
                (15, -2, lambda q, par: send(q, par, 1))], scan)
            for par in range(2):
                pool.wait_ge(s_sent[par], SENT * (Q // 2))

        @block.scalar
        def _(act):
            act.preload_act_table_set(LN_EXP)
            act.wait_ge(s_w, WEIGHTS)
            act.wait_ge(s_zero, 8)
            act.wait_ge(s_cst, CONSTS)

            def x_rstd(q, par):
                act.wait_ge(s_mom, S * (q + 1))
                act.activation(lnvar[:], moments[:, :, 1], ACT.Ln, bias=eps[:]).then_inc(s_lnv, 1)
                act.wait_ge(s_lnv, q + 1)
                act.wait_ge(s_xn, S * q)
                act.wait_ge(s_shift, q)
                act.activation(rstd[:], lnvar[:], ACT.Exp, scale=-0.5).then_inc(s_rstd, 1)
                act.activation(minus[:], moments[:, :, 0], ACT.Copy, scale=-1.0).then_inc(s_minus, 1)

            def norm_x(q, par):
                act.wait_ge(s_shift, q + 1)
                act.wait_ge(s_rstd, q + 1)
                act.wait_ge(s_xT, q)
                for s in range(S):
                    act.activation(xn[:, s], xin[:, par, s], ACT.Identity, scale=rstd[:, s:s + 1],
                                   bias=shift[:, s:s + 1]).then_inc(s_xn, 1)

            def scale_x(q, par):
                act.wait_ge(s_xT, q + 1)
                act.wait_ge(s_in, 2 * J * q)
                act.activation(nT[:], p_mm[0][:], ACT.Identity, scale=nw[:], bias=nb[:]).then_inc(s_nT, 1)

            def take_xb(q, par):
                for j in range(J):
                    act.wait_ge(s_in, 2 * J * q + j + 1)
                    act.wait_ge(s_conv_product, q)
                    act.wait_ge(s_conv, (J - 1) * CONV * q)
                    if par == 0:
                        act.activation(xb[:, j, 0:CONV - 1], keep.ident[:, 0:CONV - 1], ACT.Copy,
                                       scale=0.0).then_inc(s_edge, 1)
                    else:
                        act.activation(xb[:, j, 0:CONV - 1], xb[:, j, C:C + CONV - 1], ACT.Copy).then_inc(s_edge, 1)
                    act.wait_ge(s_edge, J * q + j + 1)
                    act.activation(xb[:, j, CONV - 1:], p_mm[j + 1][:], ACT.Identity,
                                   bias=b_in[:, j:j + 1]).then_inc(s_xb, 1)

            def take_conv(q, par):
                act.wait_ge(s_conv_product, q + 1)
                act.wait_ge(s_xa, J * q)
                act.activation(conv[:, 0, 1], p_mm[0][:], ACT.Copy).then_inc(s_conv_taken, 1)

            def take_z(q, par):
                for j in range(J):
                    act.wait_ge(s_in, 2 * J * q + J + j + 1)
                    if later(q, 2):
                        act.wait_ge(s_g, q - 1)
                    act.activation(zs[:, par, j], p_mm[j + 1][:], ACT.Silu,
                                   bias=b_in[:, J + j:J + j + 1]).then_inc(s_z, 1)

            def take_xa(q, par):
                for j in range(J):
                    if j:
                        act.wait_ge(s_conv, CONV * ((J - 1) * q + j))
                    else:
                        act.wait_ge(s_conv_taken, q + 1)
                    if later(q, 2):
                        act.wait_ge(s_drive, N * (q - 1))
                        act.wait_ge(s_bcd, q - 1)
                    act.activation(xa[:, par, j], conv[:, j, 1], ACT.Silu, bias=b_conv[:, j:j + 1]).then_inc(s_xa, 1)
                act.preload_act_table_set(LN_EXP)

            def take_bcd(q, par):
                act.wait_ge(s_bcd, q + 1)
                act.wait_ge(s_dtp, J * q)
                act.activation(dtr[2 * N:, :], p_mm[0][2 * N:2 * N + R, :], ACT.Identity,
                               bias=b_dtr[2 * N:, :]).then_inc(s_dtr, 1)
                act.wait_ge(s_bc, q)
                act.activation(bcs[:], p_mm[0][0:2 * N, :], ACT.Identity, bias=b_bc[:]).then_inc(s_bcs, 1)

            def dt_exp(q, par):
                act.wait_ge(s_dte, q)
                for j in range(J):
                    act.wait_ge(s_dtp, J * q + j + 1)
                    act.activation(dtn[:, j], p_mm[j + 1][:], ACT.Relu, scale=-1.0,
                                   bias=minus_b_dt[:, j:j + 1]).then_inc(s_dtn, 1)
                act.wait_ge(s_dtn, J * (q + 1))
                act.wait_ge(s_dtl, q)
                act.activation(dte[:], dtn[:], ACT.Exp, scale=-1.0).then_inc(s_dte, 1)

            def dt_log(q, par):
                act.wait_ge(s_dte, q + 1)
                act.wait_ge(s_dt, q)
                act.activation(dtl[:], dte[:], ACT.Ln, bias=1.0).then_inc(s_dtl, 1)

            def place_parts(q, par):
                act.wait_ge(s_split, 4 * q + 3)
                act.activation(parts[2 * N:4 * N, par], mid[:], ACT.Copy).then_inc(s_parts, 1)
                act.wait_ge(s_split, 4 * q + 4)
                act.activation(parts[4 * N:6 * N, par], rest2[:], ACT.Copy).then_inc(s_parts, 1)

            def copy_b(q, n):
                act.wait_ge(s_pb, N * q + n + 1)
                if later(q, 1) or n >= DEEP:
                    act.wait_ge(s_drive, N * q + n + 1 - DEEP)
                act.activation(b_all[:, n % DEEP], p_b[:], ACT.Copy).then_inc(s_ball, 1)

            def scan(q, par, n):
                done = N * q + n
                if n == 0:
                    act.wait_ge(s_dt, q + 1)
                if later(q, 1) or n >= DEEP:
                    act.wait_ge(s_h, J * (done + 1 - DEEP))
                act.activation(decay[:, n % DEEP], dt[:, par], ACT.Exp, scale=-(n + 1.0)).then_inc(s_decay, 1)
                if n + 1 < N:
                    copy_b(q, n + 1)
                elif not isinstance(q, int) or q + 1 < Q:
                    copy_b(q + 1, 0)

            def out_rstd(q, par):
                act.wait_ge(s_omom, S * (q + 1))
                act.activation(olnvar[:], omoments[:, :, 1], ACT.Ln, bias=eps[:]).then_inc(s_olnv, 1)
                act.wait_ge(s_olnv, q + 1)
                act.wait_ge(s_x1, S * q)
                act.wait_ge(s_oshift, q)
                act.activation(orstd[:], olnvar[:], ACT.Exp, scale=-0.5).then_inc(s_orstd, 1)
                act.activation(ominus[:], omoments[:, :, 0], ACT.Copy, scale=-1.0).then_inc(s_ominus, 1)

            def norm_out(q, par):
                act.wait_ge(s_oshift, q + 1)
                act.wait_ge(s_orstd, q + 1)
                if later(q, 2):
                    act.wait_ge(s_x1out[par], 8 * (q - par))
                    act.wait_ge(s_sent[par], SENT // 2 * (q - par))
                for s in range(S):
                    act.activation(x1[:, par, s], res[:, s], ACT.Identity, scale=orstd[:, s:s + 1],
                                   bias=oshift[:, s:s + 1]).then_inc(s_x1, 1)

            def take_x1(q, par):
                act.wait_ge(s_x1t, q + 1)
                act.wait_ge(s_lp, q)
                act.activation(x1T[:], p_mm[2][:], ACT.Copy).then_inc(s_x1T, 1)

            def take_logits(q, par):
                act.wait_ge(s_lp, q + 1)
                if later(q, 1):
                    act.wait_ge(s_route, STEPS * q)
                act.activation(logits[:], p_logits, ACT.Copy).then_inc(s_logits, 1)

            run_chunks(Q, N, act.Fori, [
                (7, -1, out_rstd), (9, -1, norm_out), (11, -1, take_x1), (13, -1, take_logits),
                (15, 2, take_xb), (3, 1, take_conv), (5, 1, take_z), (5, 1, take_xa), (8, 2, x_rstd),
                (10, 2, norm_x), (12, 2, scale_x), (7, 1, take_bcd),
                (9, 1, dt_exp), (9, 1, dt_log), (13, 1, place_parts)], scan, start=lambda: copy_b(0, 0))

        @block.tensor
        def _(pe):
            pe.wait_ge(s_w, WEIGHTS)
            pe.wait_ge(s_cst, CONSTS)

            def turn_x(q, par):
                pe.wait_ge(s_xn, S * (q + 1))
                if later(q, 1):
                    pe.wait_ge(s_bcs, q)
                for s in range(S):
                    t = pe.transpose(p_mm[0][:, P * s:P * s + P], xn[:, s], keep.ident[:])
                t.then_inc(s_xT, 1)

            def turn_x1(q, par):
                pe.wait_ge(s_x1, S * (q + 1))
                if not isinstance(q, int) or q + 2 < Q:
                    pe.wait_ge(s_dtn, J * (q + 3))
                for s in range(S):
                    t = pe.transpose(p_mm[2][:, P * s:P * s + P], x1[:, par, s], keep.ident[:])
                t.then_inc(s_x1t, 1)

            def project_logits(q, par):
                pe.wait_ge(s_x1T, q + 1)
                for s in range(S):
                    t = pe.matmul(p_logits[:, s], x1T[:, P * s:P * s + P], wg[:], start=True, stop=True)
                t.then_inc(s_lp, 1)

            def ranks(q, par):
                pe.wait_ge(s_route, STEPS * q + 11)
                if not isinstance(q, int) or q + 1 < Q:
                    pe.wait_ge(s_res, q + 2)
                flat = p_rank.rearrange("p s k e -> p (s k e)")
                pe.matmul(flat, keep.before[:], chosen[:].rearrange("p s k e -> p (s k e)"), start=True, stop=True)
                for back in range(1, S + 1):
                    t = pe.matmul(flat[:, K * E * back:], keep.ones[:],
                                  chosen[:, 0:S + 1 - back].rearrange("p s k e -> p (s k e)"), start=False, stop=True,
                                  skip_group_check=True)
                t.then_inc(s_ranks, 1)

            def project_in(q, c):
                pe.wait_ge(s_nT, q + 1)
                if c == 0:
                    pe.wait_ge(s_bc, q)
                if c == 1:
                    pe.wait_ge(s_dtn, J * q)
                    if later(q, 3):
                        pe.wait_ge(s_logits, q - 2)
                if c >= J:
                    pe.wait_ge(s_xb, J * q + c - J + 1)
                pe.matmul(p_mm[c % J + 1][:], w_in[:, P * c:P * c + P], nT[:], start=True, stop=True).then_inc(s_in, 1)

            def convolve_first(q, par):
                pe.wait_ge(s_xb, J * q + 1)
                for k in range(CONV):
                    t = pe.matmul(p_mm[0][:], tap_diag[:, k], xb[:, 0, k:k + C], start=(k == 0), stop=(k == CONV - 1))
                t.then_inc(s_conv_product, 1)

            def project_bcd(q, par):
                pe.wait_ge(s_xa, J * (q + 1))
                if later(q, 3):
                    pe.wait_ge(s_route, STEPS * (q - 3) + RANKED)
                if later(q, 1):
                    pe.wait_ge(s_res, q - 1)
                for j in range(J):
                    t = pe.matmul(p_mm[0][0:2 * N + R, :], w_bcd[:, j], xa[:, par, j], start=(j == 0), stop=(j == J - 1))
                t.then_inc(s_bcd, 1)

            def project_dt(q, par):
                pe.wait_ge(s_dtr, q + 1)
                pe.wait_ge(s_z, J * (q + 1))
                for j in range(J):
                    pe.matmul(p_mm[j + 1][:], w_dt[2 * N:, P * j:P * j + P], dtr[2 * N:, :], start=True,
                              stop=True).then_inc(s_dtp, 1)

            def mean_dt(q, par):
                pe.wait_ge(s_dt, q + 1)
                pe.wait_ge(s_dtn, J * (q + 1))
                for j in range(J):
                    t = pe.matmul(p_mm[1][0:2 * N, :], mean_w[:], dt[:, par, j], start=(j == 0), stop=(j == J - 1))
                t.then_inc(s_mean, 1)

            def spread_b(q, par, n):
                if n == 0:
                    pe.wait_ge(s_parts, 2 * q + 2)
                if later(q, 1) or n:
                    pe.wait_ge(s_ball, N * q + n)
                pe.matmul(p_b[:], pick[:, n], parts[:, par], start=True, stop=True).then_inc(s_pb, 1)

            def spread_c(q, par, n):
                if later(q, 1) or n >= 2:
                    pe.wait_ge(s_hc, N * q + n - 1)
                pe.matmul(p_c[:, n % 2], pick[:, N + n], parts[:, par], start=True, stop=True).then_inc(s_pc, 1)

            def ahead(spread, q, par, n):
                if n < N:
                    spread(q, par, n)
                elif not isinstance(q, int) or q + 1 < Q:
                    spread(q + 1, 1 - par, n - N)

            def sum_state(q, par, n):
                pe.wait_ge(s_hc, N * q + n + 1)
                if n == 0 and later(q, 1):
                    pe.wait_ge(s_g, q)
                for j in range(J):
                    t = pe.matmul(p_y[:, j], keep.ident[:], hc[:, n % DEEP, j], start=(n == 0), stop=(n == N - 1))
                t.then_inc(s_y, 1)

            def scan(q, par, n):
                ahead(spread_b, q, par, n + 2)
                ahead(spread_c, q, par, n + 1)
                if n > 0:
                    sum_state(q, par, n - 1)

            def project_out(q, par):
                pe.wait_ge(s_g, q + 1)
                if not isinstance(q, int) or q + 2 < Q:
                    pe.wait_ge(s_conv_taken, q + 3)
                elif q + 2 == Q:
                    pe.wait_ge(s_bcs, q + 2)
                else:
                    pe.wait_ge(s_route, STEPS * (q - 2) + RANKED)
                for s in range(S):
                    for j in range(J):
                        t = pe.matmul(p_mm[0][:, P * s:P * s + P], gated[:, j, P * s:P * s + P], w_out[:, j],
                                      start=(j == 0), stop=(j == J - 1))
                t.then_inc(s_o, 1)

            def start():
                pe.wait_ge(s_pick, 4)
                for n in range(2):
                    spread_b(0, 0, n)
                spread_c(0, 0, 0)

            run_chunks(Q, N, pe.Fori, [
                (0, -1, lambda q, par: sum_state(q, par, N - 1)), (2, -1, project_out),
                (10, -1, turn_x1), (12, -1, project_logits), (4, -2, ranks), (15, 2, convolve_first),
                (13, 2, lambda q, par: project_in(q, 0)), (13, 2, lambda q, par: project_in(q, 1)),
                (1, 1, lambda q, par: project_in(q, 2)), (1, 1, lambda q, par: project_in(q, 3)),
                (6, 1, project_bcd), (8, 1, project_dt), (11, 2, turn_x), (11, 1, mean_dt)], scan, start=start)


def moe(nc, keep, c_fc, c_proj):
    E, D, F = c_fc.shape
    FB = F // P
    K, CAP = keep.K, keep.CAP
    CT = CAP // P
    NT = keep.x1.shape[0] // P

    with ExitStack() as ctx:
        m = Space(nc, ctx, "expert")
        w1, w2 = m.sb("w1", [P, 2, F]), m.sb("w2", [P, 2, FB, D])
        xe, xT = m.sb("xe", [P, 2, CT, D]), m.sb("xT", [P, CAP])
        hT = m.sb("hT", [P, FB, CAP])
        ye = m.sb("ye", [P, 2, CT, D])
        first_of = m.sb("first_of", [P, 1, E])
        before = m.sb("before", [P, E])
        begin = m.sb("begin", [P, 1, E])
        begin_at = m.sb("begin_at", [P, E], I32)
        mask, picked = m.sb("mask", [P, NT * K, E]), m.sb("picked", [P, NT * K, E])
        base, local, fits, room, at = (m.sb(n, [P, NT, K]) for n in ("base", "local", "fits", "room", "at"))
        gap, ratio, den, p1 = (m.sb(n, [P, NT]) for n in ("gap", "ratio", "den", "p1"))
        s_iota, s_r, s_ratio = m.sem("iota_made"), m.sem("table_steps"), m.sem("ratio_made")
        p_t = [m.ps(f"p_t{i}", [P, 4 * P]) for i in range(2)]
        p_h = [m.ps(f"p_h{i}", [P, 4 * P]) for i in range(4)]
        p_o = [m.ps(f"p_o{i}", [P, 4, D]) for i in range(2)]
        s_in = [m.sem(f"expert_loaded{i}") for i in range(2)]
        s_t, s_xT, s_h, s_g, s_o, s_y = (m.sem("transposed"), m.sem("xT_made"), m.sem("h_product"),
                                         m.sem("gelu_made"), m.sem("out_product"), m.sem("y_copied"))
        s_out = [m.sem(f"y_stored{i}") for i in range(2)]
        block = m.block()
        BEGINS, GAP = 3, 4
        groups = [(a, min(a + 4, CT)) for a in range(0, CT, 4)]
        NG = len(groups)
        ye_rows = keep.ye.rearrange("(e c p) d -> e p c d", e=E, p=P)
        w2_rows = c_proj.rearrange("e (c p) d -> e p c d", p=P)

        @block.sync
        def _(sp):
            def load(e, par):
                if isinstance(e, int):
                    begins, b, c = begin_at[0:1, e:e + 1], c_fc[e], w2_rows[e]
                else:
                    begins = begin_at[0:1, bass.ds(e, 1)]
                    b, c = c_fc[bass.ds(e, 1)].rearrange("a p f -> (a p) f"), at_chunk(w2_rows, e)
                sp.dma_start(w1[:, par], b).then_inc(s_in[par], 16)
                sp.dma_start(w2[:, par], c).then_inc(s_in[par], 16)
                if isinstance(e, int) and e == 0:
                    sp.wait_ge(s_r, BEGINS)
                row = sp.value_load(begins, min_val=0, max_val=(2 * E - 1) * CAP)
                sp.dma_start(xe[:, par], keep.xe[bass.ds(row, CAP), :].rearrange("(c p) d -> p c d", p=P)).then_inc(s_in[par], 16)

            def store(e, par):
                sp.wait_ge(s_y, NG * (e + 1))
                sp.wait_ge(s_y, 1)
                sp.dma_start(at_chunk(ye_rows, e), ye[:, par]).then_inc(s_out[par], 16)

            load(0, 0)
            load(1, 1)
            with sp.Fori(1, E // 2) as i:
                for par in range(2):
                    store(2 * i + par - 2, par)
                    load(2 * i + par, par)
            for par in range(2):
                store(E - 2 + par, par)
            for par in range(2):
                sp.wait_ge(s_out[par], 16 * (E // 2))

        @block.tensor
        def _(pe):
            with pe.Fori(0, E // 2) as i:
                for par in range(2):
                    e = 2 * i + par
                    pe.wait_ge(s_in[par], 48 * i + 48)
                    for n, (a, b) in enumerate(groups):
                        k_ = (NG * par + n) % 2
                        if NG * par + n >= 2:
                            pe.wait_ge(s_xT, NG * e + n - 1)
                        else:
                            pe.wait_ge(s_xT, NG * e)
                        for c in range(a, b):
                            t = pe.transpose(p_t[k_][:, P * (c - a):P * (c - a) + P], xe[:, par, c], keep.ident[:])
                        t.then_inc(s_t, 1)

                    def out(n):
                        a, b = groups[n]
                        k_ = (NG * par + n) % 2
                        pe.wait_ge(s_g, FB * (NG * e + n + 1))
                        if NG * par + n >= 2:
                            pe.wait_ge(s_y, NG * e + n - 1)
                        else:
                            pe.wait_ge(s_y, NG * e)
                        for c in range(a, b):
                            for f in range(FB):
                                t = pe.matmul(p_o[k_][:, c - a], hT[:, f, P * c:P * c + P], w2[:, par, f],
                                              start=(f == 0), stop=(f == FB - 1))
                        t.then_inc(s_o, 1)

                    for n, (a, b) in enumerate(groups):
                        pe.wait_ge(s_xT, NG * e + n + 1)
                        for f in range(FB):
                            done = FB * (NG * e + n) + f
                            if NG * par + n == 0:
                                pe.wait_ge(s_g, FB * NG * e)
                            else:
                                pe.wait_ge(s_g, done - FB + 1)
                            pe.matmul(p_h[f][:, 0:P * (b - a)], w1[:, par, P * f:P * f + P], xT[:, P * a:P * b],
                                      start=True, stop=True).then_inc(s_h, 1)
                        if n:
                            out(n - 1)
                    out(NG - 1)

        @block.gpsimd
        def _(pool):
            pool.iota(first_of[:, 0], pattern=[[-1, E]], base=E, channel_multiplier=0,
                      allow_small_or_imprecise_dtypes=True).then_inc(s_iota, 1)
            pool.iota(before[:], pattern=[[2 * CAP, E]], base=CAP, channel_multiplier=0,
                      allow_small_or_imprecise_dtypes=True).then_inc(s_iota, 1)

        @block.scalar
        def _(act):
            act.wait_ge(s_r, GAP)
            act.activation(ratio[:], gap[:], ACT.Exp).then_inc(s_ratio, 1)
            with act.Fori(0, E // 2) as i:
                for par in range(2):
                    e = 2 * i + par
                    act.wait_ge(s_o, NG * e)
                    for n, (a, b) in enumerate(groups):
                        for f in range(FB):
                            act.wait_ge(s_h, FB * (NG * e + n) + f + 1)
                            act.activation(hT[:, f, P * a:P * b], p_h[f][:, 0:P * (b - a)],
                                           ACT.Gelu).then_inc(s_g, 1)

        @block.vector
        def _(dve):
            steps = [0]

            def step(ins):
                ins.then_inc(s_r, 1)
                steps[0] += 1
                dve.wait_ge(s_r, steps[0])

            dve.wait_ge(s_iota, 2)
            step(dve.tensor_scalar(begin[:, 0], keep.count[:, 0, 0], float(CAP), None, ALU.min))
            step(dve.tensor_tensor(begin[:, 0], before[:], begin[:, 0], ALU.subtract))
            step(dve.tensor_copy(begin_at[:], begin[:, 0]))
            step(dve.tensor_tensor(gap[:], keep.best[:, :, 1], keep.best[:, :, 0], ALU.subtract))
            flat = lambda v: v[:].rearrange("p t k -> p (t k)")
            wide = (P, NT * K, E)
            step(dve.tensor_tensor(mask[:], flat(keep.pref)[:, :, None].broadcast_to(wide),
                                   first_of[:].broadcast_to(wide), ALU.is_equal))
            step(dve.tensor_tensor(picked[:], mask[:], begin[:].broadcast_to(wide), ALU.mult))
            step(dve.tensor_reduce(flat(base), picked[:], AX.X, ALU.add))
            step(dve.tensor_tensor(local[:], keep.row[:], base[:], ALU.subtract))
            step(dve.tensor_scalar(fits[:], local[:], 0.0, None, ALU.is_ge))
            step(dve.tensor_scalar(room[:], local[:], float(CAP), None, ALU.is_lt))
            step(dve.tensor_tensor(fits[:], fits[:], room[:], ALU.mult))
            step(dve.tensor_scalar(at[:], keep.pref[:], -float(CAP), float(E * CAP), ALU.mult, ALU.add))
            step(dve.tensor_tensor(at[:], at[:], local[:], ALU.add))
            step(dve.tensor_tensor(at[:], at[:], fits[:], ALU.mult))
            for c in range(K):
                step(dve.tensor_copy(keep.from_slot[:, c], at[:, :, c]))
            dve.wait_ge(s_ratio, 1)
            step(dve.tensor_scalar(den[:], ratio[:], 1.0, None, ALU.add))
            step(dve.reciprocal(p1[:], den[:]))
            step(dve.tensor_tensor(keep.weight[:, 0], p1[:], fits[:, :, 0], ALU.mult))
            step(dve.tensor_tensor(den[:], p1[:], ratio[:], ALU.mult))
            step(dve.tensor_tensor(keep.weight[:, 1], den[:], fits[:, :, 1], ALU.mult))

            with dve.Fori(0, E // 2) as i:
                for par in range(2):
                    e = 2 * i + par
                    dve.wait_ge(s_h, FB * NG * e)
                    for n, (a, b) in enumerate(groups):
                        k_ = (NG * par + n) % 2
                        dve.wait_ge(s_t, NG * e + n + 1)
                        dve.tensor_copy(xT[:, P * a:P * b], p_t[k_][:, 0:P * (b - a)]).then_inc(s_xT, 1)
                    dve.wait_ge(s_out[par], 16 * i)
                    for n, (a, b) in enumerate(groups):
                        k_ = (NG * par + n) % 2
                        dve.wait_ge(s_o, NG * e + n + 1)
                        dve.tensor_copy(ye[:, par, a:b], p_o[k_][:, 0:b - a]).then_inc(s_y, 1)


def gla(nc, keep, Wq, Wk, Wv, Wg, gk_w1, gk_w2, gk_b2, g_norm_w, Wo, ffn):
    T = keep.x1.shape[0]
    D, DK = Wq.shape
    DV = Wv.shape[1]
    R = gk_w1.shape[1]
    HEADS = 4
    DH, VH = DK // HEADS, DV // HEADS
    CH = 64
    S = 4
    C = S * P
    NC = C // CH
    Q = T // C
    SCALE = DH ** -0.5
    GATE = 16.0
    assert (D, DK, DV) == (P, P, 2 * P)
    K = 2
    E = ffn.centroids.shape[0]
    ROUND, PLACES = 16 * S, 16 * S
    x1_tiles = keep.x1.rearrange("(q s p) d -> q p s d", s=S, p=P)

    with ExitStack() as ctx:
        m = Space(nc, ctx, "gla")
        wq, wk = m.sb("wq", [P, DK]), m.sb("wk", [P, DK])
        wvg = m.sb("wvg", [P, 2 * DV])
        w1, w2, b2 = m.sb("w1", [P, R]), m.sb("w2", [R, DK]), m.sb("b2", [P, 1])
        nb2 = m.sb("nb2", [P, 1])
        gnw = m.sb("gnw", [P, 1])
        wo_in, wo = m.sb("wo_in", [P, 2, D]), m.sb("wo", [P, 2, D])
        eps = keep.eps
        lnc = m.sb("lnc", [E, 3, D])
        causal = m.sb("causal", [P, 1, P])
        inside = m.sb("inside", [P, NC, CH])
        x1, y = m.sb("x1", [P, 2, S, D]), m.sb("y", [P, 2, K, S, D])
        ix, w = m.sb("ix", [P, 2, K, S], I32), m.sb("w", [P, 2, K, S])
        sum2, x2, x2r = m.sb("sum2", [P, S, D]), m.sb("x2", [P, 2, S, D]), m.sb("x2r", [P, 2, S, D])
        stats2, moments2 = m.sb("stats2", [P, S, 6]), m.sb("moments2", [P, S, 2])
        lnvar2, rstd2 = m.sb("lnvar2", [P, S]), m.sb("rstd2", [P, S])
        xT = m.sb("xT", [P, C])
        v, sg = m.sb("v", [P, 2, S, DV]), m.sb("sg", [P, 2, S, DV])
        low = m.sb("low", [R, C])
        mag, em, lm, neg = (m.sb(n, [P, C]) for n in ("mag", "em", "lm", "neg"))
        rate, cum, left = m.sb("rate", [P, C]), m.sb("cum", [P, NC, CH]), m.sb("left", [P, NC, CH])
        eq, ek, eh = m.sb("eq", [P, 2, NC, CH]), m.sb("ek", [P, C]), m.sb("eh", [P, C])
        qg, kg, khT = m.sb("qg", [P, 2, C]), m.sb("kg", [P, 1, C]), m.sb("khT", [P, C])
        kgh = m.sb("kgh", [P, 2, HEADS, C])
        of_head = m.sb("of_head", [P, HEADS, 1])
        own = m.sb("own", [P, 1, DV])
        kvm = m.sb("kvm", [P, 2, DV])
        kh = m.sb("kh", [P, 2, 2, S, DK])
        state = m.sb("state", [P, NC, DV])
        am = m.sb("am", [P, 2, HEADS, P])
        o, sq = m.sb("o", [P, S, DV]), m.sb("sq", [P, S, HEADS, VH])
        ss, lss, ri = (m.sb(n, [P, S * HEADS]) for n in ("ss", "lss", "ri"))
        on, og = (m.sb(n, [P, S * HEADS, VH]) for n in ("on", "og"))
        ogT = m.sb("ogT", [P, S, 2, P])
        res = m.sb("res", [P, S, D])
        row3 = m.sb("row3", [P, 2, S, keep.WIDE])
        numbers = m.sb("numbers", [P, 1, T // P])
        x3T = m.sb("x3T", [P, C])
        first_of = m.sb("first_of", [P, 1, E])
        hit, cand, rank, picked = (m.sb(n, [P, S, E]) for n in ("hit", "cand", "rank", "picked"))
        chosen = m.sb("chosen", [P, S + 1, E])
        pref, place = m.sb("pref", [P, S]), m.sb("place", [P, S])
        ix3 = m.sb("ix3", [P, 2, S], I32)
        stats, moments = m.sb("stats", [P, S, 6]), m.sb("moments", [P, S, 2])
        lnvar, rstd = m.sb("lnvar", [P, S]), m.sb("rstd", [P, S])
        p_a = m.ps("p_a", [P, C])
        p_q, p_k = m.ps("p_q", [P, C]), m.ps("p_k", [P, C])
        p_f = m.ps("p_f", [P, C])
        p_r = m.ps("p_r", [P, C])
        p_near = p_r[:, 0:S * E].rearrange("p (s e) -> p s e", e=E)
        p_rank = p_r[:, S * E:(2 * S + 1) * E].rearrange("p (s e) -> p s e", e=E)
        p_kv = m.ps("p_kv", [P, 2, DV])
        p_s = m.ps("p_s", [P, HEADS, P])
        p_o = m.ps("p_o", [P, DV])

        s_w, s_zero, s_mask = m.sem("weights_loaded"), m.sem("zeroed"), m.sem("masks_made")
        s_x = [m.sem(f"x1_loaded{i}") for i in range(2)]
        s_y = [[m.sem(f"rows_fetched{i}{c}") for c in range(K)] for i in range(2)]
        s_ix, s_sum2, s_st2, s_mom2, s_lnv2, s_rstd2, s_x2, s_x2r = (m.sem(n) for n in (
            "ix_made", "sum_steps", "stats2_made", "moments2_made", "lnvar2_made", "rstd2_made", "x2_made", "x2_kept"))
        s_wo, s_iota, s_wT, s_cT = m.sem("wo_scaled"), m.sem("iota_made"), m.sem("small_transposed"), m.sem("cT_made")
        s_t3, s_x3T, s_near, s_route, s_ranks = (m.sem(n) for n in (
            "x3_transposed", "x3T_made", "affinity_product", "routing_steps", "rank_products"))
        s_number, s_placed = m.sem("numbered"), [m.sem(f"rows_placed{i}") for i in range(2)]
        (s_t, s_xT, s_low, s_lows, s_vg, s_v, s_sg, s_u, s_q, s_gate, s_neg, s_lm, s_rate, s_cum, s_left, s_eq, s_ek, s_eh,
         s_qk, s_kht, s_kh) = (m.sem(n) for n in (
             "x_transposed", "xT_made", "low_product", "low_made", "vg_product", "v_made", "silu_g_made", "u_product",
             "qk_product", "gate_steps", "neg_made", "lm_made", "rate_made", "cum_made", "left_made", "eq_made",
             "ek_made", "eh_made", "qk_scaled", "kh_transposed", "kh_made"))
        s_kv, s_s, s_state, s_am, s_o = (m.sem(n) for n in ("kv_product", "score_product", "state_made", "scores_masked",
                                                            "o_product"))
        s_oo = m.sem("o_kept")
        s_sq, s_ss, s_lss, s_ri, s_on, s_og, s_ogt, s_ogT, s_out = (m.sem(n) for n in (
            "squares_made", "sums_made", "ln_sums_made", "rms_made", "o_normed", "o_gated",
            "og_transposed", "ogT_made", "out_product"))
        s_res, s_st, s_mom, s_lnv, s_rstd, s_x3 = (m.sem(n) for n in (
            "residual_made", "stats_made", "moments_made", "lnvar_made", "rstd_made", "x3_made"))
        s_kgh, s_kvm = m.sem("kg_by_head"), m.sem("kv_masked")
        s_inside = m.sem("inside_made")
        s_turn, s_sp_turn, s_pool_turn = m.sem("vector_steps"), m.sem("sync_steps"), m.sem("pool_steps")
        block = m.block()
        WEIGHTS = 16 * 13

        @block.sync
        def _(sp):
            for par in range(2):
                sp.dma_start(x1[:, par], x1_tiles[par]).then_inc(s_x[par], 16)
            sp.dma_start(wq[:], Wq).then_inc(s_w, 16)
            sp.dma_start(wk[:], Wk).then_inc(s_w, 16)
            sp.dma_start(wvg[:, 0:DV], Wv).then_inc(s_w, 16)
            sp.dma_start(wvg[:, DV:], Wg).then_inc(s_w, 16)
            sp.dma_start(w1[:], gk_w1).then_inc(s_w, 16)
            sp.dma_start(w2[:], gk_w2).then_inc(s_w, 16)
            sp.dma_start(b2[:], gk_b2.rearrange("(p a) -> p a", a=1)).then_inc(s_w, 16)
            for h in range(2):
                sp.dma_start(gnw[VH * h:VH * h + VH], g_norm_w.rearrange("(p a) -> p a", a=1)).then_inc(s_w, 16)
            sp.dma_start(wo_in[:], Wo.rearrange("(j p) n -> p j n", p=P)).then_inc(s_w, 16)
            for n, v in enumerate((ffn.centroids, ffn.ln_g, ffn.ln_b)):
                sp.dma_start(lnc[:, n], v).then_inc(s_w, 16)
            for q in range(2, 4):
                sp.wait_ge(s_sum2, 2 * S * (q - 1))
                sp.dma_start(x1[:, q % 2], x1_tiles[q]).then_inc(s_x[q % 2], 16)
            sp.dma_start(keep.w1s[:], ffn.w1.rearrange("e p f -> p e f")).then_inc(keep.s_big, 16)
            for e in range(E):
                sp.dma_start(keep.w2s[:, e], ffn.w2[e].rearrange("(c p) d -> p c d", p=P)).then_inc(keep.s_big, 16)
            sp.dma_start(keep.b1s[:], ffn.b1.rearrange("(a e) f -> a e f", a=1).broadcast_to(keep.b1s.shape)).then_inc(keep.s_big, 16)
            sp.dma_start(keep.b2s[:], ffn.b2.rearrange("(a e) d -> a e d", a=1)).then_inc(keep.s_big, 16)
            with sp.Fori(2, Q // 2) as i:
                for par in range(2):
                    q = 2 * i + par
                    sp.wait_ge(s_sum2, 2 * S * (q - 1))
                    sp.sem_inc(s_sp_turn, 1)
                    sp.dma_start(x1[:, par], at_chunk(x1_tiles, q)).then_inc(s_x[par], 16)

        @block.gpsimd
        def _(pool):
            pool.iota(first_of[:, 0], pattern=[[-1, E]], base=E, channel_multiplier=0,
                      allow_small_or_imprecise_dtypes=True).then_inc(s_iota, 1)
            pool.iota(numbers[:, 0], pattern=[[P, T // P]], base=0, channel_multiplier=1,
                      allow_small_or_imprecise_dtypes=True).then_inc(s_iota, 1)
            pool.iota(keep.base[:, 0], pattern=[[T, E]], base=0, channel_multiplier=0,
                      allow_small_or_imprecise_dtypes=True).then_inc(s_iota, 1)
            pool.wait_ge(s_zero, 6)
            pool.affine_select(out=causal[:, 0], in_=causal[:, 0], compare_op=ALU.is_ge, fill=0.0, base=0,
                               pattern=[[1, P]], channel_multiplier=-1).then_inc(s_mask, 1)
            pool.wait_ge(s_mask, 1)
            pool.affine_select(out=causal[:, 0, CH:], in_=causal[:, 0, CH:], compare_op=ALU.is_ge, fill=0.0, base=-CH,
                               pattern=[[0, CH]], channel_multiplier=1).then_inc(s_mask, 1)
            for n, (tile, width) in enumerate(((of_head, 1), (own, VH))):
                view = tile[:].rearrange("p h a -> p (h a)").rearrange("p (h e) -> p h e", h=HEADS)
                pool.affine_select(out=view, in_=view, compare_op=ALU.is_ge, fill=0.0, base=0,
                                   pattern=[[-DH, HEADS], [0, width]], channel_multiplier=1).then_inc(s_mask, 1)
                pool.wait_ge(s_mask, 3 + 2 * n)
                pool.affine_select(out=view, in_=view, compare_op=ALU.is_ge, fill=0.0, base=DH - 1,
                                   pattern=[[DH, HEADS], [0, width]], channel_multiplier=-1).then_inc(s_mask, 1)
            pool.wait_ge(s_mask, 6)

            def fetch(q, par, c):
                pool.wait_ge(s_ix, 2 * (q + 1))
                if later(q, 2):
                    pool.wait_ge(s_sum2, 2 * S * (q - 1))
                pool.sem_inc(s_pool_turn, 1)
                for s in range(S):
                    pool.indirect_dma_start(
                        out=y[:, par, c, s], out_offset=None, in_=keep.ye,
                        in_offset=bass.IndirectOffsetOnAxis(ap=ix[:, par, c, s:s + 1], axis=0),
                        bounds_check=keep.ye.shape[0] - 1, oob_is_err=False).then_inc(s_y[par][c], 16)

            def gate_o(q, par):
                pool.wait_ge(s_on, q + 1)
                pool.wait_ge(s_sg, S * (q + 1))
                pool.wait_ge(s_ogt, 2 * q)
                pool.tensor_tensor(og[:], on[:], sg[:, par].rearrange("p s (h e) -> p (s h) e", h=HEADS),
                                   ALU.mult).then_inc(s_og, 1)

            def add_rate(q, par):
                pool.wait_ge(s_lm, q + 1)
                pool.wait_ge(s_neg, q + 1)
                pool.wait_ge(s_cum, q)
                pool.tensor_tensor(rate[:], neg[:], lm[:], ALU.add).then_inc(s_rate, 1)

            def rate_left(q, par):
                pool.wait_ge(s_cum, q + 1)
                pool.wait_ge(s_eh, q)
                pool.tensor_tensor(left[:], cum[:, :, CH - 1:CH].broadcast_to((P, NC, CH)), cum[:],
                                   ALU.subtract).then_inc(s_left, 1)

            def send(q, par):
                pool.wait_ge(s_route, 10 * (q + 1))
                pool.sem_inc(s_pool_turn, 1)
                pool.wait_ge(s_number, q + 1)
                pool.sem_inc(s_pool_turn, 1)
                for s in range(S):
                    pool.indirect_dma_start(
                        out=keep.xs, out_offset=bass.IndirectOffsetOnAxis(ap=ix3[:, par, s:s + 1], axis=0),
                        in_=row3[:, par, s], in_offset=None, bounds_check=E * T - 1,
                        oob_is_err=False).then_inc(s_placed[par], 16)

            run_chunks(Q, 2 * S, pool.Fori, [
                (0, 2, lambda q, par: fetch(q, par, 0)), (2, -1, gate_o), (3, 2, lambda q, par: fetch(q, par, 1)),
                (4, 1, add_rate), (4, 1, rate_left), (7.5, -2, send)], lambda q, par, n: None)
            for par in range(2):
                pool.wait_ge(s_placed[par], PLACES * (Q // 2))

        @block.scalar
        def _(act):
            act.preload_act_table_set(LN_EXP)
            act.wait_ge(s_w, WEIGHTS)
            act.activation(nb2[:], b2[:], ACT.Copy, scale=-1.0).then_inc(s_gate, 1)
            for j in range(2):
                act.activation(wo[:, j], wo_in[:, j], ACT.Copy, scale=gnw[:]).then_inc(s_wo, 1)
            act.wait_ge(s_gate, 1)
            act.wait_ge(s_zero, 6)
            act.wait_ge(s_iota, 3)
            act.wait_ge(s_mask, 6)

            def rstd_of(q, moments, lnvar, rstd, s_mom, s_lnv, s_rstd, s_used):
                act.wait_ge(s_mom, S * (q + 1))
                act.activation(lnvar[:], moments[:, :, 1], ACT.Ln, bias=eps[:]).then_inc(s_lnv, 1)
                act.wait_ge(s_lnv, q + 1)
                act.wait_ge(s_used, S * q)
                act.activation(rstd[:], lnvar[:], ACT.Exp, scale=-0.5).then_inc(s_rstd, 1)

            def x2_rstd(q, par):
                rstd_of(q, moments2, lnvar2, rstd2, s_mom2, s_lnv2, s_rstd2, s_x2)

            def x3_rstd(q, par):
                rstd_of(q, moments, lnvar, rstd, s_mom, s_lnv, s_rstd, s_x3)

            def take_x2(q, par):
                act.wait_ge(s_t, q + 1)
                act.wait_ge(s_vg, S * q)
                act.wait_ge(s_q, 2 * q)
                act.activation(xT[:], p_a[:], ACT.Copy).then_inc(s_xT, 1)

            def keep_x2(q, par):
                act.wait_ge(s_x2, S * (q + 1))
                if later(q, 2):
                    act.wait_ge(s_res, q - 1)
                act.activation(x2r[:, par], x2[:, par], ACT.Copy).then_inc(s_x2r, 1)

            def take_low(q, par):
                act.wait_ge(s_low, q + 1)
                act.wait_ge(s_u, q)
                act.activation(low[:], p_a[0:R, :], ACT.Copy).then_inc(s_lows, 1)

            def take_vg(q, par, tiles):
                if later(q, 2):
                    act.wait_ge(s_o, S * (q - 1))
                    act.wait_ge(s_og, q - 1)
                for s in tiles:
                    p = (p_q, p_k)[s % 2]
                    act.wait_ge(s_vg, S * q + s + 1)
                    act.activation(sg[:, par, s], p[:, DV:], ACT.Silu).then_inc(s_sg, 1)
                    act.activation(v[:, par, s], p[:, 0:DV], ACT.Copy).then_inc(s_v, 1)
                if S - 1 in tiles:
                    act.preload_act_table_set(LN_EXP)

            def gate(q, par):
                act.wait_ge(s_u, q + 1)
                act.activation(mag[:], p_a[:], ACT.Abs, bias=b2[:]).then_inc(s_gate, 1)
                act.wait_ge(s_rate, q)
                act.activation(neg[:], p_a[:], ACT.Relu, scale=-1.0, bias=nb2[:]).then_inc(s_neg, 1)
                act.wait_ge(s_gate, 2 * q + 2)
                act.activation(em[:], mag[:], ACT.Exp, scale=-1.0).then_inc(s_gate, 1)
                act.wait_ge(s_gate, 2 * q + 3)
                act.activation(lm[:], em[:], ACT.Ln, bias=1.0).then_inc(s_lm, 1)

            def decays(q, par):
                flat = cum[:].rearrange("p c t -> p (c t)")
                act.wait_ge(s_cum, q + 1)
                if later(q, 2):
                    act.wait_ge(s_state, NC * (q - 1))
                act.activation(eq[:, par].rearrange("p c t -> p (c t)"), flat, ACT.Exp, scale=-1 / GATE).then_inc(s_eq, 1)
                act.wait_ge(s_qk, 3 * q)
                act.activation(ek[:], flat, ACT.Exp, scale=1 / GATE).then_inc(s_ek, 1)
                act.wait_ge(s_left, q + 1)
                act.activation(eh[:], left[:].rearrange("p c t -> p (c t)"), ACT.Exp, scale=-1 / GATE).then_inc(s_eh, 1)

            def keys_by_head(q, par):
                act.wait_ge(s_qk, 3 * q + 2)
                if later(q, 2):
                    act.wait_ge(s_s, S * (q - 1))
                for h in range(HEADS):
                    act.activation(kgh[:, par, h], kg[:, 0], ACT.Copy, scale=of_head[:, h]).then_inc(s_kgh, 1)

            def take_kh(q, par):
                act.wait_ge(s_kht, q + 1)
                if later(q, 2):
                    act.wait_ge(s_kv, S * (q - 1))
                for c in range(2):
                    part = slice(CH * c, CH * c + CH)
                    act.activation(kh[part, par, c], p_a[part, :].rearrange("p (s d) -> p s d", s=S),
                                   ACT.Copy).then_inc(s_kh, 1)

            def take_o(q, s):
                act.wait_ge(s_o, S * q + s + 1)
                act.wait_ge(s_on, q)
                act.activation(o[:, s], p_o[:], ACT.Copy).then_inc(s_oo, 1)
                act.wait_ge(s_oo, S * q + s + 1)
                act.wait_ge(s_ss, q)
                act.activation(sq[:, s].rearrange("p h e -> p (h e)"), o[:, s], ACT.Square).then_inc(s_sq, 1)

            def o_rms(q, par):
                act.wait_ge(s_ss, q + 1)
                act.activation(lss[:], ss[:], ACT.Ln, scale=1.0 / VH, bias=eps[:]).then_inc(s_lss, 1)
                act.wait_ge(s_lss, q + 1)
                act.wait_ge(s_on, q)
                act.activation(ri[:], lss[:], ACT.Exp, scale=-0.5).then_inc(s_ri, 1)

            def take_x3(q, par):
                act.wait_ge(s_t3, q + 1)
                act.wait_ge(s_near, q)
                act.activation(x3T[:], p_r[:], ACT.Copy).then_inc(s_x3T, 1)
                if later(q, 2):
                    act.wait_ge(s_placed[par], PLACES // 2 * (q - par))
                at = slice(S * q, S * q + S) if isinstance(q, int) else bass.ds(S * q, S)
                act.activation(row3[:, par, :, D + 1], numbers[:, 0, at], ACT.Copy).then_inc(s_number, 1)

            run_chunks(Q, 2 * S, act.Fori, [
                (0, -1, lambda q, par: take_o(q, 3)), (0, 1, take_x2), (1, -1, o_rms), (1, 1, take_low),
                (2, -2, x3_rstd), (2, 0, lambda q, par: take_o(q, 0)), (2, 1, gate), (3, 0, keep_x2),
                (3, 1, lambda q, par: take_vg(q, par, (0, 1))), (4, 0, lambda q, par: take_o(q, 1)),
                (4, 1, lambda q, par: take_vg(q, par, (2, 3))), (5, 1, decays), (5, -2, take_x3), (5, 2, x2_rstd),
                (6, 0, lambda q, par: take_o(q, 2)), (6, 1, keys_by_head), (7, 1, take_kh)], lambda q, par, n: None)

        @block.vector
        def _(dve):
            dve.memset(causal[:], 1.0).then_inc(s_zero, 1)
            dve.memset(inside[:], 1.0).then_inc(s_zero, 1)
            dve.memset(of_head[:], 1.0).then_inc(s_zero, 1)
            dve.memset(own[:], 1.0).then_inc(s_zero, 1)
            dve.memset(kh[:], 0.0).then_inc(s_zero, 1)
            dve.memset(chosen[:], 0.0).then_inc(s_zero, 1)
            dve.wait_ge(s_zero, 6)
            dve.memset(inside[:, :, 0:1], 0.0).then_inc(s_inside, 1)
            dve.wait_ge(s_inside, 1)
            dve.wait_ge(s_mask, 6)
            dve.wait_ge(s_iota, 3)
            dve.wait_ge(s_wT, 1)
            for n, tile in enumerate((keep.cT, keep.gT, keep.bT)):
                dve.tensor_copy(tile[:], p_kv[:, 0, E * n:E * n + E]).then_inc(s_cT, 1)

            def moments_of(q, src, stats, moments, s_st, s_mom):
                for s in range(S):
                    dve.bn_stats(stats[:, s], src[:, s]).then_inc(s_st, 1)
                dve.wait_ge(s_st, S * (q + 1))
                dve.sem_inc(s_turn, 1)
                for s in range(S):
                    dve.bn_aggr(moments[:, s], stats[:, s]).then_inc(s_mom, 1)

            def indices(q, par):
                at = slice(S * q, S * q + S) if isinstance(q, int) else bass.ds(S * q, S)
                if later(q, 2):
                    for c in range(K):
                        dve.wait_ge(s_y[par][c], ROUND // 2 * (q - par))
                dve.tensor_copy(ix[:, par], keep.from_slot[:, :, at]).then_inc(s_ix, 1)
                dve.tensor_copy(w[:, par], keep.weight[:, :, at]).then_inc(s_ix, 1)

            def sum_expert(q, par, c):
                dve.wait_ge(s_ix, 2 * q + 2)
                if c == 0:
                    dve.wait_ge(s_x[par], 8 * (q - par) + 16)
                    dve.wait_ge(s_x2, S * q)
                else:
                    dve.wait_ge(s_sum2, 2 * S * q + S)
                dve.wait_ge(s_y[par][c], ROUND // 2 * (q - par) + ROUND)
                for s in range(S):
                    dve.scalar_tensor_tensor(out=sum2[:, s], in0=y[:, par, c, s], scalar=w[:, par, c, s:s + 1],
                                             in1=sum2[:, s] if c else x1[:, par, s], op0=ALU.mult,
                                             op1=ALU.add).then_inc(s_sum2, 1)
                if c == K - 1:
                    dve.wait_ge(s_sum2, 2 * S * q + 2 * S)
                    moments_of(q, sum2, stats2, moments2, s_st2, s_mom2)

            def norm_x2(q, par):
                dve.wait_ge(s_rstd2, q + 1)
                dve.wait_ge(s_mom2, S * (q + 1))
                if later(q, 2):
                    dve.wait_ge(s_t, q - 1)
                    dve.wait_ge(s_x2r, q - 1)
                for s in range(S):
                    dve.tensor_scalar(x2[:, par, s], sum2[:, s], moments2[:, s, 0:1], rstd2[:, s:s + 1],
                                      ALU.subtract, ALU.mult).then_inc(s_x2, 1)

            def cumulate(q, par):
                dve.wait_ge(s_rate, q + 1)
                dve.wait_ge(s_ek, q)
                dve.wait_ge(s_left, q)
                dve.tensor_tensor_scan(cum[:].rearrange("p c t -> p (c t)"), inside[:].rearrange("p c t -> p (c t)"),
                                       rate[:], 0.0, ALU.mult, ALU.add).then_inc(s_cum, 1)

            def scale_qk(q, par):
                dve.wait_ge(s_q, 2 * q + 2)
                dve.wait_ge(s_ek, q + 1)
                dve.wait_ge(s_kgh, HEADS * q)
                dve.tensor_tensor(kg[:, 0], p_k[:], ek[:], ALU.mult).then_inc(s_qk, 1)
                dve.wait_ge(s_eq, q + 1)
                if later(q, 2):
                    dve.wait_ge(s_o, S * (q - 1))
                dve.scalar_tensor_tensor(out=qg[:, par], in0=p_q[:], scalar=SCALE,
                                         in1=eq[:, par].rearrange("p c t -> p (c t)"), op0=ALU.mult,
                                         op1=ALU.mult).then_inc(s_qk, 1)
                dve.wait_ge(s_eh, q + 1)
                dve.wait_ge(s_kht, q)
                dve.tensor_tensor(khT[:], p_k[:], eh[:], ALU.mult).then_inc(s_qk, 1)

            def attend(q, par, n):
                if n % 2 == 0:
                    return
                s = n // 2
                dve.wait_ge(s_s, S * q + s + 1)
                if later(q, 1) or s >= 2:
                    dve.wait_ge(s_o, S * q + s - 1)
                dve.tensor_tensor(am[:, s % 2], p_s[:], causal[:].broadcast_to((P, HEADS, P)), ALU.mult).then_inc(s_am, 1)
                dve.wait_ge(s_kv, S * q + s + 1)
                if later(q, 1) or s >= 1:
                    dve.wait_ge(s_state, NC * q + 2 * s)
                dve.tensor_tensor(kvm[:], p_kv[:], own[:].broadcast_to((P, 2, DV)), ALU.mult).then_inc(s_kvm, 1)
                dve.wait_ge(s_kvm, S * q + s + 1)
                if later(q, 1) or s >= 3:
                    dve.wait_ge(s_o, S * q + s - 2)
                for c in range(2):
                    i = 2 * s + c
                    if par == 0 and i == 0:
                        dve.tensor_copy(state[:, 1], kvm[:, 0]).then_inc(s_state, 1)
                        continue
                    dve.wait_ge(s_state, NC * q + i)
                    dve.scalar_tensor_tensor(out=state[:, (i + 1) % NC], in0=state[:, i % NC],
                                             scalar=eq[:, par, i, CH - 1:CH], in1=kvm[:, c], op0=ALU.mult,
                                             op1=ALU.add).then_inc(s_state, 1)

            def sum_squares(q, par):
                dve.wait_ge(s_sq, S * (q + 1))
                dve.wait_ge(s_lss, q)
                dve.tensor_reduce(ss[:], sq[:].rearrange("p s h e -> p (s h) e"), AX.X, ALU.add).then_inc(s_ss, 1)

            def norm_o(q, par):
                dve.wait_ge(s_ri, q + 1)
                dve.wait_ge(s_oo, S * (q + 1))
                dve.wait_ge(s_og, q)
                dve.tensor_tensor(on[:], o[:].rearrange("p s (h e) -> p (s h) e", h=HEADS),
                                  ri[:, :, None].broadcast_to((P, S * HEADS, VH)), ALU.mult).then_inc(s_on, 1)

            def take_og(q, g):
                dve.wait_ge(s_ogt, 2 * q + g + 1)
                dve.wait_ge(s_out, q)
                dve.tensor_copy(ogT[:, 2 * g:2 * g + 2].rearrange("p s j t -> p (s j t)"), p_f[:]).then_inc(s_ogT, 1)

            def residual(q, par):
                dve.wait_ge(s_out, q + 1)
                dve.wait_ge(s_x3, S * q)
                dve.wait_ge(s_x2r, q + 1)
                dve.tensor_tensor(res[:], p_f[:].rearrange("p (s d) -> p s d", s=S), x2r[:, par],
                                  ALU.add).then_inc(s_res, 1)
                dve.wait_ge(s_res, q + 1)
                moments_of(q, res, stats, moments, s_st, s_mom)

            def norm_x3(q, par):
                dve.wait_ge(s_rstd, q + 1)
                dve.wait_ge(s_mom, S * (q + 1))
                if later(q, 2):
                    dve.wait_ge(s_placed[par], PLACES // 2 * (q - par))
                for s in range(S):
                    dve.tensor_scalar(row3[:, par, s, 0:D], res[:, s], moments[:, s, 0:1], rstd[:, s:s + 1],
                                      ALU.subtract, ALU.mult).then_inc(s_x3, 1)

            def step(q, n, ins):
                ins.then_inc(s_route, 1)
                dve.wait_ge(s_route, 10 * q + n)

            def choose(q, par):
                best = row3[:, par, :, D:D + 1]
                wide = (P, S, E)
                dve.wait_ge(s_near, q + 1)
                if later(q, 2):
                    dve.wait_ge(s_placed[par], PLACES // 2 * (q - par))
                step(q, 1, dve.tensor_reduce(best, p_near, AX.X, ALU.max))
                step(q, 2, dve.tensor_tensor(hit[:], p_near, best.broadcast_to(wide), ALU.is_equal))
                step(q, 3, dve.tensor_tensor(cand[:], hit[:], first_of[:].broadcast_to(wide), ALU.mult))
                step(q, 4, dve.tensor_reduce(pref[:], cand[:], AX.X, ALU.max))
                dve.wait_ge(s_ranks, q)
                step(q, 5, dve.tensor_tensor(chosen[:, 0:S], cand[:], pref[:, :, None].broadcast_to(wide), ALU.is_equal))

            def locate(q, par):
                dve.wait_ge(s_ranks, q + 1)
                step(q, 6, dve.tensor_tensor(rank[:], p_rank[:, 0:S], keep.base[:].broadcast_to((P, S, E)), ALU.add))
                step(q, 7, dve.tensor_tensor(keep.base[:], p_rank[:, S:S + 1], keep.base[:], ALU.add))
                step(q, 8, dve.tensor_tensor(picked[:], rank[:], chosen[:, 0:S], ALU.mult))
                step(q, 9, dve.tensor_reduce(place[:], picked[:], AX.X, ALU.add))
                step(q, 10, dve.tensor_copy(ix3[:, par], place[:]))

            run_chunks(Q, 2 * S, dve.Fori, [
                (0, -1, sum_squares), (0, 2, indices), (1, -2, residual), (2, -1, norm_o), (3, -2, norm_x3),
                (3, 2, lambda q, par: sum_expert(q, par, 0)), (4, 1, cumulate), (5, 2, lambda q, par: sum_expert(q, par, 1)),
                (5, -1, lambda q, par: take_og(q, 0)), (6, 1, scale_qk), (6, -2, choose), (6, 2, norm_x2),
                (7, -1, lambda q, par: take_og(q, 1)), (7.5, -2, locate)], attend)

        @block.tensor
        def _(pe):
            pe.wait_ge(s_w, WEIGHTS)
            for n in range(3):
                t = pe.transpose(p_kv[:, 0, E * n:E * n + E], lnc[:, n], keep.ident[0:E, 0:E])
            t.then_inc(s_wT, 1)
            pe.wait_ge(s_cT, 3)
            pe.wait_ge(s_wo, 2)

            def turn_x2(q, par):
                pe.wait_ge(s_x2, S * (q + 1))
                pe.wait_ge(s_kh, 2 * q)
                for s in range(S):
                    t = pe.transpose(p_a[:, P * s:P * s + P], x2[:, par, s], keep.ident[:])
                t.then_inc(s_t, 1)

            def project_low(q, par):
                pe.wait_ge(s_xT, q + 1)
                pe.matmul(p_a[0:R, :], w1[:], xT[:], start=True, stop=True).then_inc(s_low, 1)

            def project_vg(q, par, tiles):
                pe.wait_ge(s_qk, 3 * q)
                for s in tiles:
                    if s >= 2:
                        pe.wait_ge(s_v, S * q + s - 1)
                    pe.matmul((p_q, p_k)[s % 2][:], xT[:, P * s:P * s + P], wvg[:], start=True,
                              stop=True).then_inc(s_vg, 1)

            def project_u(q, par):
                pe.wait_ge(s_lows, q + 1)
                pe.matmul(p_a[:], w2[:], low[:], start=True, stop=True).then_inc(s_u, 1)

            def project_qk(q, par):
                pe.wait_ge(s_v, S * (q + 1))
                pe.matmul(p_q[:], wq[:], xT[:], start=True, stop=True).then_inc(s_q, 1)
                pe.matmul(p_k[:], wk[:], xT[:], start=True, stop=True).then_inc(s_q, 1)

            def turn_kh(q, par):
                pe.wait_ge(s_qk, 3 * q + 3)
                pe.wait_ge(s_neg, q + 1)
                pe.wait_ge(s_gate, 2 * q + 3)
                for s in range(S):
                    t = pe.transpose(p_a[:, P * s:P * s + P], khT[:, P * s:P * s + P], keep.ident[:])
                t.then_inc(s_kht, 1)

            def products(q, par, s):
                pe.wait_ge(s_kgh, HEADS * (q + 1))
                if later(q, 1) or s:
                    pe.wait_ge(s_am, S * q + s)
                cols = slice(P * s, P * s + P)
                for h in range(HEADS):
                    t = pe.matmul(p_s[:, h], kgh[:, par, h, cols], qg[:, par, cols], start=True, stop=True)
                t.then_inc(s_s, 1)
                pe.wait_ge(s_kh, 2 * q + 2)
                if later(q, 1) or s:
                    pe.wait_ge(s_kvm, S * q + s)
                for c in range(2):
                    t = pe.matmul(p_kv[:, c], kh[:, par, c, s], v[:, par, s], start=True, stop=True)
                t.then_inc(s_kv, 1)

            def output(q, par, s):
                if later(q, 1) or s >= 1:
                    pe.wait_ge(s_oo, S * q + s)
                pe.wait_ge(s_am, S * q + s + 1)
                pe.wait_ge(s_state, NC * q + 2 * s + 1)
                for h in range(HEADS):
                    out = slice(VH * h, VH * h + VH)
                    pe.matmul(p_o[:, out], am[:, s % 2, h], v[:, par, s, out], start=(h == 0), stop=False,
                              skip_group_check=True)
                for c in range(2):
                    i = 2 * s + c
                    if par == 0 and i == 0:
                        continue
                    cols = slice(P * s + CH * c, P * s + CH * c + CH)
                    t = pe.matmul(p_o[CH * c:CH * c + CH, :], qg[:, par, cols], state[:, i % NC],
                                  start=False, stop=(c == 1), skip_group_check=True)
                t.then_inc(s_o, 1)

            def attend(q, par, n):
                if n % 2 == 0:
                    products(q, par, n // 2)
                else:
                    output(q, par, n // 2)

            def turn_og(q, g):
                pe.wait_ge(s_og, q + 1)
                if g:
                    pe.wait_ge(s_ogT, 2 * q + 1)
                elif later(q, 1):
                    pe.wait_ge(s_res, q)
                for s in range(2):
                    for j in range(2):
                        at = P * (2 * s + j)
                        src = og[:, HEADS * (2 * g + s) + 2 * j:HEADS * (2 * g + s) + 2 * j + 2]
                        t = pe.transpose(p_f[:, at:at + P], src.rearrange("p h e -> p (h e)"), keep.ident[:])
                t.then_inc(s_ogt, 1)

            def project_out(q, par):
                pe.wait_ge(s_ogT, 2 * q + 2)
                for s in range(S):
                    for j in range(2):
                        t = pe.matmul(p_f[:, P * s:P * s + P], ogT[:, s, j], wo[:, j], start=(j == 0), stop=(j == 1))
                t.then_inc(s_out, 1)

            def turn_x3(q, par):
                pe.wait_ge(s_x3, S * (q + 1))
                if later(q, 1):
                    pe.wait_ge(s_route, 10 * q)
                for s in range(S):
                    t = pe.transpose(p_r[:, P * s:P * s + P], row3[:, par, s, 0:D], keep.ident[:])
                t.then_inc(s_t3, 1)

            def affinities(q, par):
                pe.wait_ge(s_x3T, q + 1)
                for s in range(S):
                    t = pe.matmul(p_near[:, s], x3T[:, P * s:P * s + P], keep.cT[:], start=True, stop=True)
                t.then_inc(s_near, 1)

            def ranks(q, par):
                pe.wait_ge(s_route, 10 * q + 5)
                flat = p_rank.rearrange("p s e -> p (s e)")
                pe.matmul(flat, keep.before[:], chosen[:].rearrange("p s e -> p (s e)"), start=True, stop=True)
                for back in range(1, S + 1):
                    t = pe.matmul(flat[:, E * back:], keep.ones[:],
                                  chosen[:, 0:S + 1 - back].rearrange("p s e -> p (s e)"), start=False, stop=True,
                                  skip_group_check=True)
                t.then_inc(s_ranks, 1)

            run_chunks(Q, 2 * S, pe.Fori, [
                (0, 1, turn_x2), (0, -2, project_out), (1, 1, project_low), (2, 1, project_u),
                (3, 1, lambda q, par: project_vg(q, par, (0, 1))), (4, 1, lambda q, par: project_vg(q, par, (2, 3))),
                (4, -1, lambda q, par: turn_og(q, 0)), (4, -2, turn_x3), (5, 1, project_qk), (5, -2, affinities),
                (6, -1, lambda q, par: turn_og(q, 1)), (7, -2, ranks), (7, 1, turn_kh)], attend)


def routed_ffn(nc, keep, ffn, out):
    T = keep.x1.shape[0]
    E, D = ffn.centroids.shape
    F = ffn.w1.shape[2]
    FB = F // P
    NT = T // P
    TILES = NT + E
    NONE = 4.0 * E * T
    WIDE = keep.WIDE
    out_rows = out.rearrange("b l d -> (b l) d")
    w1s, w2s, b1s, gT, bT, eps = keep.w1s, keep.w2s, keep.b1s, keep.gT, keep.bT, keep.eps

    with ExitStack() as outer:
        k = Space(nc, outer, "ffn")
        owner = k.sb("owner", [P, TILES], I32)
        start = k.sb("start", [P, TILES], I32)

        with ExitStack() as ctx:
            m = Space(nc, ctx, "cut")
            full = m.sb("full", [P, 1, NT])
            order = m.sb("order", [P, TILES, 1])
            first_row = m.sb("first_row", [P, E])
            lane = m.sb("lane", [P, 1])
            count = m.sb("count", [P, E])
            more = m.sb("more", [P, E, NT])
            size, end, spare = m.sb("size", [P, E]), m.sb("end", [P, E]), m.sb("spare", [P, 1, E])
            passed, skip = m.sb("passed", [P, TILES, E]), m.sb("skip", [P, TILES, E])
            who, at = m.sb("who", [P, TILES]), m.sb("at", [P, TILES])
            row, limit, over = m.sb("row", [P, E]), m.sb("limit", [P, E]), m.sb("over", [P, E])
            pad_at = m.sb("pad_at", [P, E], I32)
            pad = m.sb("pad", [P, WIDE])
            s_iota, s_r, s_pad, s_padded = m.sem("iota_made"), m.sem("cutting_steps"), m.sem("pad_made"), m.sem("padded")
            s_last = m.sem("last_tile_padded")
            block = m.block()
            PADS = 10

            @block.sync
            def _(sp):
                sp.wait_ge(s_pad, 2)
                sp.dma_start(keep.xs[E * T:E * T + P, :], pad[:]).then_inc(s_last, 16)
                sp.wait_ge(s_last, 16)

            @block.gpsimd
            def _(pool):
                for tile, step, base in ((full[:, 0], P, 0), (order[:, :, 0], 1, 0), (first_row[:], T, 0)):
                    pool.iota(tile, pattern=[[step, tile.shape[1]]], base=base, channel_multiplier=0,
                              allow_small_or_imprecise_dtypes=True).then_inc(s_iota, 1)
                pool.iota(lane[:], pattern=[[1, 1]], base=0, channel_multiplier=1,
                          allow_small_or_imprecise_dtypes=True).then_inc(s_iota, 1)
                pool.wait_ge(s_r, PADS)
                pool.wait_ge(s_pad, 2)
                for e in range(E):
                    pool.indirect_dma_start(
                        out=keep.xs, out_offset=bass.IndirectOffsetOnAxis(ap=pad_at[:, e:e + 1], axis=0),
                        in_=pad[:], in_offset=None, bounds_check=E * T - 1, oob_is_err=False).then_inc(s_padded, 16)
                pool.wait_ge(s_padded, 16 * E)

            @block.vector
            def _(dve):
                steps = [0]

                def step(ins):
                    ins.then_inc(s_r, 1)
                    steps[0] += 1
                    dve.wait_ge(s_r, steps[0])

                dve.memset(pad[:, 0:D + 1], 0.0).then_inc(s_pad, 1)
                dve.memset(pad[:, D + 1:], NONE).then_inc(s_pad, 1)
                dve.wait_ge(s_iota, 4)
                step(dve.tensor_tensor(count[:], keep.base[:, 0], first_row[:], ALU.subtract))
                step(dve.tensor_tensor(more[:], count[:, :, None].broadcast_to((P, E, NT)),
                                       full[:].broadcast_to((P, E, NT)), ALU.is_gt))
                step(dve.tensor_reduce(size[:], more[:], AX.X, ALU.add))
                step(dve.tensor_scalar(limit[:], size[:], float(P), None, ALU.mult))
                step(dve.tensor_tensor(limit[:], limit[:], first_row[:], ALU.add))
                step(dve.tensor_scalar(row[:], keep.base[:, 0], lane[:], None, ALU.add))
                step(dve.tensor_tensor(over[:], row[:], limit[:], ALU.is_ge))
                step(dve.tensor_scalar(over[:], over[:], NONE, None, ALU.mult))
                step(dve.tensor_tensor(row[:], row[:], over[:], ALU.add))
                step(dve.tensor_copy(pad_at[:], row[:]))
                step(dve.tensor_tensor_scan(end[:], keep.ones[:, 0:E], size[:], 0.0, ALU.mult, ALU.add))
                step(dve.tensor_tensor(passed[:], order[:].broadcast_to((P, TILES, E)),
                                       end[:, None, :].broadcast_to((P, TILES, E)), ALU.is_ge))
                step(dve.tensor_reduce(who[:], passed[:], AX.X, ALU.add))
                step(dve.tensor_scalar(who[:], who[:], float(E - 1), None, ALU.min))
                step(dve.tensor_copy(owner[:], who[:]))
                step(dve.tensor_scalar(spare[:, 0], size[:], -1.0, float(NT), ALU.mult, ALU.add))
                step(dve.tensor_tensor(skip[:], passed[:], spare[:].broadcast_to((P, TILES, E)), ALU.mult))
                step(dve.tensor_reduce(at[:], skip[:], AX.X, ALU.add))
                step(dve.tensor_tensor(at[:], at[:], order[:, :, 0], ALU.add))
                step(dve.tensor_scalar(at[:], at[:], float(E * NT), float(P), ALU.min, ALU.mult))
                step(dve.tensor_copy(start[:], at[:]))

        with ExitStack() as ctx:
            m = Space(nc, ctx, "tiles")
            DEEP = 4
            rows = m.sb("rows", [P, DEEP, WIDE])
            twice = m.sb("twice", [P, DEEP, WIDE])
            stats, moments = m.sb("stats", [P, DEEP, 6]), m.sb("moments", [P, DEEP, 2])
            lnvar, rstd = m.sb("lnvar", [P, DEEP]), m.sb("rstd", [P, DEEP])
            xn, xT = m.sb("xn", [P, 2, D]), m.sb("xT", [P, 2, P])
            h, hT = m.sb("h", [P, 2, F]), m.sb("hT", [P, 2, F])
            away, alpha = m.sb("away", [P, DEEP]), m.sb("alpha", [P, DEEP])
            token = m.sb("token", [P, DEEP], I32)
            res = m.sb("res", [P, DEEP, D])
            ostats, omoments = m.sb("ostats", [P, DEEP, 6]), m.sb("omoments", [P, DEEP, 2])
            olnvar, orstd = m.sb("olnvar", [P, DEEP]), m.sb("orstd", [P, DEEP])
            done = m.sb("done", [P, DEEP, D])
            p_t = [m.ps(f"p_t{i}", [P, 512]) for i in range(2)]
            p_h = [m.ps(f"p_h{i}", [P, F]) for i in range(2)]
            p_r = [m.ps(f"p_r{i}", [P, F]) for i in range(2)]
            p_y = [m.ps(f"p_y{i}", [P, 512]) for i in range(2)]
            s_in = [m.sem(f"rows_loaded{i}") for i in range(DEEP)]
            s_out = [m.sem(f"rows_sent{i}") for i in range(DEEP)]
            s_st, s_mom, s_lnv, s_rstd, s_xn, s_twice = (m.sem(n) for n in (
                "stats_made", "moments_made", "lnvar_made", "rstd_made", "xn_made", "doubled"))
            s_t, s_xT, s_h, s_hs, s_r, s_hT, s_yp = (m.sem(n) for n in (
                "transposed", "xT_made", "h_product", "h_made", "h_transposed", "hT_made", "y_product"))
            s_exp, s_one, s_alpha, s_token, s_res = (m.sem(n) for n in (
                "exp_made", "one_added", "alpha_made", "token_made", "residual_made"))
            s_ost, s_omom, s_olnv, s_orstd, s_done = (m.sem(n) for n in (
                "out_stats", "out_moments", "out_lnvar", "out_rstd", "output_made"))
            s_turn, s_sp_turn, s_pool_turn = m.sem("vector_steps"), m.sem("sync_steps"), m.sem("pool_steps")
            block = m.block()
            WEIGHTS = 16 * (E + 3)

            def pipeline(eng, *stages):
                depth = max(stage[0] for stage in stages) + 1
                looked_up = [stage for stage in stages if len(stage) == 3]

                def turns(first):
                    known = isinstance(first, int)
                    entry = {}
                    if looked_up:
                        table = looked_up[0][2]
                        late, early = max(s[0] for s in looked_up), min(s[0] for s in looked_up)
                        for d in range(-late, DEEP - early):
                            j = first + d
                            if not known or 0 <= j < TILES:
                                entry[d] = eng.value_load(table[0:1, j:j + 1] if known else table[0:1, bass.ds(j, 1)],
                                                          min_val=0, max_val=E * T if table is start else E - 1)
                    for b in range(DEEP):
                        for n, work, *tables in stages:
                            j = first + b - n
                            if not known or 0 <= j < TILES:
                                work(j, (b - n) % DEEP, *(entry[b - n] for _ in tables))

                head = (-(-depth // DEEP) + 1) * DEEP
                for first in range(0, head, DEEP):
                    turns(first)
                with eng.Fori(0, (TILES - head) // DEEP) as i:
                    turns(DEEP * i + head)
                for first in range(TILES, TILES + depth - 1, DEEP):
                    turns(first)

            def rounds(j, b):
                return (j - b) * (16 // DEEP)

            @block.sync
            def _(sp):
                def load(j, b, first):
                    if later(j, DEEP):
                        sp.wait_ge(s_twice, j + 1 - DEEP)
                        sp.sem_inc(s_sp_turn, 1)
                        sp.wait_ge(s_xn, j + 1 - DEEP)
                        sp.sem_inc(s_sp_turn, 1)
                    sp.dma_start(rows[:, b], keep.xs[bass.ds(first, P), :]).then_inc(s_in[b], 16)

                pipeline(sp, (0, load, start))

            @block.tensor
            def _(pe):
                pe.wait_ge(keep.s_big, WEIGHTS)

                def turn_x(j, b):
                    par = b % 2
                    pe.wait_ge(s_xn, j + 1)
                    if later(j, 2):
                        pe.wait_ge(s_xT, j - 1)
                    pe.transpose(p_t[par][:, 0:P], xn[:, par], keep.ident[:]).then_inc(s_t, 1)

                def up(j, b, e):
                    par = b % 2
                    pe.wait_ge(s_xT, j + 1)
                    if later(j, 2):
                        pe.wait_ge(s_hs, j - 1)
                    pe.matmul(p_h[par][:], xT[:, par], w1s[:, bass.ds(e, 1), :].rearrange("p a f -> p (a f)"),
                              start=True, stop=True).then_inc(s_h, 1)

                def turn_h(j, b):
                    par = b % 2
                    pe.wait_ge(s_hs, j + 1)
                    if later(j, 2):
                        pe.wait_ge(s_hT, j - 1)
                    for f in range(FB):
                        t = pe.transpose(p_r[par][:, P * f:P * f + P], h[:, par, P * f:P * f + P], keep.ident[:])
                    t.then_inc(s_r, 1)

                def down(j, b, e):
                    par = b % 2
                    pe.wait_ge(s_hT, j + 1)
                    if later(j, 2):
                        pe.wait_ge(s_res, j - 1)
                    for f in range(FB):
                        t = pe.matmul(p_y[par][:, 0:D], hT[:, par, P * f:P * f + P],
                                      w2s[:, bass.ds(e, 1), f, :].rearrange("p a d -> p (a d)"),
                                      start=(f == 0), stop=False)
                    t = pe.matmul(p_y[par][:, 0:D], keep.ones[0:1, :],
                                  keep.b2s[0:1, bass.ds(e, 1), :].rearrange("p a d -> p (a d)"), start=False, stop=True)
                    t.then_inc(s_yp, 1)

                pipeline(pe, (5, down, owner), (4, turn_h), (3, up, owner), (2, turn_x))

            @block.vector
            def _(dve):
                dve.wait_ge(keep.s_big, WEIGHTS)

                def x_stats(j, b):
                    dve.wait_ge(s_in[b], rounds(j, b) + 16)
                    if later(j, DEEP):
                        dve.wait_ge(s_mom, j + 1 - DEEP)
                    dve.bn_stats(stats[:, b], rows[:, b, 0:D]).then_inc(s_st, 1)

                def x_moments(j, b):
                    if later(j, DEEP):
                        dve.wait_ge(s_xn, j + 1 - DEEP)
                        dve.wait_ge(s_lnv, j + 1 - DEEP)
                    dve.wait_ge(s_st, j + 1)
                    dve.sem_inc(s_turn, 1)
                    dve.bn_aggr(moments[:, b], stats[:, b]).then_inc(s_mom, 1)

                def norm_x(j, b):
                    dve.wait_ge(s_rstd, j + 1)
                    dve.wait_ge(s_mom, j + 1)
                    if later(j, 2):
                        dve.wait_ge(s_t, j - 1)
                    dve.tensor_scalar(xn[:, b % 2], rows[:, b, 0:D], moments[:, b, 0:1], rstd[:, b:b + 1],
                                      ALU.subtract, ALU.mult).then_inc(s_xn, 1)

                def affine(j, b, e):
                    par = b % 2
                    dve.wait_ge(s_t, j + 1)
                    if later(j, 2):
                        dve.wait_ge(s_h, j - 1)
                    dve.tensor_scalar(xT[:, par], p_t[par][:, 0:P], gT[:, bass.ds(e, 1)], bT[:, bass.ds(e, 1)],
                                      ALU.mult, ALU.add).then_inc(s_xT, 1)

                def bias_h(j, b, e):
                    par = b % 2
                    dve.wait_ge(s_h, j + 1)
                    if later(j, 2):
                        dve.wait_ge(s_r, j - 1)
                    dve.tensor_tensor(h[:, par], p_h[par][:], b1s[:, bass.ds(e, 1), :].rearrange("p a f -> p (a f)"),
                                      ALU.add).then_inc(s_hs, 1)

                def weigh(j, b):
                    dve.wait_ge(s_exp, j + 1)
                    dve.tensor_scalar(away[:, b:b + 1], away[:, b:b + 1], 1.0, None, ALU.add).then_inc(s_one, 1)
                    if later(j, DEEP):
                        dve.wait_ge(s_res, j + 1 - DEEP)
                        dve.wait_ge(s_out[b], rounds(j, b))
                    dve.tensor_scalar(token[:, b:b + 1], twice[:, b, D + 1:D + 2], 0.5, None, ALU.mult).then_inc(s_token, 1)
                    dve.wait_ge(s_one, j + 1)
                    dve.reciprocal(alpha[:, b:b + 1], away[:, b:b + 1]).then_inc(s_alpha, 1)

                def residual(j, b):
                    dve.wait_ge(s_yp, j + 1)
                    dve.wait_ge(s_alpha, j + 1)
                    if later(j, DEEP):
                        dve.wait_ge(s_done, j + 1 - DEEP)
                    dve.scalar_tensor_tensor(out=res[:, b], in0=p_y[b % 2][:, 0:D], scalar=alpha[:, b:b + 1],
                                             in1=twice[:, b, 0:D], op0=ALU.mult, op1=ALU.add).then_inc(s_res, 1)

                def out_stats(j, b):
                    dve.wait_ge(s_res, j + 1)
                    if later(j, DEEP):
                        dve.wait_ge(s_omom, j + 1 - DEEP)
                    dve.bn_stats(ostats[:, b], res[:, b]).then_inc(s_ost, 1)

                def out_moments(j, b):
                    if later(j, DEEP):
                        dve.wait_ge(s_olnv, j + 1 - DEEP)
                    dve.wait_ge(s_ost, j + 1)
                    dve.sem_inc(s_turn, 1)
                    dve.bn_aggr(omoments[:, b], ostats[:, b]).then_inc(s_omom, 1)

                def norm_out(j, b):
                    dve.wait_ge(s_orstd, j + 1)
                    dve.wait_ge(s_omom, j + 1)
                    if later(j, DEEP):
                        dve.wait_ge(s_out[b], rounds(j, b))
                    dve.tensor_scalar(done[:, b], res[:, b], omoments[:, b, 0:1], orstd[:, b:b + 1],
                                      ALU.subtract, ALU.mult).then_inc(s_done, 1)

                pipeline(dve, (2, norm_x), (1, x_stats), (6, residual), (1, x_moments), (5, weigh), (6, out_stats),
                         (4, bias_h, owner), (6, out_moments), (7, norm_out), (3, affine, owner))

            @block.scalar
            def _(act):
                act.preload_act_table_set(LN_EXP)

                def x_rstd(j, b):
                    act.wait_ge(s_mom, j + 1)
                    if later(j, DEEP):
                        act.wait_ge(s_rstd, j + 1 - DEEP)
                    act.activation(lnvar[:, b:b + 1], moments[:, b, 1:2], ACT.Ln, bias=eps[:]).then_inc(s_lnv, 1)
                    act.wait_ge(s_lnv, j + 1)
                    if later(j, DEEP):
                        act.wait_ge(s_xn, j + 1 - DEEP)
                    act.activation(rstd[:, b:b + 1], lnvar[:, b:b + 1], ACT.Exp, scale=-0.5).then_inc(s_rstd, 1)

                def double(j, b):
                    act.wait_ge(s_in[b], rounds(j, b) + 16)
                    if later(j, DEEP):
                        act.wait_ge(s_res, j + 1 - DEEP)
                        act.wait_ge(s_token, j + 1 - DEEP)
                    act.activation(twice[:, b], rows[:, b], ACT.Copy, scale=2.0).then_inc(s_twice, 1)
                    act.wait_ge(s_twice, j + 1)
                    if later(j, DEEP):
                        act.wait_ge(s_alpha, j + 1 - DEEP)
                    act.activation(away[:, b:b + 1], twice[:, b, D:D + 1], ACT.Exp, scale=-0.5).then_inc(s_exp, 1)

                def rectify(j, b):
                    act.wait_ge(s_r, j + 1)
                    if later(j, 2):
                        act.wait_ge(s_yp, j - 1)
                    act.activation(hT[:, b % 2], p_r[b % 2][:], ACT.Relu).then_inc(s_hT, 1)

                def out_rstd(j, b):
                    act.wait_ge(s_omom, j + 1)
                    if later(j, DEEP):
                        act.wait_ge(s_orstd, j + 1 - DEEP)
                    act.activation(olnvar[:, b:b + 1], omoments[:, b, 1:2], ACT.Ln, bias=eps[:]).then_inc(s_olnv, 1)
                    act.wait_ge(s_olnv, j + 1)
                    if later(j, DEEP):
                        act.wait_ge(s_done, j + 1 - DEEP)
                    act.activation(orstd[:, b:b + 1], olnvar[:, b:b + 1], ACT.Exp, scale=-0.5).then_inc(s_orstd, 1)

                pipeline(act, (1, x_rstd), (6, out_rstd), (3, double), (4, rectify))

            @block.gpsimd
            def _(pool):
                def send(j, b):
                    pool.wait_ge(s_token, j + 1)
                    pool.sem_inc(s_pool_turn, 1)
                    pool.wait_ge(s_done, j + 1)
                    pool.sem_inc(s_pool_turn, 1)
                    pool.indirect_dma_start(
                        out=out_rows, out_offset=bass.IndirectOffsetOnAxis(ap=token[:, b:b + 1], axis=0),
                        in_=done[:, b], in_offset=None, bounds_check=T - 1, oob_is_err=False).then_inc(s_out[b], 16)

                pipeline(pool, (8, send))
                for b in range(DEEP):
                    pool.wait_ge(s_out[b], 16 * (TILES // DEEP))


def network(nc, a, out):
    T = a["L0_attn_x"].shape[0] * a["L0_attn_x"].shape[1]
    with ExitStack() as ctx:
        s = Space(nc, ctx, "keep")
        keep = Buffers()
        keep.ident = s.sb("ident", [P, P])
        keep.ones = s.sb("ones", [P, P])
        keep.before = s.sb("before", [P, P])
        keep.eps = s.sb("eps", [P, 1])
        E0 = a["L0_ffn_w_g"].shape[1]
        keep.K = 2
        keep.CAP = keep.K * 5 * T // (4 * E0)
        keep.CAP += keep.CAP % 2
        keep.best, keep.pref, keep.row = (s.sb(n, [P, T // P, keep.K]) for n in ("best", "pref", "row"))
        keep.count = s.sb("count", [P, 1, keep.K, E0])
        keep.weight, keep.from_slot = s.sb("weight", [P, keep.K, T // P]), s.sb("from_slot", [P, keep.K, T // P], I32)
        ffn = Buffers()
        ffn.centroids, ffn.ln_g, ffn.ln_b, ffn.w1, ffn.b1, ffn.w2, ffn.b2 = (
            a["L1_ffn_" + n] for n in ("centroids", "ln_g", "ln_b", "w1", "b1", "w2", "b2"))
        E, _, F = ffn.w1.shape
        keep.WIDE = P + 2
        rows = lambda name, n, width: nc.dram_tensor(name, (n, width), F32, kind="Internal").ap()
        keep.x1 = rows("x1_rows", T, P)
        keep.xe = rows("expert_in_rows", 2 * E0 * keep.CAP, P)
        keep.ye = rows("expert_out_rows", E0 * keep.CAP, P)
        keep.xs = rows("rows_by_centroid", E * T + P, keep.WIDE)
        constants(nc, keep)
        mamba(nc, keep, *(a["L0_attn_" + n] for n in (
            "x", "norm_w", "norm_b", "in_w", "in_b", "conv_w", "conv_b", "bc_w", "bc_b", "dtr_w", "dtr_b", "dt_w",
            "dt_b", "out_w", "out_b")), a["L0_ffn_w_g"])
        moe(nc, keep, a["L0_ffn_c_fc"], a["L0_ffn_c_proj"])

        s = Space(nc, ctx, "layer1")
        keep.base = s.sb("base", [P, 1, E])
        keep.cT, keep.gT, keep.bT = (s.sb(n, [P, E]) for n in ("cT", "gT", "bT"))
        keep.w1s, keep.w2s = s.sb("w1s", [P, E, F]), s.sb("w2s", [P, E, F // P, P])
        keep.b1s, keep.b2s = s.sb("b1s", [P, E, F]), s.sb("b2s", [1, E, P])
        keep.s_big = s.sem("ffn_weights_loaded")
        gla(nc, keep, *(a["L1_attn_" + n] for n in (
            "Wq", "Wk", "Wv", "Wg", "gk_w1", "gk_w2", "gk_b2", "g_norm_w", "Wo")), ffn)
        routed_ffn(nc, keep, ffn, out)


def kernel(**inputs):
    import numpy as np
    import concourse.bacc as bacc
    from concourse.bass_utils import run_bass_kernel_spmd

    nc = bacc.Bacc("TRN2", target_bir_lowering=False, num_devices=1)
    arrays, views = {}, {}
    for name, value in inputs.items():
        arrays[f"in_{name}"] = np.ascontiguousarray(value)
        views[name] = nc.dram_tensor(f"in_{name}", value.shape, mybir.dt.from_np(arrays[f"in_{name}"].dtype),
                                     kind="ExternalInput").ap()
    out = nc.dram_tensor("out", inputs["L0_attn_x"].shape, F32, kind="ExternalOutput").ap()
    network(nc, views, out)
    return run_bass_kernel_spmd(nc, [arrays], core_ids=[0]).results[0]["out"]
```
